# Optimizing a Trainium2 kernel written in Bass

```python
import numpy as np
import jax
import jax.numpy as jnp

def _softmax(x, axis=-1):
    return jax.nn.softmax(x, axis=axis)

def _gelu(x):
    return jax.nn.gelu(x, approximate=True)

def _silu(x):
    return jax.nn.silu(x)

def _sigmoid(x):
    return jax.nn.sigmoid(x)

def _layernorm(x, axis=-1, eps=1e-05):
    m = jnp.mean(x, axis=axis, keepdims=True)
    v = jnp.var(x, axis=axis, keepdims=True)
    return (x - m) / jnp.sqrt(v + eps)

def _scatter_add(tgt, idx, src, axis=0):
    return tgt.at[idx].add(src)

def _segment_sum(src, seg, n):
    return jax.ops.segment_sum(src, seg, n)
kernel_name = 'mk_adaln_d1_jaxref_r4_a8c630'

def setup_inputs(seed: int=0):
    np.random.seed(seed)
    _w = jnp.asarray

    def _L0_attn_setup():
        import jax, jax.numpy as jnp
        import numpy as np
        B, S, DIM = (2, 512, 256)
        H, DH = (16, 64)
        WIN = 128
        key = jax.random.key(seed)
        k1, k2, k3 = jax.random.split(key, 3)
        x = jax.random.normal(k1, (B, S, DIM), dtype=jnp.float32)
        Wqkv = jax.random.normal(k2, (DIM, 3 * H * DH), dtype=jnp.float32) * DIM ** (-0.5)
        Wout = jax.random.normal(k3, (H * DH, DIM), dtype=jnp.float32) * (H * DH) ** (-0.5)
        return {'x': x, 'Wqkv': Wqkv, 'Wout': Wout}
    _L0_attn_in = _L0_attn_setup()

    def _L0_ffn_setup():
        import math
        import jax, jax.numpy as jnp
        import numpy as np
        B, L, D, FF, E, K = (4, 512, 256, 1024, 8, 2)
        CAPACITY_FACTOR = 1.25
        T = B * L
        CAP = math.ceil(CAPACITY_FACTOR * T * K / E)
        key = jax.random.key(seed)
        ks = jax.random.split(key, 7)
        return {'h': jax.random.normal(ks[0], (B, L, D), dtype=jnp.float32), 'gate_w': 0.02 * jax.random.normal(ks[1], (E, D), dtype=jnp.float32), 'gate_b': jnp.zeros((E,), dtype=jnp.float32), 'W1': 0.02 * jax.random.normal(ks[2], (E, D, FF), dtype=jnp.float32), 'b1': jnp.zeros((E, FF), dtype=jnp.float32), 'W2': 0.02 * jax.random.normal(ks[3], (E, FF, D), dtype=jnp.float32), 'b2': jnp.zeros((E, D), dtype=jnp.float32)}
    _L0_ffn_in = _L0_ffn_setup()
    _L0_c = _w((lambda *s: np.random.randn(*s).astype(np.float32) * 0.05)(2, 256))
    _L0_wmod = _w((lambda *s: np.random.randn(*s).astype(np.float32) * 0.05)(256, 6 * 256) * 256 ** (-0.5))
    _d = {'L0_attn_x': _L0_attn_in['x'], 'L0_attn_Wqkv': _L0_attn_in['Wqkv'], 'L0_attn_Wout': _L0_attn_in['Wout'], 'L0_ffn_gate_w': _L0_ffn_in['gate_w'], 'L0_ffn_gate_b': _L0_ffn_in['gate_b'], 'L0_ffn_W1': _L0_ffn_in['W1'], 'L0_ffn_b1': _L0_ffn_in['b1'], 'L0_ffn_W2': _L0_ffn_in['W2'], 'L0_ffn_b2': _L0_ffn_in['b2'], 'L0_c': _L0_c, 'L0_wmod': _L0_wmod}
    _x0 = _d['L0_attn_x']
    _d['L0_attn_x'] = jax.random.normal(jax.random.fold_in(jax.random.key(seed), 1), (2, 2048, 256), dtype=_x0.dtype)
    del _x0
    return _d

def reference(L0_attn_x, L0_attn_Wqkv, L0_attn_Wout, L0_ffn_gate_w, L0_ffn_gate_b, L0_ffn_W1, L0_ffn_b1, L0_ffn_W2, L0_ffn_b2, L0_c, L0_wmod):

    def _L0_attn_ref(x, Wqkv, Wout):
        import jax, jax.numpy as jnp
        import numpy as np
        B, S, DIM = (2, 512, 256)
        H, DH = (16, 64)
        WIN = 128
        b, s, _ = x.shape
        qkv = jnp.einsum('bsd,de->bse', x, Wqkv)
        q, k, v = jnp.split(qkv, 3, axis=-1)
        q = q.reshape(b, s, H, DH).transpose(0, 2, 1, 3)
        k = k.reshape(b, s, H, DH).transpose(0, 2, 1, 3)
        v = v.reshape(b, s, H, DH).transpose(0, 2, 1, 3)
        scale = DH ** (-0.5)
        scores = jnp.einsum('bhsd,bhtd->bhst', q, k) * scale
        i = jnp.arange(s)[:, None]
        j = jnp.arange(s)[None, :]
        mask = (j >= i - WIN + 1) & (j <= i)
        mask_value = -jnp.finfo(scores.dtype).max
        scores = jnp.where(mask[None, None], scores, mask_value)
        attn = jax.nn.softmax(scores, axis=-1)
        out = jnp.einsum('bhst,bhtd->bhsd', attn, v)
        out = out.transpose(0, 2, 1, 3).reshape(b, s, H * DH)
        return jnp.einsum('bse,ed->bsd', out, Wout)

    def _L0_ffn_ref(h, gate_w, gate_b, W1, b1, W2, b2):
        import math
        import jax, jax.numpy as jnp
        import numpy as np
        B, L, D, FF, E, K = (4, 512, 256, 1024, 8, 2)
        CAPACITY_FACTOR = 1.25
        T = B * L
        CAP = math.ceil(CAPACITY_FACTOR * T * K / E)
        Bb, Ll, Dm = h.shape
        Tt = Bb * Ll
        x = h.reshape(Tt, Dm)
        logits = x @ gate_w.T + gate_b
        probs = jax.nn.softmax(logits, axis=-1)
        topk_prob, topk_idx = jax.lax.top_k(probs, K)
        y = jnp.zeros((Tt, Dm), dtype=h.dtype)
        n_slots = E * CAP
        for c in range(K):
            idx = topk_idx[:, c]
            prb = topk_prob[:, c]
            oh = jax.nn.one_hot(idx, E, dtype=jnp.int32)
            pos = jnp.take_along_axis(jnp.cumsum(oh, axis=0) - 1, idx[:, None], axis=1)[:, 0]
            keep = pos < CAP
            buf_idx = jnp.where(keep, idx * CAP + pos, n_slots)
            xbuf = jnp.zeros((n_slots, Dm), x.dtype).at[buf_idx].set(x, mode='drop')
            xb = xbuf.reshape(E, CAP, Dm)
            hmid = jax.nn.relu(jnp.einsum('ecd,edf->ecf', xb, W1) + b1[:, None, :])
            yb = jnp.einsum('ecf,efd->ecd', hmid, W2) + b2[:, None, :]
            ytok = yb.reshape(n_slots, Dm)[jnp.clip(buf_idx, 0, n_slots - 1)]
            y = y + ytok * (prb * keep.astype(prb.dtype))[:, None]
        return y.reshape(Bb, Ll, Dm)
    x = L0_attn_x
    mod = (_silu(L0_c) @ L0_wmod).reshape(L0_c.shape[0], 6, 1, -1)
    sa, ca, ga, sb, cb, gb = (mod[:, 0], mod[:, 1], mod[:, 2], mod[:, 3], mod[:, 4], mod[:, 5])
    ga = (2 * (ga >= 0) - 1) * jnp.maximum(jnp.abs(ga), 0.25)
    gb = (2 * (gb >= 0) - 1) * jnp.maximum(jnp.abs(gb), 0.25)
    h = _layernorm(x, axis=-1) * (1 + ca) + sa
    x = x + ga * _L0_attn_ref(h, L0_attn_Wqkv, L0_attn_Wout)
    h = _layernorm(x, axis=-1) * (1 + cb) + sb
    x = x + gb * _L0_ffn_ref(h, L0_ffn_gate_w, L0_ffn_gate_b, L0_ffn_W1, L0_ffn_b1, L0_ffn_W2, L0_ffn_b2)
    return x

_drawn_inputs = setup_inputs


def setup_inputs(seed=0):
    import zlib

    import numpy as np

    out = dict(_drawn_inputs(seed))
    spreads = {'L0_ffn_gate_b': (0.0, 0.8), 'L0_ffn_b1': (0.0, 0.8), 'L0_ffn_b2': (0.0, 0.8)}
    factors = {'L0_ffn_gate_w': 5.811, 'L0_ffn_W1': 7.522, 'L0_ffn_W2': 6.024}
    for name, (base, spread) in spreads.items():
        noise = np.random.default_rng([zlib.crc32(name.encode()), seed]).standard_normal(out[name].shape)
        drawn = base * np.exp(spread * noise) if base else spread * noise
        out[name] = jnp.asarray(drawn.astype(out[name].dtype))
    for name, factor in factors.items():
        out[name] = (out[name] * factor).astype(out[name].dtype)
    return out
```

```python
from contextlib import ExitStack

import concourse.bass as bass
from concourse import mybir

ALU = mybir.AluOpType
ACT = mybir.ActivationFunctionType
AX = mybir.AxisListType
F32 = mybir.dt.float32
F16 = mybir.dt.float16
BF16 = mybir.dt.bfloat16
I32 = mybir.dt.int32
U32 = mybir.dt.uint32

W_SCALE = 64.0
SPLIT_PRODUCTS = ((0, 0), (0, 1), (1, 0))
MASKED = -3.0e38

P = 128
D = 256
KD = D // P
H, DH = 16, 64
PAIRS = H // 2
INNER = H * DH
CHUNK = 512
TILES = CHUNK // P
FF, E, K = 1024, 8, 2
FT = FF // P


def group_order(names):
    place, count = {}, [0, 0]
    for n, name in enumerate(names):
        place[name] = (n % 2, count[n % 2])
        count[n % 2] += 1
    return place, count


def build(nc, x_in, wqkv_in, wout_in, gate_w, gate_b, w1_in, b1_in, w2_in, b2_in, c_in, wmod_in, out):
    B, S, _ = x_in.shape
    T = B * S
    NT = T // P
    NC = T // CHUNK
    CPB = S // CHUNK
    CAP = 640
    SLOTS = E * K * CAP
    ST = K * CAP // P
    NPART = ((0, 512), (512, 512), (1024, 256))
    FAR = 100000.0

    x_rows = x_in.rearrange("b s d -> (b s) d")
    out_rows = out.rearrange("b s d -> (b s) d")
    xbuf = nc.dram_tensor("slot_inputs", (SLOTS, 2 * D), F16, kind="Internal").ap()
    ybuf = nc.dram_tensor("slot_outputs", (SLOTS, D), F32, kind="Internal").ap()

    whole = ExitStack()
    with whole:
        def alloc(stack):
            return lambda name, shape, dt: stack.enter_context(nc.sbuf_tensor(name, shape, dt))

        def sem(name):
            return whole.enter_context(nc.semaphore(name))

        keep_sb = alloc(whole)
        x = keep_sb("x", [P, NT, D], F32)
        modrow = keep_sb("modrow", [P, B, 4, D], F32)
        weight = keep_sb("weight", [P, NT, K], F32)
        fetch = keep_sb("fetch", [P, NT, K], U32)
        ident16 = keep_sb("ident16", [P, P], F16)

        x0_loaded, x_loaded, small_loaded, zero_sent = (sem(n) for n in ("x0_loaded", "x_loaded", "small_loaded", "zero_sent"))
        stage_loaded = [sem(f"stage_loaded{i}") for i in range(4)]
        consts = sem("consts")
        exp_c, sil, sil_b, mod_mm, mod_row, split_hi, split_lo = (
            sem(n) for n in ("exp_c", "sil", "sil_b", "mod_mm", "mod_row", "split_hi", "split_lo"))

        def stand_ge(eng, *waits):
            ready = [(s, v if isinstance(v, int) else eng.compute_val(v)) for s, v in waits]
            if not all(isinstance(v, int) for _, v in ready):
                eng.wait_ge(consts, 2)
            for s, v in ready:
                eng.wait_ge(s, v)

        def at_least(eng, s, value):
            if not isinstance(value, int) or value > 0:
                eng.wait_ge(s, value)

        attn_stack = ExitStack()
        with attn_stack:
            sb = alloc(attn_stack)
            ps = lambda name, shape, dt: attn_stack.enter_context(nc.psum_tensor(name, shape, dt))
            wqkv = sb("wqkv", [P, KD, 2, 3 * INNER], F16)
            wout = sb("wout", [P, PAIRS, 2, D], F16)
            hT = sb("hT", [P, 2, KD, 2, CHUNK], F16)
            q = sb("q", [P, PAIRS, 2, CHUNK], F16)
            k = sb("k", [P, PAIRS, 2, P + CHUNK], F16)
            v = sb("v", [P, 1 + TILES, 2, INNER], F16)
            attn = sb("attn", [P, PAIRS, 2, CHUNK], F16)
            prob = sb("prob", [P, 2, TILES, P], F32)
            prob16 = sb("prob16", [P, 2, 2, TILES, P], F16)
            probT = sb("probT", [P, 2, 2 * TILES, P], F16)
            probT_cur = sb("probT_cur", [P, 2, 2 * TILES, P], F16)
            probT_prev = sb("probT_prev", [P, 2, 2 * TILES, P], F16)
            xn = sb("xn", [P, TILES, D], F32)
            h32 = sb("h32", [P, KD, CHUNK], F32)
            h2 = sb("h2", [P, TILES, D], F32)
            packed = sb("packed", [P, TILES, 2 * D], F16)
            h2T = sb("h2T", [P, KD, CHUNK], F32)
            gated = sb("gated", [P, 2, D], F32)
            zero_row = sb("zero_row", [P, 2 * D], F16)
            identf = sb("identf", [P, P], F32)
            onesf = sb("onesf", [P, P], F32)
            above = sb("above", [P, P], F32)
            keys_cur = sb("keys_cur", [P, P], F16)
            ones_row = sb("ones_row", [1, P], BF16)
            no_prev = sb("no_prev", [1, NC, P], BF16)
            cT = sb("cT", [P, KD, B], F32)
            silT = sb("silT", [P, 3, KD * B], F32)
            silB = sb("silB", [P, KD * B, P], F32)
            modcol = sb("modcol", [P, 4, B], F32)
            gwT = sb("gwT", [P, KD, E], F32)
            gbB = sb("gbB", [P, E], F32)
            expert_no = sb("expert_no", [P, E], F32)
            choice_base = sb("choice_base", [P, TILES, K], F32)
            half_neg = sb("half_neg", [P, TILES], F32)
            rowmax = sb("rowmax", [P, 2, TILES], F32)
            negmax = sb("negmax", [P, 2, TILES], F32)
            rowsum = sb("rowsum", [P, 2, TILES], F32)
            rinv = sb("rinv", [P, 2, TILES], F32)
            stats = [sb(f"stats{i}", [P, TILES, 6], F32) for i in range(2)]
            meanvar = [sb(f"meanvar{i}", [P, TILES, 2], F32) for i in range(2)]
            rstd = [sb(f"rstd{i}", [P, 2, TILES], F32) for i in range(2)]
            logit = sb("logit", [P, TILES, E], F32)
            lmax = sb("lmax", [P, TILES], F32)
            lsum = sb("lsum", [P, 2, TILES], F32)
            top = sb("top", [P, TILES, 8], F32)
            topi = sb("topi", [P, TILES, 8], U32)
            topf = sb("topf", [P, TILES, K], F32)
            onehot = sb("onehot", [P, TILES, K, E], F32)
            cum = sb("cum", [P, TILES, K, E], F32)
            carry = sb("carry", [P, K, E], F32)
            pos = sb("pos", [P, TILES, K], F32)
            posc = sb("posc", [P, TILES, K], F32)
            slot = sb("slot", [P, TILES, K], F32)
            drop = sb("drop", [P, TILES, K], F32)
            send = sb("send", [P, TILES, K], U32)

            score = [ps(f"score{i}", [P, TILES, 2 * P], F32) for i in range(2)]
            pt = ps("pt", [P, 2 * TILES, P], F16)
            pv = ps("pv", [P, CHUNK], F32)
            gen = [ps(f"gen{i}", [P, 512], F32) for i in range(2)]

            stage = [q[:].rearrange("p a b c -> p (a b c)").bitcast(F32)[:, i * 2048:(i + 1) * 2048] for i in range(2)]
            wmod = k[:].rearrange("p a b c -> p (a b c)").bitcast(F32)[:, 0:KD * 6 * D].rearrange("p (k n) -> p k n", k=KD)
            stage_src = [wqkv_in.rearrange("(k p) n -> p k n", p=P)[:, :, i * INNER:(i + 1) * INNER] for i in range(3)]
            stage_src.append(wout_in.rearrange("(j p) n -> p j n", p=P))
            stage_view = [stage[i % 2].rearrange("p (k n) -> p k n", k=KD if i < 3 else PAIRS) for i in range(4)]

            def stage_dst(i, part):
                return wqkv[:, :, part, i * INNER:(i + 1) * INNER] if i < 3 else wout[:, :, part, :]

            with nc.Block() as block:
                @block.sync
                def _(sp):
                    for b in range(B):
                        sp.dma_start(cT[:, :, b], c_in[b].rearrange("(k p) -> p k", p=P), allow_slow_non_contiguous=True)\
                          .then_inc(small_loaded, 16)
                    sp.dma_start(wmod, wmod_in.rearrange("(k p) n -> p k n", p=P)).then_inc(small_loaded, 16)
                    for kd in range(KD):
                        sp.dma_start(gwT[:, kd, :], gate_w[:, kd * P:(kd + 1) * P].rearrange("e p -> p e"),
                                     allow_slow_non_contiguous=True).then_inc(small_loaded, 16)
                    sp.dma_start(gbB[:], gate_b.partition_broadcast(P)).then_inc(small_loaded, 16)
                    for i in range(4):
                        if i >= 2:
                            sp.wait_ge(split_lo, i - 1)
                        sp.dma_start(stage_view[i], stage_src[i]).then_inc(stage_loaded[i], 16)
                    xt = x_rows.rearrange("(t p) d -> p t d", p=P)
                    sp.dma_start(x[:, 0:2 * TILES, :], xt[:, 0:2 * TILES, :]).then_inc(x0_loaded, 16)
                    sp.dma_start(x[:, 2 * TILES:, :], xt[:, 2 * TILES:, :]).then_inc(x_loaded, 16)

                @block.gpsimd
                def _(pool):
                    pool.memset(onesf[:], 1.0)
                    pool.memset(identf[:], 0.0)
                    pool.memset(keys_cur[:], 1.0).then_inc(consts, 1)
                    pool.wait_ge(consts, 1)
                    pool.affine_select(out=identf[:], in_=identf[:], pattern=[[-1, P]], compare_op=ALU.not_equal,
                                       fill=1.0, base=0, channel_multiplier=1)
                    pool.affine_select(out=above[:], in_=onesf[:], pattern=[[1, P]], compare_op=ALU.is_gt,
                                       fill=0.0, base=0, channel_multiplier=-1)
                    pool.affine_select(out=keys_cur[:], in_=keys_cur[:], pattern=[[1, P]], compare_op=ALU.is_ge,
                                       fill=0.0, base=0, channel_multiplier=-1)
                    pool.iota(expert_no[:], pattern=[[1, E]], base=0, channel_multiplier=0,
                              allow_small_or_imprecise_dtypes=True).then_inc(consts, 1)

                @block.vector
                def _(dve):
                    dve.memset(zero_row[:], 0.0)
                    dve.memset(ones_row[:], 1.0)
                    for c in range(NC):
                        dve.memset(no_prev[:, c, :], MASKED if c % CPB == 0 else 0.0)
                    dve.memset(carry[:], 0.0)
                    for c in range(K):
                        dve.memset(choice_base[:, :, c:c + 1], float(c * CAP))
                    dve.memset(half_neg[:], -0.5)
                    dve.wait_ge(consts, 2)
                    dve.tensor_copy(ident16[:], identf[:])
                    dve.wait_ge(exp_c, 1)
                    dve.tensor_scalar(silT[:, 1, :], silT[:, 0, :], 1.0, None, ALU.add).then_inc(sil, 1)
                    dve.wait_ge(sil, 1)
                    dve.reciprocal(silT[:, 2, :], silT[:, 1, :]).then_inc(sil, 1)
                    dve.wait_ge(sil, 2)
                    dve.tensor_tensor(silT[:, 0, :], silT[:, 2, :], cT[:].rearrange("p k b -> p (k b)"), ALU.mult).then_inc(sil, 1)
                    dve.wait_ge(sil, 3)
                    dve.tensor_copy(silB[:], silT[:, 0, :].unsqueeze(2).to_broadcast([P, KD * B, P])).then_inc(sil_b, 1)
                    dve.wait_ge(mod_mm, 1)
                    mc = gen[0][:, 0:4 * B].rearrange("p (j b) -> p j b", b=B)
                    dve.tensor_copy(modcol[:, 0:2, :], mc[:, 0:2, :])
                    dve.tensor_scalar(modcol[:, 2:4, :], mc[:, 2:4, :], 1.0, None, ALU.add)
                    for b in range(B):
                        dve.wait_ge(mod_mm, 2 + b)
                        ga, gb = score[b][:, 0:1, :], score[b][:, 3:4, :]
                        dve.tensor_copy(modrow[:, b, 1:2, :], score[b][:, 1:2, :])
                        dve.tensor_scalar(modrow[:, b, 2:3, :], score[b][:, 2:3, :], 1.0, None, ALU.add)
                        for n, (gate, row) in enumerate(((ga, 0), (gb, 3))):
                            dve.tensor_scalar(gated[:, 0:1, :], gate, 0.0, 2.0, ALU.is_ge, ALU.mult).then_inc(mod_row, 1)
                            dve.tensor_scalar(h2[:, 0:1, :], gate, -1.0, None, ALU.mult).then_inc(mod_row, 1)
                            dve.wait_ge(mod_row, 8 * b + 4 * n + 2)
                            dve.scalar_tensor_tensor(gated[:, 1:2, :], gate, 0.25, h2[:, 0:1, :], ALU.max, ALU.max).then_inc(mod_row, 1)
                            dve.wait_ge(mod_row, 8 * b + 4 * n + 3)
                            dve.scalar_tensor_tensor(modrow[:, b, row:row + 1, :], gated[:, 0:1, :], -1.0,
                                                     gated[:, 1:2, :], ALU.add, ALU.mult).then_inc(mod_row, 1)
                            dve.wait_ge(mod_row, 8 * b + 4 * n + 4)
                    for i in range(4):
                        dve.wait_ge(split_hi, i + 1)
                        dve.scalar_tensor_tensor(stage_dst(i, 1), stage_view[i], W_SCALE, stage_dst(i, 0),
                                                 ALU.mult, ALU.subtract).then_inc(split_lo, 1)

                @block.scalar
                def _(act):
                    act.wait_ge(small_loaded, 16 * (B + KD + 2))
                    act.activation(silT[:, 0, :], cT[:].rearrange("p k b -> p (k b)"), ACT.Exp, scale=-1.0).then_inc(exp_c, 1)
                    for i in range(4):
                        act.wait_ge(stage_loaded[i], 16)
                        act.activation(stage_dst(i, 0), stage_view[i], ACT.Copy, scale=W_SCALE).then_inc(split_hi, 1)

                @block.tensor
                def _(pe):
                    pe.wait_ge(sil, 3)
                    pe.wait_ge(small_loaded, 16 * (B + KD + 2))
                    silm = silT[:, 0, :].rearrange("p (k b) -> p k b", b=B)
                    for j in range(4):
                        for kd in range(KD):
                            mm = pe.matmul(gen[0][:, j * B:(j + 1) * B], wmod[:, kd, j * P:(j + 1) * P], silm[:, kd, :],
                                           start=(kd == 0), stop=(kd == KD - 1))
                    mm.then_inc(mod_mm, 1)
                    pe.wait_ge(sil_b, 1)
                    for b in range(B):
                        flat = score[b][:].rearrange("p a b -> p (a b)")
                        for half in range(2):
                            for kd in range(KD):
                                mm = pe.matmul(flat[:, half * 512:(half + 1) * 512], silB[:, kd * B + b, :],
                                               wmod[:, kd, 2 * D + half * 512:2 * D + (half + 1) * 512],
                                               start=(kd == 0), stop=(kd == KD - 1))
                        mm.then_inc(mod_mm, 1)

            ln_groups = [("lnT", 0), ("lnT", 1)]
            route_groups = [("h2T", 0), ("h2T", 1), ("logits",), ("counts",)]
            out_groups = [("out", 0), ("out", 1)]
            STEPS = H + 3
            v_half = lambda half: [("v", half, s) for s in range(TILES)]
            qk_pair = lambda j: [("q", j), ("k", j)]
            HEAD = ([("ln0", 0), ("ln0", 1), ("lnT", 0), ("lnT", 1)] + sum([qk_pair(j) for j in range(PAIRS)], [])
                    + v_half(0) + v_half(1))

            def chunk_groups(first, last):
                names = []
                for i in range(STEPS):
                    if i < H and i % 2 == 1 and not last:
                        names += qk_pair(i // 2)
                    if i in (H, H + 1) and not last:
                        names += v_half(0)[2 * (i - H):2 * (i - H) + 2]
                    if not first:
                        names += {4: route_groups[0:2], 6: route_groups[2:3], 10: route_groups[3:4]}.get(i, [])
                    if i == 8 and not last:
                        names += ln_groups
                return names + ([] if last else v_half(1)) + out_groups

            kinds = [HEAD, chunk_groups(True, False), chunk_groups(False, False), chunk_groups(False, True), route_groups]
            orders = [group_order(names) for names in kinds]

            def group(c, name):
                kind = 0 if isinstance(c, int) and c == -1 else 1 if isinstance(c, int) and c == 0 else \
                    4 if isinstance(c, int) and c == NC else 3 if isinstance(c, int) and c == NC - 1 else 2
                bank, before = orders[kind][0][name]
                counts = [o[1][bank] for o in orders]
                if kind >= 1:
                    before = before + counts[0]
                if kind == 2:
                    before = before + counts[1] + (c - 1) * counts[2]
                if kind >= 3:
                    before = before + counts[1] + (NC - 2) * counts[2]
                if kind == 4:
                    before = before + counts[3]
                return bank, before

            gen_full = [sem(f"gen_full{i}") for i in range(2)]
            gen_free = [sem(f"gen_free{i}") for i in range(2)]
            (scores_done, merged, maxed, neg_ready, exp_done, rinv_ready, norm_ready, hi_ready, lo_ready, pt_done,
             probT_ready, cur_ready, prev_ready, pv_done, attn_hi, attn_lo, proj_hi, k_halo, v_halo) = (sem(n) for n in (
                 "scores_done", "merged", "maxed", "neg_ready", "exp_done", "rinv_ready", "norm_ready", "hi_ready",
                 "lo_ready", "pt_done", "probT_ready", "cur_ready", "prev_ready", "pv_done", "attn_hi", "attn_lo",
                 "proj_hi", "k_halo", "v_halo"))
            ln_stat, ln_mv, ln_var, ln_rstd, ln_xn, ln_h32, ln_hi, ln_lo = (
                sem(n) for n in ("ln_stat", "ln_mv", "ln_var", "ln_rstd", "ln_xn", "ln_h32", "ln_hi", "ln_lo"))
            x2_ready, r_stat, r_mv, r_var, r_rstd, r_xn, r_scaled, r_h2, r_pack_hi, r_pack = (
                sem(n) for n in ("x2_ready", "r_stat", "r_mv", "r_var", "r_rstd", "r_xn", "r_scaled",
                                 "r_h2", "r_pack_hi", "r_pack"))
            r_soft, r_exp, r_count, r_send, sent = (sem(n) for n in ("r_soft", "r_exp", "r_count", "r_send", "sent"))
            PROJ = 2 * PAIRS + 2 * TILES

            def proj_no(c, name):
                n = 2 * name[1] + (name[0] == "k") if name[0] != "v" else 2 * PAIRS + TILES * name[1] + name[2]
                return c * PROJ + n + 1

            def batch(c):
                return c // CPB

            with nc.Block() as block:
                @block.sync
                def _(sp):
                    with sp.Fori(0, SLOTS // P) as i:
                        sp.dma_start(xbuf[bass.ts(i, P), :], zero_row[:]).then_inc(zero_sent, 16)
                    sp.wait_ge(zero_sent, 16 * (SLOTS // P))

                @block.tensor
                def _(pe):
                    def claim(c, name):
                        bank, before = group(c, name)
                        at_least(pe, gen_free[bank], before)
                        return gen[bank], gen_full[bank]

                    def ln_transposes(c, cn, label):
                        pe.wait_ge(ln_xn, cn + 1)
                        for kd in range(KD):
                            dst, full = claim(c, (label, kd))
                            for s in range(TILES):
                                mm = pe.transpose(dst[:, s * P:(s + 1) * P], xn[:, s, kd * P:(kd + 1) * P], identf[:])
                            mm.then_inc(full, 1)

                    def project_qk(c, j):
                        cn = c + 1
                        if j == 0:
                            pe.wait_ge(ln_lo, cn + 1)
                        for name, col in (("q", j * P), ("k", INNER + j * P)):
                            dst, full = claim(c, (name, j))
                            n = 0
                            for a, b in SPLIT_PRODUCTS:
                                for kd in range(KD):
                                    mm = pe.matmul(dst[:], wqkv[:, kd, a, col:col + P], hT[:, cn % 2, kd, b, :],
                                                   start=(n == 0), stop=(n == 5))
                                    n += 1
                            mm.then_inc(full, 1)

                    def project_v(c, half, tiles=range(TILES)):
                        cn = c + 1
                        for s in tiles:
                            dst, full = claim(c, ("v", half, s))
                            n = 0
                            for a, b in SPLIT_PRODUCTS:
                                for kd in range(KD):
                                    mm = pe.matmul(dst[:], hT[:, cn % 2, kd, a, s * P:(s + 1) * P],
                                                   wqkv[:, kd, b, 2 * INNER + half * 512:2 * INNER + (half + 1) * 512],
                                                   start=(n == 0), stop=(n == 5))
                                    n += 1
                            mm.then_inc(full, 1)

                    def scores(c, h):
                        u, j, r = H * c + h, h // 2, DH * (h % 2)
                        dst = score[h % 2]
                        if h % 2 == 0:
                            if isinstance(c, int) and c == 0:
                                for name in qk_pair(j):
                                    bank, before = group(-1, name)
                                    pe.wait_ge(gen_free[bank], before + 1)
                            else:
                                pe.wait_ge(norm_ready, H * (c - 1) + h + 2)
                        at_least(pe, exp_done, u - 1)
                        for b in range(TILES):
                            for n, (a, m) in enumerate(SPLIT_PRODUCTS):
                                mm = pe.matmul(dst[:, b, :], q[r:r + DH, j, a, b * P:(b + 1) * P],
                                               k[r:r + DH, j, m, b * P:(b + 2) * P], start=(n == 0),
                                               stop=(n == 2), skip_group_check=(b == 0))
                            if b == 0:
                                mm = pe.matmul(dst[:, 0, 0:P], ones_row[:], no_prev[:, c, :], start=False, stop=True,
                                               skip_group_check=True)
                        mm.then_inc(scores_done, 1)

                    def transposes(c, h):
                        u = H * c + h
                        pe.wait_ge(lo_ready, u + 1)
                        at_least(pe, probT_ready, u)
                        for part in range(2):
                            for b in range(TILES):
                                mm = pe.transpose(pt[:, part * TILES + b, :], prob16[:, h % 2, part, b, :], ident16[:])
                        mm.then_inc(pt_done, 1)

                    def weighted_values(c, h):
                        u, j, r = H * c + h, h // 2, DH * (h % 2)
                        pe.wait_ge(prev_ready, u + 1)
                        pe.wait_ge(cur_ready, u + 1)
                        if h % 2 == 0:
                            at_least(pe, attn_lo, PAIRS * c + j)
                        if h % (H // 2) == 0:
                            half = h // (H // 2)
                            if isinstance(c, int) and c == 0:
                                for s in range(TILES):
                                    bank, before = group(-1, ("v", half, s))
                                    pe.wait_ge(gen_free[bank], before + 1)
                            elif half == 0:
                                pe.wait_ge(attn_lo, PAIRS * c)
                            else:
                                pe.wait_ge(x2_ready, 2 * c)
                        for b in range(TILES):
                            n = 0
                            for a, m in SPLIT_PRODUCTS:
                                for blk, pr in ((b + 1, probT_cur), (b, probT_prev)):
                                    mm = pe.matmul(pv[r:r + DH, b * P:(b + 1) * P], v[:, blk, a, h * DH:(h + 1) * DH],
                                                   pr[:, h % 2, m * TILES + b, :], start=(n == 0), stop=(n == 5))
                                    n += 1
                        mm.then_inc(pv_done, 1)

                    def project_out(c):
                        pe.wait_ge(attn_lo, PAIRS * (c + 1))
                        for p in range(2):
                            dst, full = claim(c, ("out", p))
                            for s in range(2):
                                t = 2 * p + s
                                n = 0
                                for j in range(PAIRS):
                                    for a, b in SPLIT_PRODUCTS:
                                        mm = pe.matmul(dst[:, s * D:(s + 1) * D], attn[:, j, a, t * P:(t + 1) * P],
                                                       wout[:, j, b, :], start=(n == 0), stop=(n == 3 * PAIRS - 1))
                                        n += 1
                            mm.then_inc(full, 1)

                    def route_transposes(c):
                        pe.wait_ge(r_h2, c)
                        for kd in range(KD):
                            dst, full = claim(c, ("h2T", kd))
                            for s in range(TILES):
                                mm = pe.transpose(dst[:, s * P:(s + 1) * P], h2[:, s, kd * P:(kd + 1) * P], identf[:])
                            mm.then_inc(full, 1)

                    def route_logits(c):
                        for kd in range(KD):
                            bank, before = group(c, ("h2T", kd))
                            pe.wait_ge(gen_free[bank], before + 1)
                        dst, full = claim(c, ("logits",))
                        for s in range(TILES):
                            for kd in range(KD):
                                mm = pe.matmul(dst[:, s * E:(s + 1) * E], h2T[:, kd, s * P:(s + 1) * P], gwT[:, kd, :],
                                               start=(kd == 0), stop=(kd == KD - 1))
                        mm.then_inc(full, 1)

                    def route_counts(c):
                        pe.wait_ge(r_soft, 11 * c)
                        dst, full = claim(c, ("counts",))
                        KE = K * E
                        hot = onehot[:].rearrange("p s c e -> p s (c e)")
                        for s in range(TILES + 1):
                            last = min(s, TILES - 1)
                            for m in range(last + 1):
                                mm = pe.matmul(dst[:, s * KE:(s + 1) * KE], above[:] if m == s else onesf[:], hot[:, m, :],
                                               start=(m == 0), stop=(m == last))
                        mm.then_inc(full, 1)

                    def chunk(c, first, last):
                        for i in range(STEPS):
                            if i < H:
                                scores(c, i)
                            if i < H and i % 2 == 1 and not last:
                                project_qk(c, i // 2)
                            if i in (H, H + 1) and not last:
                                project_v(c, 0, range(2 * (i - H), 2 * (i - H) + 2))
                            if not first and i == 4:
                                route_transposes(c)
                            if not first and i == 6:
                                route_logits(c)
                            if not first and i == 10:
                                route_counts(c)
                            if i == 8 and not last:
                                ln_transposes(c, c + 2, "lnT")
                            if 2 <= i < H + 2:
                                transposes(c, i - 2)
                            if i >= 3:
                                weighted_values(c, i - 3)
                        if not last:
                            project_v(c, 1)
                        project_out(c)

                    ln_transposes(-1, 0, "ln0")
                    ln_transposes(-1, 1, "lnT")
                    for j in range(PAIRS):
                        project_qk(-1, j)
                    project_v(-1, 0)
                    project_v(-1, 1)
                    chunk(0, True, False)
                    with pe.Fori(1, NC - 1) as c:
                        chunk(c, False, False)
                    chunk(NC - 1, False, True)
                    route_transposes(NC)
                    route_logits(NC)
                    route_counts(NC)

                @block.scalar
                def _(act):
                    def ln_modulate(c, cn, label):
                        for kd in range(KD):
                            bank, before = group(c, (label, kd))
                            stand_ge(act, (gen_full[bank], before + 1))
                            at_least(act, ln_lo, cn)
                            b = batch(clip(cn))
                            act.activation(h32[:, kd, :], gen[bank][:], ACT.Identity,
                                           bias=modcol[:, kd, bass.ds(b, 1)], scale=modcol[:, 2 + kd, bass.ds(b, 1)])\
                               .then_inc(gen_free[bank], 1)

                    def high(c, name):
                        cn = c + 1
                        bank, before = group(c, name)
                        act.wait_ge(gen_full[bank], before + 1)
                        if name[0] == "q":
                            at_least(act, scores_done, H * c + 2 * name[1] + 2)
                            dst = q[:, name[1], 0, :]
                        elif name[0] == "k":
                            act.wait_ge(k_halo, PAIRS * cn + name[1] + 1)
                            dst = k[:, name[1], 0, P:]
                        else:
                            act.wait_ge(v_halo, 2 * cn + name[1] + 1)
                            dst = v[:, 1 + name[2], 0, name[1] * 512:(name[1] + 1) * 512]
                        act.activation(dst, gen[bank][:], ACT.Copy, scale=1 / W_SCALE).then_inc(proj_hi, 1)

                    def exponentials(c, h):
                        u = H * c + h
                        act.wait_ge(neg_ready, u + 1)
                        at_least(act, lo_ready, u - 1)
                        for b in range(TILES):
                            mm = act.activation(prob[:, h % 2, b, :], score[h % 2][:, b, P:], ACT.Exp, scale=DH ** -0.5,
                                                bias=negmax[:, h % 2, b:b + 1], accum_out=rowsum[:, h % 2, b:b + 1])
                        mm.then_inc(exp_done, 1)

                    def prob_high(c, h):
                        u = H * c + h
                        act.wait_ge(norm_ready, u + 1)
                        at_least(act, pt_done, u - 1)
                        act.activation(prob16[:, h % 2, 0], prob[:, h % 2], ACT.Copy).then_inc(hi_ready, 1)

                    def copy_probT(c, h):
                        u = H * c + h
                        act.wait_ge(pt_done, u + 1)
                        at_least(act, prev_ready, u - 1)
                        at_least(act, cur_ready, u - 1)
                        act.activation(probT[:, h % 2], pt[:], ACT.Copy).then_inc(probT_ready, 1)

                    def attn_high(c, j):
                        act.wait_ge(pv_done, H * c + 2 * j + 2)
                        if j == 0:
                            at_least(act, x2_ready, 2 * c)
                        act.activation(attn[:, j, 0, :], pv[:], ACT.Copy).then_inc(attn_hi, 1)

                    def route_pack(c):
                        act.wait_ge(r_h2, c)
                        act.wait_ge(lo_ready, H * c)
                        act.activation(packed[:, :, 0:D], h2[:], ACT.Copy).then_inc(r_pack_hi, 1)

                    def route_h2T(c):
                        for kd in range(KD):
                            bank, before = group(c, ("h2T", kd))
                            act.wait_ge(gen_full[bank], before + 1)
                            act.activation(h2T[:, kd, :], gen[bank][:], ACT.Copy).then_inc(gen_free[bank], 1)

                    def route_exp(c):
                        act.wait_ge(r_soft, 11 * (c - 1) + 3)
                        act.activation(logit[:], logit[:], ACT.Exp).then_inc(r_exp, 1)

                    def chunk(c, first, last):
                        for i in range(STEPS):
                            if 1 <= i <= H:
                                exponentials(c, i - 1)
                            if i < H and i % 2 == 1 and not last:
                                high(c, ("q", i // 2))
                                high(c, ("k", i // 2))
                            if i in (H, H + 1) and not last:
                                for s in range(2):
                                    high(c, ("v", 0, 2 * (i - H) + s))
                            if not first and i == 4:
                                route_h2T(c)
                            if i == 8 and not last:
                                ln_modulate(c, c + 2, "lnT")
                            if 1 <= i <= H:
                                prob_high(c, i - 1)
                            if 2 <= i < H + 2:
                                copy_probT(c, i - 2)
                            if not first and i == 4:
                                route_pack(c)
                            if not first and i == 7:
                                route_exp(c)
                            if i >= 4 and i % 2 == 0:
                                attn_high(c, (i - 4) // 2)
                        if not last:
                            for s in range(TILES):
                                high(c, ("v", 1, s))

                    def clip(cn):
                        return cn % NC

                    ln_modulate(-1, 0, "ln0")
                    ln_modulate(-1, 1, "lnT")
                    for name in HEAD[4:]:
                        high(-1, name)
                    chunk(0, True, False)
                    with act.Fori(1, NC - 1) as c:
                        chunk(c, False, False)
                    chunk(NC - 1, False, True)
                    route_h2T(NC)
                    route_pack(NC)
                    route_exp(NC)

                @block.vector
                def _(dve):
                    def clip(cn):
                        return cn % NC

                    def norm_stats(tile0, st, mv, stat_sem, mv_sem, n):
                        for s in range(TILES):
                            op = dve.bn_stats(st[:, s, :], x[:, tile0 + s, :])
                        op.then_inc(stat_sem, 1)
                        stand_ge(dve, (stat_sem, n))
                        for s in range(TILES):
                            op = dve.bn_aggr(mv[:, s, :], st[:, s, :])
                        op.then_inc(mv_sem, 1)

                    def norm_rows(tile0, dst, mv, rs, rs_sem, xn_sem, n):
                        dve.wait_ge(rs_sem, n)
                        for s in range(TILES):
                            op = dve.tensor_scalar(dst[:, s, :], x[:, tile0 + s, :], mv[:, s, 0:1], rs[:, 1, s:s + 1],
                                                   ALU.subtract, ALU.mult)
                        op.then_inc(xn_sem, 1)

                    def ln_first(cn):
                        norm_stats(clip(cn) * TILES, stats[0], meanvar[0], ln_stat, ln_mv, cn + 1)

                    def ln_second(cn):
                        norm_rows(clip(cn) * TILES, xn, meanvar[0], rstd[0], ln_rstd, ln_xn, cn + 1)

                    def ln_high(c, cn, label):
                        for kd in range(KD):
                            bank, before = group(c, (label, kd))
                            dve.wait_ge(gen_free[bank], before + 1)
                        dve.tensor_copy(hT[:, cn % 2, :, 0, :], h32[:]).then_inc(ln_hi, 1)

                    def low(c, name):
                        cn = c + 1
                        bank, _ = group(c, name)
                        dve.wait_ge(proj_hi, proj_no(cn, name))
                        if name[0] == "q":
                            hi, lo = q[:, name[1], 0, :], q[:, name[1], 1, :]
                        elif name[0] == "k":
                            hi, lo = k[:, name[1], 0, P:], k[:, name[1], 1, P:]
                        else:
                            hi, lo = (v[:, 1 + name[2], m, name[1] * 512:(name[1] + 1) * 512] for m in range(2))
                        dve.scalar_tensor_tensor(lo, gen[bank][:], 1 / W_SCALE, hi, ALU.mult, ALU.subtract)\
                           .then_inc(gen_free[bank], 1)

                    def keep_k(c, j):
                        dve.wait_ge(scores_done, H * c + 2 * j + 2)
                        dve.tensor_copy(k[:, j, :, 0:P], k[:, j, :, CHUNK:]).then_inc(k_halo, 1)

                    def keep_v(c, half):
                        dve.wait_ge(pv_done, H * c + (H // 2) * (half + 1))
                        cols = slice(half * 512, (half + 1) * 512)
                        dve.tensor_copy(v[:, 0, :, cols], v[:, TILES, :, cols]).then_inc(v_halo, 1)

                    def mask_own(c, h):
                        u = H * c + h
                        dve.wait_ge(probT_ready, u + 1)
                        at_least(dve, pv_done, u - 1)
                        dve.tensor_tensor(probT_cur[:, h % 2], probT[:, h % 2],
                                          keys_cur[:].unsqueeze(1).to_broadcast([P, 2 * TILES, P]), ALU.mult).then_inc(cur_ready, 1)

                    def row_max(c, h):
                        u = H * c + h
                        sc = score[h % 2]
                        stand_ge(dve, (scores_done, u + 1))
                        dve.copy_predicated(sc[:, :, P:], above[:].bitcast(I32).unsqueeze(1).to_broadcast([P, TILES, P]), sc[:, :, 0:P])\
                           .then_inc(merged, 1)
                        dve.wait_ge(merged, u + 1)
                        dve.reduce_max(rowmax[:, h % 2, :], sc[:, :, P:], AX.X).then_inc(maxed, 1)
                        dve.wait_ge(maxed, u + 1)
                        dve.tensor_scalar(negmax[:, h % 2, :], rowmax[:, h % 2, :], -(DH ** -0.5), None, ALU.mult).then_inc(neg_ready, 1)

                    def invert_sum(c, h):
                        dve.wait_ge(exp_done, H * c + h + 1)
                        dve.reciprocal(rinv[:, h % 2, :], rowsum[:, h % 2, :]).then_inc(rinv_ready, 1)

                    def normalise(c, h):
                        dve.wait_ge(rinv_ready, H * c + h + 1)
                        dve.tensor_tensor(prob[:, h % 2], prob[:, h % 2], rinv[:, h % 2, :].unsqueeze(2).to_broadcast([P, TILES, P]), ALU.mult)\
                           .then_inc(norm_ready, 1)

                    def attn_low(c, j):
                        dve.wait_ge(attn_hi, PAIRS * c + j + 1)
                        dve.tensor_tensor(attn[:, j, 1, :], pv[:], attn[:, j, 0, :], ALU.subtract).then_inc(attn_lo, 1)

                    def add_attention(c):
                        for p in range(2):
                            bank, before = group(c, ("out", p))
                            at_least(dve, x2_ready, 2 * c + p)
                            dve.wait_ge(gen_full[bank], before + 1)
                            ga = modrow[:, batch(c), 0:1, :].to_broadcast([P, 2, D])
                            dve.scalar_tensor_tensor(gated[:], gen[bank][:].rearrange("p (s d) -> p s d", s=2), 1 / W_SCALE,
                                                     ga, ALU.mult, ALU.mult).then_inc(gen_free[bank], 1)
                            dve.wait_ge(gen_free[bank], before + 1)
                            tiles = x[:, bass.ds(c * TILES + 2 * p, 2), :]
                            dve.tensor_tensor(tiles, tiles, gated[:], ALU.add).then_inc(x2_ready, 1)

                    def route_rows(c):
                        g = c - 1
                        dve.wait_ge(r_xn, c)
                        wide = [P, TILES, D]
                        dve.tensor_tensor(h2[:], h2[:], modrow[:, batch(g), 2:3, :].to_broadcast(wide), ALU.mult).then_inc(r_scaled, 1)
                        dve.wait_ge(r_scaled, c)
                        dve.tensor_tensor(h2[:], h2[:], modrow[:, batch(g), 1:2, :].to_broadcast(wide), ALU.add).then_inc(r_h2, 1)

                    def route_low(c):
                        dve.wait_ge(r_pack_hi, c)
                        dve.tensor_tensor(packed[:, :, D:], h2[:], packed[:, :, 0:D], ALU.subtract).then_inc(r_pack, 1)

                    def route_softmax(c):
                        bank, before = group(c, ("logits",))
                        n = 11 * (c - 1)
                        dve.wait_ge(gen_full[bank], before + 1)
                        dve.tensor_tensor(logit[:], gen[bank][:, 0:TILES * E].rearrange("p (s e) -> p s e", e=E),
                                          gbB[:].unsqueeze(1).to_broadcast([P, TILES, E]), ALU.add).then_inc(gen_free[bank], 1)
                        dve.wait_ge(gen_free[bank], before + 1)
                        dve.reduce_max(lmax[:], logit[:], AX.X).then_inc(r_soft, 2)
                        dve.wait_ge(r_soft, n + 2)
                        dve.tensor_tensor(logit[:], logit[:], lmax[:].unsqueeze(2).to_broadcast([P, TILES, E]), ALU.subtract).then_inc(r_soft, 1)

                    def route_top(c):
                        n = 11 * (c - 1)
                        dve.wait_ge(r_exp, c)
                        dve.reduce_sum(lsum[:, 0, :], logit[:], AX.X).then_inc(r_soft, 1)
                        dve.wait_ge(r_soft, n + 4)
                        dve.reciprocal(lsum[:, 1, :], lsum[:, 0, :]).then_inc(r_soft, 1)
                        dve.wait_ge(r_soft, n + 5)
                        dve.tensor_tensor(logit[:], logit[:], lsum[:, 1, :].unsqueeze(2).to_broadcast([P, TILES, E]), ALU.mult).then_inc(r_soft, 1)
                        stand_ge(dve, (r_soft, n + 6))
                        for s in range(TILES):
                            op = dve.max(top[:, s, :], logit[:, s, :])
                        op.then_inc(r_soft, 1)
                        stand_ge(dve, (r_soft, n + 7))
                        for s in range(TILES):
                            op = dve.max_index(topi[:, s, :], top[:, s, :], logit[:, s, :])
                        op.then_inc(r_soft, 1)
                        dve.wait_ge(r_soft, n + 8)
                        dve.tensor_copy(topf[:], topi[:, :, 0:K]).then_inc(r_soft, 1)
                        dve.wait_ge(r_soft, n + 9)
                        for m in range(K):
                            dve.tensor_tensor(onehot[:, :, m, :], expert_no[:].unsqueeze(1).to_broadcast([P, TILES, E]),
                                              topf[:, :, m:m + 1].to_broadcast([P, TILES, E]), ALU.is_equal).then_inc(r_soft, 1)

                    def route_slots(c):
                        g = c - 1
                        n = 8 * (c - 1)
                        KE = K * E
                        bank, before = group(c, ("counts",))
                        dve.wait_ge(gen_full[bank], before + 1)
                        flat = cum[:].rearrange("p s c e -> p s (c e)")
                        cflat = carry[:].rearrange("p c e -> p (c e)")
                        dve.tensor_tensor(flat, gen[bank][:, 0:TILES * KE].rearrange("p (s n) -> p s n", n=KE),
                                          cflat.unsqueeze(1).to_broadcast([P, TILES, KE]), ALU.add).then_inc(r_count, 1)
                        dve.wait_ge(r_count, n + 1)
                        dve.tensor_tensor(cflat, cflat, gen[bank][:, TILES * KE:(TILES + 1) * KE], ALU.add).then_inc(gen_free[bank], 1)
                        dve.tensor_tensor(cum[:], cum[:], onehot[:], ALU.mult).then_inc(r_count, 1)
                        dve.wait_ge(r_count, n + 2)
                        dve.reduce_sum(pos[:], cum[:], AX.X).then_inc(r_count, 1)
                        dve.wait_ge(r_count, n + 3)
                        tile0 = g * TILES
                        dve.scalar_tensor_tensor(weight[:, bass.ds(tile0, TILES), :], pos[:], float(CAP), top[:, :, 0:K], ALU.is_lt, ALU.mult)
                        dve.tensor_scalar(drop[:], pos[:], float(CAP), FAR, ALU.is_ge, ALU.mult)
                        dve.tensor_tensor(posc[:], pos[:], choice_base[:], ALU.add).then_inc(r_count, 1)
                        dve.wait_ge(r_count, n + 4)
                        dve.scalar_tensor_tensor(slot[:], topf[:], float(K * CAP), posc[:], ALU.mult, ALU.add).then_inc(r_count, 1)
                        dve.wait_ge(r_count, n + 5)
                        dve.tensor_scalar(fetch[:, bass.ds(tile0, TILES), :], slot[:], float(SLOTS - 1), None, ALU.min).then_inc(r_count, 3)
                        dve.wait_ge(lo_ready, H * c)
                        dve.tensor_tensor(send[:], slot[:], drop[:], ALU.add).then_inc(r_send, 1)

                    def chunk(c, first, last):
                        if not first:
                            dve.wait_ge(x2_ready, 2 * c)
                            norm_stats((c - 1) * TILES, stats[1], meanvar[1], r_stat, r_mv, c)
                        for i in range(STEPS):
                            if i >= 5 and i % 2 == 1:
                                attn_low(c, (i - 5) // 2)
                            if 2 <= i <= H and i % 2 == 0 and not last:
                                keep_k(c, i // 2 - 1)
                                low(c, ("q", i // 2 - 1))
                                low(c, ("k", i // 2 - 1))
                            if i in (H + 1, H + 2) and not last:
                                for s in range(2):
                                    low(c, ("v", 0, 2 * (i - H - 1) + s))
                            if not first and i == 7:
                                route_softmax(c)
                            if not first and i == 11:
                                route_slots(c)
                            if 1 <= i <= H:
                                invert_sum(c, i - 1)
                            if i >= 3:
                                mask_own(c, i - 3)
                            if 1 <= i <= H:
                                normalise(c, i - 1)
                            if i < H:
                                row_max(c, i)
                            if i == H and not last:
                                keep_v(c, 0)
                            if not first and i == 1:
                                norm_rows((c - 1) * TILES, h2, meanvar[1], rstd[1], r_rstd, r_xn, c)
                            if not first and i == 2:
                                route_rows(c)
                            if not first and i == 5:
                                route_low(c)
                            if not first and i == 8:
                                route_top(c)
                            if i == 4 and not last:
                                ln_first(c + 2)
                            if i == 6 and not last:
                                ln_second(c + 2)
                            if i == 9 and not last:
                                ln_high(c, c + 2, "lnT")
                        attn_low(c, PAIRS - 1)
                        if not last:
                            keep_v(c, 1)
                            for s in range(TILES):
                                low(c, ("v", 1, s))
                        add_attention(c)

                    dve.wait_ge(x0_loaded, 16)
                    dve.memset(k[:, :, :, 0:P], 0.0).then_inc(k_halo, PAIRS)
                    dve.memset(v[:, 0, :, :], 0.0).then_inc(v_halo, 2)
                    ln_first(0)
                    ln_second(0)
                    ln_high(-1, 0, "ln0")
                    ln_first(1)
                    ln_second(1)
                    ln_high(-1, 1, "lnT")
                    for name in HEAD[4:]:
                        low(-1, name)
                    dve.wait_ge(x_loaded, 16)
                    chunk(0, True, False)
                    with dve.Fori(1, NC - 1) as c:
                        chunk(c, False, False)
                    chunk(NC - 1, False, True)
                    dve.wait_ge(x2_ready, 2 * NC)
                    norm_stats((NC - 1) * TILES, stats[1], meanvar[1], r_stat, r_mv, NC)
                    norm_rows((NC - 1) * TILES, h2, meanvar[1], rstd[1], r_rstd, r_xn, NC)
                    route_rows(NC)
                    route_low(NC)
                    route_softmax(NC)
                    route_top(NC)
                    route_slots(NC)

                @block.gpsimd
                def _(pool):
                    def reciprocal_std(mv, rs, mv_sem, var_sem, rs_sem, n):
                        stand_ge(pool, (mv_sem, n))
                        pool.tensor_scalar(rs[:, 0, :], mv[:, :, 1], 1e-5, None, ALU.add).then_inc(var_sem, 1)
                        pool.wait_ge(var_sem, n)
                        pool.tensor_tensor(rs[:, 1, :], rs[:, 0, :], half_neg[:], ALU.pow).then_inc(rs_sem, 1)

                    def ln_rstd_of(cn):
                        reciprocal_std(meanvar[0], rstd[0], ln_mv, ln_var, ln_rstd, cn + 1)

                    def ln_low(cn):
                        pool.wait_ge(ln_hi, cn + 1)
                        pool.tensor_tensor(hT[:, cn % 2, :, 1, :], h32[:], hT[:, cn % 2, :, 0, :], ALU.subtract).then_inc(ln_lo, 1)

                    def prob_low(c, h):
                        pool.wait_ge(hi_ready, H * c + h + 1)
                        pool.tensor_tensor(prob16[:, h % 2, 1], prob[:, h % 2], prob16[:, h % 2, 0], ALU.subtract).then_inc(lo_ready, 1)

                    def mask_previous(c, h):
                        u = H * c + h
                        waits = [(probT_ready, u + 1)]
                        if not isinstance(c, int) or u >= 2:
                            waits.append((pv_done, u - 1))
                        stand_ge(pool, *waits)
                        pool.affine_select(out=probT_prev[:, h % 2], in_=probT[:, h % 2], pattern=[[0, 2 * TILES], [-1, P]],
                                           compare_op=ALU.is_gt, fill=zero, base=0, channel_multiplier=1).then_inc(prev_ready, 1)

                    def scatter(c):
                        stand_ge(pool, (r_pack, c))
                        pool.wait_ge(r_send, c)
                        for s in range(TILES):
                            for m in range(K):
                                pool.indirect_dma_start(
                                    out=xbuf, out_offset=bass.IndirectOffsetOnAxis(ap=send[:, s, m:m + 1], axis=0),
                                    in_=packed[:, s, :], in_offset=None, bounds_check=limit, oob_is_err=False)\
                                    .then_inc(sent, 16)

                    def chunk(c, first, last):
                        if not first:
                            reciprocal_std(meanvar[1], rstd[1], r_mv, r_var, r_rstd, c)
                        for i in range(STEPS):
                            if i >= 3:
                                mask_previous(c, i - 3)
                            if i == 5 and not last:
                                ln_rstd_of(c + 2)
                            if not first and i == 12:
                                scatter(c)
                            if i == 11 and not last:
                                ln_low(c + 2)
                            if not first and i == H:
                                pool.wait_ge(sent, 16 * TILES * K * c)
                            if 1 <= i <= H:
                                prob_low(c, i - 1)

                    limit = pool.to_reg(SLOTS - 1)
                    zero = pool.to_reg(0.0)
                    ln_rstd_of(0)
                    ln_low(0)
                    ln_rstd_of(1)
                    ln_low(1)
                    pool.wait_ge(zero_sent, 16 * (SLOTS // P))
                    chunk(0, True, False)
                    with pool.Fori(1, NC - 1) as c:
                        chunk(c, False, False)
                    chunk(NC - 1, False, True)
                    reciprocal_std(meanvar[1], rstd[1], r_mv, r_var, r_rstd, NC)
                    scatter(NC)
                    pool.wait_ge(sent, 16 * TILES * K * NC)

        ffn_stack = ExitStack()
        with ffn_stack:
            sb = alloc(ffn_stack)
            ps = lambda name, shape, dt: ffn_stack.enter_context(nc.psum_tensor(name, shape, dt))
            w32 = sb("w32", [P, 2, 2048], F32)
            w1 = sb("w1", [P, 2, KD, 2, FF], F16)
            w2 = sb("w2", [P, 2, FT, 2, D], F16)
            rows = sb("rows", [P, 2, ST, 2 * D], F16)
            xT = sb("xT", [P, 2, 2 * KD, ST * P], F16)
            hid = sb("hid", [P, FT, 2, ST * P], F16)
            hid32 = sb("hid32", [P, 4, 512], F32)
            b1T = sb("b1T", [P, E, FT], F32)
            b2B = sb("b2B", [P, E, D], F32)
            y32 = sb("y32", [P, 2, 2, D], F32)
            up = [ps(f"up{i}", [P, 512], F32) for i in range(4)]
            down = [ps(f"down{i}", [P, 2, D], F32) for i in range(2)]
            tp = [ps(f"tp{i}", [P, 2 * KD, 2, P], F16) for i in range(2)]

            bias_loaded = sem("bias_loaded")
            rows_loaded = [sem(f"rows_loaded{i}") for i in range(2)]
            (w_loaded, w_hi, w_lo, xT_full, xT_ready, up_full, up_out, hid_hi, hid_ready, down_full,
             y_ready) = (sem(n) for n in ("w_loaded", "w_hi", "w_lo", "xT_full", "xT_ready", "up_full",
                                          "up_out", "hid_hi", "hid_ready", "down_full", "y_ready"))
            y_sent = [sem(f"y_sent{i}") for i in range(2)]
            UG = len(NPART) * FT
            DG = ST // 2
            w1v = w1_in.rearrange("e (k p) n -> e p k n", p=P)
            w2v = w2_in.rearrange("e (f p) n -> e p f n", p=P)
            rowv = xbuf.rearrange("(e t p) d -> e p t d", p=P, t=ST)
            yv = ybuf.rearrange("(e g s p) d -> e g p s d", p=P, s=2, g=DG)

            def split_views(par, i, part):
                if i < 2:
                    return w32[:, 0, i * FF:(i + 1) * FF], w1[:, par, i, part, :]
                f = (i - 2) * FT // 2
                return (w32[:, 1, (i - 2) * 1024:(i - 1) * 1024].rearrange("p (f n) -> p f n", n=D),
                        w2[:, par, f:f + FT // 2, part, :])

            with nc.Block() as block:
                @block.sync
                def _(sp):
                    sp.dma_start(b1T[:].rearrange("p e f -> p (e f)"), b1_in.rearrange("e (f p) -> p (e f)", p=P), allow_slow_non_contiguous=True).then_inc(bias_loaded, 16)
                    sp.dma_start(b2B[:], b2_in.partition_broadcast(P)).then_inc(bias_loaded, 16)

                    def load_weights(e):
                        if not isinstance(e, int) or e > 0:
                            sp.wait_ge(w_lo, 4 * e)
                        sp.dma_start(w32[:, 0, :].rearrange("p (k n) -> p k n", k=KD),
                                     w1v[bass.ds(e, 1)].rearrange("e p k n -> (e p) k n")).then_inc(w_loaded, 16)
                        sp.dma_start(w32[:, 1, :].rearrange("p (f n) -> p f n", f=FT),
                                     w2v[bass.ds(e, 1)].rearrange("e p f n -> (e p) f n")).then_inc(w_loaded, 16)

                    def load_rows(e, par):
                        if not isinstance(e, int) or e > 0:
                            sp.wait_ge(xT_full, DG * e)
                        sp.dma_start(rows[:, par], rowv[bass.ds(e, 1)].rearrange("e p t d -> (e p) t d")).then_inc(rows_loaded[par], 16)

                    def store(e, g, par):
                        sp.wait_ge(y_ready, 2 + DG * e + g + 1)
                        n = (par * DG + g) % 2
                        sp.dma_start(yv[bass.ds(e, 1), g].rearrange("e p s d -> (e p) s d"), y32[:, n]).then_inc(y_sent[n], 16)

                    for n in range(2):
                        sp.sem_inc(y_sent[n], 16)
                    load_weights(0)
                    load_rows(0, 0)
                    def expert(e, par, last):
                        if not last:
                            load_weights(e + 1)
                            load_rows(e + 1, 1 - par)
                        for g in range(DG):
                            store(e, g, par)

                    with sp.Fori(0, E // 2 - 1) as i:
                        for par in range(2):
                            expert(2 * i + par, par, False)
                    expert(E - 2, 0, False)
                    expert(E - 1, 1, True)
                    for n in range(2):
                        sp.wait_ge(y_sent[n], 16 * (E * DG // 2 + 1))

                @block.tensor
                def _(pe):
                    def transposes(e, par):
                        pe.wait_ge(rows_loaded[par], 8 * (e - par) + 16)
                        for g in range(DG):
                            n = (par * DG + g) % 2
                            pe.wait_ge(xT_ready, DG * e + g + 1)
                            for s in range(2):
                                for m in range(2 * KD):
                                    mm = pe.transpose(tp[n][:, m, s, :], rows[:, par, 2 * g + s, m * P:(m + 1) * P], ident16[:])
                            mm.then_inc(xT_full, 1)

                    def go_up(e, par, n):
                        if n == 0:
                            pe.wait_ge(w_lo, 4 * (e + 1))
                        lo, size = NPART[n]
                        pe.wait_ge(xT_ready, 2 + DG * e + (lo + size) // (2 * P))
                        for ft in range(FT):
                            g = UG * e + n * FT + ft
                            bank = up[ft % 4]
                            pe.wait_ge(up_out, g + 1)
                            i = 0
                            for kd in range(KD):
                                for a, b in SPLIT_PRODUCTS:
                                    mm = pe.matmul(bank[:, 0:size], w1[:, par, kd, a, ft * P:(ft + 1) * P],
                                                   xT[:, par, b * KD + kd, lo:lo + size], start=(i == 0), stop=(i == 5))
                                    i += 1
                            mm.then_inc(up_full, 1)

                    def go_down(e, par, g):
                        n = (par * DG + g) % 2
                        part = min(g // 2, 2)
                        pe.wait_ge(hid_ready, 4 + UG * e + (part + 1) * FT)
                        pe.wait_ge(y_ready, DG * e + g + 1)
                        for s in range(2):
                            t = 2 * g + s
                            i = 0
                            for ft in range(FT):
                                for a, b in SPLIT_PRODUCTS:
                                    mm = pe.matmul(down[n][:, s, :], hid[:, ft, a, t * P:(t + 1) * P], w2[:, par, ft, b, :],
                                                   start=(i == 0), stop=(i == 3 * FT - 1))
                                    i += 1
                        mm.then_inc(down_full, 1)

                    def expert(e, par, last):
                        go_up(e, par, 0)
                        go_up(e, par, 1)
                        go_down(e, par, 0)
                        go_down(e, par, 1)
                        go_up(e, par, 2)
                        go_down(e, par, 2)
                        go_down(e, par, 3)
                        if not last:
                            transposes(e + 1, 1 - par)
                        go_down(e, par, 4)

                    pe.sem_inc(down_full, DG)
                    pe.sem_inc(xT_full, DG)
                    pe.sem_inc(up_full, UG)
                    transposes(0, 0)
                    with pe.Fori(0, E // 2 - 1) as i:
                        for par in range(2):
                            expert(2 * i + par, par, False)
                    expert(E - 2, 0, False)
                    expert(E - 1, 1, True)

                @block.scalar
                def _(act):
                    act.wait_ge(bias_loaded, 32)

                    def split_high(e, par, i):
                        if i == 0:
                            act.wait_ge(w_loaded, 32 * (e + 1))
                            if not isinstance(e, int) or e > 1:
                                act.wait_ge(down_full, DG * e)
                        src, dst = split_views(par, i, 0)
                        act.activation(dst, src, ACT.Copy, scale=W_SCALE).then_inc(w_hi, 1)

                    def expert(e, par, last):
                        for k_ in range(UG):
                            n, ft = divmod(k_, FT)
                            g = UG * e + k_
                            size = NPART[n][1]
                            stand_ge(act, (up_full, UG + g + 1), (hid_ready, g + 1))
                            act.activation(hid32[:, k_ % 4, 0:size], up[ft % 4][:, 0:size], ACT.Relu, scale=1 / W_SCALE,
                                           bias=b1T[:, bass.ds(e, 1), ft:ft + 1].rearrange("p a b -> p (a b)")).then_inc(up_out, 1)
                            if k_ % 4 == 3 and 1 <= k_ // 4 <= 4 and not last:
                                split_high(e + 1, 1 - par, k_ // 4 - 1)

                    act.sem_inc(up_out, len(up))
                    for i in range(4):
                        split_high(0, 0, i)
                    with act.Fori(0, E // 2 - 1) as i:
                        for par in range(2):
                            expert(2 * i + par, par, False)
                    expert(E - 2, 0, False)
                    expert(E - 1, 1, True)

                @block.vector
                def _(dve):
                    dve.wait_ge(bias_loaded, 32)

                    def split_low(e, par, i):
                        dve.wait_ge(w_hi, 4 * e + i + 1)
                        src, hi = split_views(par, i, 0)
                        _, lo = split_views(par, i, 1)
                        dve.scalar_tensor_tensor(lo, src, W_SCALE, hi, ALU.mult, ALU.subtract).then_inc(w_lo, 1)

                    def copy_xT(e, par):
                        for g in range(DG):
                            n = (par * DG + g) % 2
                            dve.wait_ge(xT_full, DG * (e + 1) + g + 1)
                            if g == 0 and (not isinstance(e, int) or e > 0):
                                dve.wait_ge(up_full, UG * e)
                            dve.tensor_copy(xT[:, par, :, 2 * g * P:2 * (g + 1) * P],
                                            tp[n][:].rearrange("p m s q -> p m (s q)")).then_inc(xT_ready, 1)

                    def hidden(e, k_):
                        n, ft = divmod(k_, FT)
                        g = UG * e + k_
                        lo, size = NPART[n]
                        dve.wait_ge(up_out, 4 + g + 1)
                        if ft == 0:
                            dve.wait_ge(down_full, DG * e + min(2 * (n + 1), DG))
                        dve.tensor_copy(hid[:, ft, 0, lo:lo + size], hid32[:, k_ % 4, 0:size]).then_inc(hid_hi, 1)
                        dve.wait_ge(hid_hi, g + 1)
                        dve.tensor_tensor(hid[:, ft, 1, lo:lo + size], hid32[:, k_ % 4, 0:size],
                                          hid[:, ft, 0, lo:lo + size], ALU.subtract).then_inc(hid_ready, 1)

                    def finish(e, par, g):
                        n = (par * DG + g) % 2
                        dve.wait_ge(down_full, DG * (e + 1) + g + 1)
                        dve.wait_ge(y_sent[n], 8 * (DG * e + g - n) + 16)
                        b2 = b2B[:, bass.ds(e, 1), :].to_broadcast([P, 2, D])
                        dve.scalar_tensor_tensor(y32[:, n], down[n][:], 1 / W_SCALE, b2, ALU.mult, ALU.add).then_inc(y_ready, 1)

                    def expert(e, par, last):
                        for k_ in range(2 * FT):
                            hidden(e, k_)
                            if k_ % 4 == 3 and k_ // 4 >= 1 and not last:
                                split_low(e + 1, 1 - par, k_ // 4 - 1)
                        finish(e, par, 0)
                        finish(e, par, 1)
                        for k_ in range(2 * FT, UG):
                            hidden(e, k_)
                            if k_ % 4 == 3 and k_ == 19 and not last:
                                split_low(e + 1, 1 - par, 3)
                        finish(e, par, 2)
                        finish(e, par, 3)
                        if not last:
                            copy_xT(e + 1, 1 - par)
                        finish(e, par, 4)

                    dve.sem_inc(hid_ready, 4)
                    dve.sem_inc(xT_ready, len(tp))
                    dve.sem_inc(y_ready, len(down))
                    for i in range(4):
                        split_low(0, 0, i)
                    copy_xT(0, 0)
                    with dve.Fori(0, E // 2 - 1) as i:
                        for par in range(2):
                            expert(2 * i + par, par, False)
                    expert(E - 2, 0, False)
                    expert(E - 1, 1, True)

        fin_stack = ExitStack()
        with fin_stack:
            sb = alloc(fin_stack)
            RING = 4
            ytok = sb("ytok", [P, RING, K, D], F32)
            mixed = sb("mixed", [P, RING, 2, D], F32)
            fetched = [sem(f"fetched{r}") for r in range(RING)]
            out_sent = sem("out_sent")
            f_mix, out_ready = sem("f_mix"), sem("out_ready")
            with nc.Block() as block:
                @block.gpsimd
                def _(pool):
                    def fetch_tiles(i):
                        for r in range(RING):
                            at_least(pool, f_mix, 3 * (RING * (i - 1) + r + 1))
                            for m in range(K):
                                pool.indirect_dma_start(
                                    out=ytok[:, r, m, :], out_offset=None, in_=ybuf,
                                    in_offset=bass.IndirectOffsetOnAxis(
                                        ap=fetch[:, RING * i + r, m:m + 1], axis=0),
                                    bounds_check=SLOTS - 1, oob_is_err=False).then_inc(fetched[r], 16)

                    for i in range(NT // RING):
                        fetch_tiles(i)

                @block.vector
                def _(dve):
                    with dve.Fori(0, NT // RING) as i:
                        for r in range(RING):
                            t = RING * i + r
                            n = 3 * t
                            dve.wait_ge(fetched[r], 32 * (i + 1))
                            w = [weight[:, bass.ds(t, 1), m:m + 1].rearrange("p a b -> p (a b)") for m in range(K)]
                            dve.tensor_scalar(mixed[:, r, 0, :], ytok[:, r, 0, :], w[0], None, ALU.mult).then_inc(f_mix, 1)
                            dve.wait_ge(f_mix, n + 1)
                            dve.scalar_tensor_tensor(mixed[:, r, 1, :], ytok[:, r, 1, :], w[1], mixed[:, r, 0, :], ALU.mult, ALU.add)\
                               .then_inc(f_mix, 1)
                            dve.wait_ge(f_mix, n + 2)
                            gb = modrow[:, t // (NT // B), 3, :]
                            dve.tensor_tensor(mixed[:, r, 0, :], mixed[:, r, 1, :], gb, ALU.mult).then_inc(f_mix, 1)
                            dve.wait_ge(f_mix, n + 3)
                            dve.tensor_tensor(x[:, t, :], x[:, t, :], mixed[:, r, 0, :], ALU.add).then_inc(out_ready, 1)

                @block.sync
                def _(sp):
                    ot = out_rows.rearrange("(t p) d -> t p d", p=P)
                    with sp.Fori(0, NT) as t:
                        sp.wait_ge(out_ready, t + 1)
                        sp.dma_start(ot[bass.ds(t, 1)].rearrange("a p d -> (a p) d"), x[:, t, :]).then_inc(out_sent, 16)
                    sp.wait_ge(out_sent, 16 * NT)


_INS = ["L0_attn_x", "L0_attn_Wqkv", "L0_attn_Wout", "L0_ffn_gate_w", "L0_ffn_gate_b", "L0_ffn_W1", "L0_ffn_b1",
        "L0_ffn_W2", "L0_ffn_b2", "L0_c", "L0_wmod"]


def kernel(**inputs):
    import numpy as _np
    import concourse.bacc as _bacc
    from concourse import mybir as _mybir
    from concourse.bass_utils import run_bass_kernel_spmd as _run

    nc = _bacc.Bacc("TRN2", target_bir_lowering=False, num_devices=1)
    arrays, args = {}, []
    for name in _INS:
        a = _np.ascontiguousarray(inputs[name])
        arrays[f"in_{name}"] = a
        args.append(nc.dram_tensor(f"in_{name}", a.shape, _mybir.dt.from_np(a.dtype), kind="ExternalInput").ap())
    out = nc.dram_tensor("out", inputs["L0_attn_x"].shape, _mybir.dt.float32, kind="ExternalOutput").ap()
    build(nc, *args, out)
    r = _run(nc, [arrays], core_ids=[0])
    return r.results[0]["out"]
```

```python
from contextlib import ExitStack

import concourse.bass as bass
from concourse import mybir

ALU = mybir.AluOpType
ACT = mybir.ActivationFunctionType
AX = mybir.AxisListType
F32 = mybir.dt.float32
F16 = mybir.dt.float16
BF16 = mybir.dt.bfloat16
I32 = mybir.dt.int32
U32 = mybir.dt.uint32

W_SCALE = 64.0
SPLIT_PRODUCTS = ((0, 0), (0, 1), (1, 0))
MASKED = -3.0e38

P = 128
D = 256
KD = D // P
H, DH = 16, 64
PAIRS = H // 2
INNER = H * DH
CHUNK = 512
TILES = CHUNK // P
FF, E, K = 1024, 8, 2
FT = FF // P


def group_order(names):
    place, count = {}, [0, 0]
    for n, name in enumerate(names):
        place[name] = (n % 2, count[n % 2])
        count[n % 2] += 1
    return place, count


def build(nc, x_in, wqkv_in, wout_in, gate_w, gate_b, w1_in, b1_in, w2_in, b2_in, c_in, wmod_in, out):
    B, S, _ = x_in.shape
    T = B * S
    NT = T // P
    NC = T // CHUNK
    CPB = S // CHUNK
    CAP = 640
    SLOTS = E * K * CAP
    ST = K * CAP // P
    NPART = ((0, 512), (512, 512), (1024, 256))
    FAR = 100000.0

    x_rows = x_in.rearrange("b s d -> (b s) d")
    out_rows = out.rearrange("b s d -> (b s) d")
    w1v = w1_in.rearrange("e (k p) n -> e p k n", p=P)
    w2v = w2_in.rearrange("e (f p) n -> e p f n", p=P)
    xbuf = nc.dram_tensor("slot_inputs", (SLOTS, 2 * D), F16, kind="Internal").ap()
    ybuf = nc.dram_tensor("slot_outputs", (SLOTS, D), F32, kind="Internal").ap()

    whole = ExitStack()
    with whole:
        def alloc(stack):
            return lambda name, shape, dt: stack.enter_context(nc.sbuf_tensor(name, shape, dt))

        def sem(name):
            return whole.enter_context(nc.semaphore(name))

        keep_sb = alloc(whole)
        x = keep_sb("x", [P, NT, D], F32)
        modrow = keep_sb("modrow", [P, B, 4, D], F32)
        weight = keep_sb("weight", [P, NT, K], F32)
        fetch = keep_sb("fetch", [P, NT, K], U32)
        b1T = keep_sb("b1T", [P, E, FT], F32)
        big = keep_sb("big", [P, KD * 2 * 3 * INNER], F16)
        w32 = big[:, 0:4 * KD * FF].bitcast(F32).rearrange("p (m n) -> p m n", m=2)
        ident16 = keep_sb("ident16", [P, P], F16)

        x0_loaded, x_loaded, small_loaded, zero_sent = (sem(n) for n in ("x0_loaded", "x_loaded", "small_loaded", "zero_sent"))
        stage_loaded = [sem(f"stage_loaded{i}") for i in range(4)]
        consts, b1_loaded, v_scaled = sem("consts"), sem("b1_loaded"), sem("v_scaled")
        w_loaded = sem("w_loaded")
        exp_c, sil, sil_b, mod_mm, mod_row, split_hi, split_lo = (
            sem(n) for n in ("exp_c", "sil", "sil_b", "mod_mm", "mod_row", "split_hi", "split_lo"))

        def stand_ge(eng, *waits):
            ready = [(s, v if isinstance(v, int) else eng.compute_val(v)) for s, v in waits]
            if not all(isinstance(v, int) for _, v in ready):
                eng.wait_ge(consts, 2)
            for s, v in ready:
                eng.wait_ge(s, v)

        def load_expert(sp, dst, e):
            sp.dma_start(dst[:, 0, :].rearrange("p (k n) -> p k n", k=KD),
                         w1v[bass.ds(e, 1)].rearrange("e p k n -> (e p) k n")).then_inc(w_loaded, 16)
            sp.dma_start(dst[:, 1, :].rearrange("p (f n) -> p f n", f=FT),
                         w2v[bass.ds(e, 1)].rearrange("e p f n -> (e p) f n")).then_inc(w_loaded, 16)

        def at_least(eng, s, value):
            if not isinstance(value, int) or value > 0:
                eng.wait_ge(s, value)

        attn_stack = ExitStack()
        with attn_stack:
            sb = alloc(attn_stack)
            ps = lambda name, shape, dt: attn_stack.enter_context(nc.psum_tensor(name, shape, dt))
            wqkv = big[:].rearrange("p (a b c) -> p a b c", a=KD, b=2)
            wout = sb("wout", [P, PAIRS, 2, D], F16)
            hT = sb("hT", [P, 2, KD, 2, CHUNK], F16)
            q = sb("q", [P, PAIRS, 2, CHUNK], F16)
            k = sb("k", [P, PAIRS, 2, P + CHUNK], F16)
            v = sb("v", [P, 1 + TILES, 2, INNER], F16)
            attn = sb("attn", [P, PAIRS, 2, CHUNK], F16)
            prob = sb("prob", [P, 2, TILES, P], F32)
            prob16 = sb("prob16", [P, 2, 2, TILES, P], F16)
            probT = sb("probT", [P, 2, 2 * TILES, P], F16)
            probT_cur = sb("probT_cur", [P, 2, 2 * TILES, P], F16)
            probT_prev = sb("probT_prev", [P, 2, 2 * TILES, P], F16)
            xn = sb("xn", [P, TILES, D], F32)
            h32 = sb("h32", [P, KD, CHUNK], F32)
            h2 = sb("h2", [P, TILES, D], F32)
            packed = sb("packed", [P, TILES, 2 * D], F16)
            h2T = sb("h2T", [P, KD, CHUNK], F32)
            gated = sb("gated", [P, 2, D], F32)
            zero_row = sb("zero_row", [P, 2 * D], F16)
            identf = sb("identf", [P, P], F32)
            onesf = sb("onesf", [P, P], F32)
            above = sb("above", [P, P], F32)
            keys_cur = sb("keys_cur", [P, P], F16)
            ones_row = sb("ones_row", [1, P], BF16)
            no_prev = sb("no_prev", [1, NC, P], BF16)
            cT = sb("cT", [P, KD, B], F32)
            silT = sb("silT", [P, 3, KD * B], F32)
            silB = sb("silB", [P, KD * B, P], F32)
            modcol = sb("modcol", [P, 4, B], F32)
            gwT = sb("gwT", [P, KD, E], F32)
            gbB = sb("gbB", [P, E], F32)
            expert_no = sb("expert_no", [P, E], F32)
            choice_base = sb("choice_base", [P, TILES, K], F32)
            half_neg = sb("half_neg", [P, TILES], F32)
            rowmax = sb("rowmax", [P, 2, TILES], F32)
            negmax = sb("negmax", [P, 2, TILES], F32)
            rowsum = sb("rowsum", [P, 2, TILES], F32)
            rinv = sb("rinv", [P, 2, TILES], F32)
            stats = [sb(f"stats{i}", [P, TILES, 6], F32) for i in range(2)]
            meanvar = [sb(f"meanvar{i}", [P, TILES, 2], F32) for i in range(2)]
            rstd = [sb(f"rstd{i}", [P, 2, TILES], F32) for i in range(2)]
            logit = sb("logit", [P, TILES, E], F32)
            lmax = sb("lmax", [P, TILES], F32)
            lsum = sb("lsum", [P, 2, TILES], F32)
            top = sb("top", [P, TILES, 8], F32)
            topi = sb("topi", [P, TILES, 8], U32)
            topf = sb("topf", [P, TILES, K], F32)
            onehot = sb("onehot", [P, TILES, K, E], F32)
            cum = sb("cum", [P, TILES, K, E], F32)
            carry = sb("carry", [P, K, E], F32)
            pos = sb("pos", [P, TILES, K], F32)
            posc = sb("posc", [P, TILES, K], F32)
            slot = sb("slot", [P, TILES, K], F32)
            drop = sb("drop", [P, TILES, K], F32)
            send = sb("send", [P, TILES, K], U32)

            score = [ps(f"score{i}", [P, TILES, 2 * P], F32) for i in range(2)]
            pt = ps("pt", [P, 2 * TILES, P], F16)
            pv = ps("pv", [P, CHUNK], F32)
            gen = [ps(f"gen{i}", [P, 512], F32) for i in range(2)]

            stage = [t[:].rearrange("p a b c -> p (a b c)").bitcast(F32)[:, i * 2048:(i + 1) * 2048]
                     for t in (q, attn) for i in range(2)]
            wmod = k[:].rearrange("p a b c -> p (a b c)").bitcast(F32)[:, 0:KD * 6 * D].rearrange("p (k n) -> p k n", k=KD)
            stage_src = [wqkv_in.rearrange("(k p) n -> p k n", p=P)[:, :, i * INNER:(i + 1) * INNER] for i in range(3)]
            stage_src.append(wout_in.rearrange("(j p) n -> p j n", p=P))
            stage_view = [stage[i].rearrange("p (k n) -> p k n", k=KD if i < 3 else PAIRS) for i in range(4)]

            def stage_dst(i, part):
                return wqkv[:, :, part, i * INNER:(i + 1) * INNER] if i < 3 else wout[:, :, part, :]

            def split_low(eng, stages):
                for i in stages:
                    eng.wait_ge(split_hi, i + 1)
                    eng.scalar_tensor_tensor(stage_dst(i, 1), stage_view[i], W_SCALE, stage_dst(i, 0),
                                             ALU.mult, ALU.subtract).then_inc(split_lo, 1)

            with nc.Block() as block:
                @block.sync
                def _(sp):
                    for b in range(B):
                        sp.dma_start(cT[:, :, b], c_in[b].rearrange("(k p) -> p k", p=P), allow_slow_non_contiguous=True)\
                          .then_inc(small_loaded, 16)
                    sp.dma_start(wmod, wmod_in.rearrange("(k p) n -> p k n", p=P)).then_inc(small_loaded, 16)
                    for kd in range(KD):
                        sp.dma_start(gwT[:, kd, :], gate_w[:, kd * P:(kd + 1) * P].rearrange("e p -> p e"),
                                     allow_slow_non_contiguous=True).then_inc(small_loaded, 16)
                    sp.dma_start(gbB[:], gate_b.partition_broadcast(P)).then_inc(small_loaded, 16)
                    xt = x_rows.rearrange("(t p) d -> p t d", p=P)
                    for i in range(4):
                        sp.dma_start(stage_view[i], stage_src[i]).then_inc(stage_loaded[i], 16)
                        if i == 1:
                            sp.dma_start(x[:, 0:2 * TILES, :], xt[:, 0:2 * TILES, :]).then_inc(x0_loaded, 16)
                    sp.dma_start(x[:, 2 * TILES:, :], xt[:, 2 * TILES:, :]).then_inc(x_loaded, 16)
                    sp.dma_start(b1T[:].rearrange("p e f -> p (e f)"), b1_in.rearrange("e (f p) -> p (e f)", p=P),
                                 allow_slow_non_contiguous=True).then_inc(b1_loaded, 16)

                @block.gpsimd
                def _(pool):
                    pool.memset(onesf[:], 1.0)
                    pool.memset(identf[:], 0.0)
                    pool.memset(keys_cur[:], 1.0).then_inc(consts, 1)
                    pool.wait_ge(consts, 1)
                    pool.affine_select(out=identf[:], in_=identf[:], pattern=[[-1, P]], compare_op=ALU.not_equal,
                                       fill=1.0, base=0, channel_multiplier=1)
                    pool.affine_select(out=above[:], in_=onesf[:], pattern=[[1, P]], compare_op=ALU.is_gt,
                                       fill=0.0, base=0, channel_multiplier=-1)
                    pool.affine_select(out=keys_cur[:], in_=keys_cur[:], pattern=[[1, P]], compare_op=ALU.is_ge,
                                       fill=0.0, base=0, channel_multiplier=-1)
                    pool.iota(expert_no[:], pattern=[[1, E]], base=0, channel_multiplier=0,
                              allow_small_or_imprecise_dtypes=True).then_inc(consts, 1)
                    pool.wait_ge(split_hi, 3)
                    pool.tensor_tensor(stage_dst(2, 1), stage_view[2], stage_dst(2, 0), ALU.subtract).then_inc(split_lo, 1)

                @block.vector
                def _(dve):
                    dve.memset(zero_row[:], 0.0)
                    dve.memset(ones_row[:], 1.0)
                    for c in range(NC):
                        dve.memset(no_prev[:, c, :], MASKED if c % CPB == 0 else 0.0)
                    dve.memset(carry[:], 0.0)
                    for c in range(K):
                        dve.memset(choice_base[:, :, c:c + 1], float(c * CAP))
                    dve.memset(half_neg[:], -0.5)
                    dve.wait_ge(consts, 2)
                    dve.tensor_copy(ident16[:], identf[:])
                    dve.wait_ge(exp_c, 1)
                    dve.tensor_scalar(silT[:, 1, :], silT[:, 0, :], 1.0, None, ALU.add).then_inc(sil, 1)
                    dve.wait_ge(sil, 1)
                    dve.reciprocal(silT[:, 2, :], silT[:, 1, :]).then_inc(sil, 1)
                    dve.wait_ge(sil, 2)
                    dve.tensor_tensor(silT[:, 0, :], silT[:, 2, :], cT[:].rearrange("p k b -> p (k b)"), ALU.mult).then_inc(sil, 1)
                    dve.wait_ge(sil, 3)
                    dve.tensor_copy(silB[:], silT[:, 0, :].unsqueeze(2).to_broadcast([P, KD * B, P])).then_inc(sil_b, 1)
                    dve.wait_ge(mod_mm, 1)
                    mc = gen[0][:, 0:4 * B].rearrange("p (j b) -> p j b", b=B)
                    dve.tensor_copy(modcol[:, 0:2, :], mc[:, 0:2, :])
                    dve.tensor_scalar(modcol[:, 2:4, :], mc[:, 2:4, :], 1.0, None, ALU.add)
                    split_low(dve, range(2))
                    for b in range(B):
                        dve.wait_ge(mod_mm, 2 + b)
                        ga, gb = score[b][:, 0:1, :], score[b][:, 3:4, :]
                        dve.tensor_copy(modrow[:, b, 1:2, :], score[b][:, 1:2, :])
                        dve.tensor_scalar(modrow[:, b, 2:3, :], score[b][:, 2:3, :], 1.0, None, ALU.add)
                        for n, (gate, row) in enumerate(((ga, 0), (gb, 3))):
                            dve.tensor_scalar(gated[:, 0:1, :], gate, 0.0, 2.0, ALU.is_ge, ALU.mult).then_inc(mod_row, 1)
                            dve.tensor_scalar(h2[:, 0:1, :], gate, -1.0, None, ALU.mult).then_inc(mod_row, 1)
                            dve.wait_ge(mod_row, 8 * b + 4 * n + 2)
                            dve.scalar_tensor_tensor(gated[:, 1:2, :], gate, 0.25, h2[:, 0:1, :], ALU.max, ALU.max).then_inc(mod_row, 1)
                            dve.wait_ge(mod_row, 8 * b + 4 * n + 3)
                            dve.scalar_tensor_tensor(modrow[:, b, row:row + 1, :], gated[:, 0:1, :], -1.0,
                                                     gated[:, 1:2, :], ALU.add, ALU.mult).then_inc(mod_row, 1)
                            dve.wait_ge(mod_row, 8 * b + 4 * n + 4)
                    split_low(dve, range(3, 4))

                @block.scalar
                def _(act):
                    act.wait_ge(small_loaded, 16 * (B + KD + 2))
                    act.activation(silT[:, 0, :], cT[:].rearrange("p k b -> p (k b)"), ACT.Exp, scale=-1.0).then_inc(exp_c, 1)
                    for i in range(4):
                        act.wait_ge(stage_loaded[i], 16)
                        if i == 2:
                            act.activation(stage_view[i], stage_view[i], ACT.Copy, scale=W_SCALE).then_inc(v_scaled, 1)
                            act.wait_ge(v_scaled, 1)
                        act.activation(stage_dst(i, 0), stage_view[i], ACT.Copy, scale=1.0 if i == 2 else W_SCALE).then_inc(split_hi, 1)

                @block.tensor
                def _(pe):
                    pe.wait_ge(sil, 3)
                    pe.wait_ge(small_loaded, 16 * (B + KD + 2))
                    silm = silT[:, 0, :].rearrange("p (k b) -> p k b", b=B)
                    for j in range(4):
                        for kd in range(KD):
                            mm = pe.matmul(gen[0][:, j * B:(j + 1) * B], wmod[:, kd, j * P:(j + 1) * P], silm[:, kd, :],
                                           start=(kd == 0), stop=(kd == KD - 1))
                    mm.then_inc(mod_mm, 1)
                    pe.wait_ge(sil_b, 1)
                    for b in range(B):
                        flat = score[b][:].rearrange("p a b -> p (a b)")
                        for half in range(2):
                            for kd in range(KD):
                                mm = pe.matmul(flat[:, half * 512:(half + 1) * 512], silB[:, kd * B + b, :],
                                               wmod[:, kd, 2 * D + half * 512:2 * D + (half + 1) * 512],
                                               start=(kd == 0), stop=(kd == KD - 1))
                        mm.then_inc(mod_mm, 1)

            ln_groups = [("lnT", 0), ("lnT", 1)]
            route_groups = [("h2T", 0), ("h2T", 1), ("logits",), ("counts",)]
            out_groups = [("out", 0), ("out", 1)]
            LAG = 4
            STEPS = range(LAG, H + LAG)
            v_half = lambda half: [("v", half, s) for s in range(TILES)]
            qk_pair = lambda j: [("q", j), ("k", j)]
            HEAD_QK = sum([qk_pair(j) for j in range(PAIRS)], [])
            HEAD_V = v_half(0) + v_half(1)
            HEAD = [("ln0", 0), ("ln0", 1)] + HEAD_QK + ln_groups + HEAD_V

            def projections_at(i):
                return [("qk"[i % 2], (i - LAG) // 2)] + ([("v", 0, i - 14)] if 14 <= i < 14 + TILES else [])

            def chunk_groups(first, last):
                names = []
                for i in STEPS:
                    if not first:
                        names += {9: route_groups[0:2], 10: route_groups[2:3], 14: route_groups[3:4]}.get(i, [])
                    if i == 11 and not last:
                        names += ln_groups
                    if not last:
                        names += projections_at(i)
                return names + ([] if last else v_half(1)) + out_groups

            kinds = [HEAD, chunk_groups(True, False), chunk_groups(False, False), chunk_groups(False, True), route_groups]
            orders = [group_order(names) for names in kinds]

            def group(c, name):
                kind = 0 if isinstance(c, int) and c == -1 else 1 if isinstance(c, int) and c == 0 else \
                    4 if isinstance(c, int) and c == NC else 3 if isinstance(c, int) and c == NC - 1 else 2
                bank, before = orders[kind][0][name]
                counts = [o[1][bank] for o in orders]
                if kind >= 1:
                    before = before + counts[0]
                if kind == 2:
                    before = before + counts[1] + (c - 1) * counts[2]
                if kind >= 3:
                    before = before + counts[1] + (NC - 2) * counts[2]
                if kind == 4:
                    before = before + counts[3]
                return bank, before

            gen_full = [sem(f"gen_full{i}") for i in range(2)]
            gen_free = [sem(f"gen_free{i}") for i in range(2)]
            (scores_done, merged, maxed, neg_ready, exp_done, rinv_ready, norm_ready, hi_ready, lo_ready, pt_done,
             probT_ready, cur_ready, prev_ready, pv_done, attn_hi, attn_lo, proj_hi, k_halo, v_halo) = (sem(n) for n in (
                 "scores_done", "merged", "maxed", "neg_ready", "exp_done", "rinv_ready", "norm_ready", "hi_ready",
                 "lo_ready", "pt_done", "probT_ready", "cur_ready", "prev_ready", "pv_done", "attn_hi", "attn_lo",
                 "proj_hi", "k_halo", "v_halo"))
            ln_stat, ln_mv, ln_var, ln_rstd, ln_xn, ln_h32, ln_hi, ln_lo = (
                sem(n) for n in ("ln_stat", "ln_mv", "ln_var", "ln_rstd", "ln_xn", "ln_h32", "ln_hi", "ln_lo"))
            x2_ready, r_stat, r_mv, r_var, r_rstd, r_xn, r_scaled, r_h2, r_pack_hi, r_pack = (
                sem(n) for n in ("x2_ready", "r_stat", "r_mv", "r_var", "r_rstd", "r_xn", "r_scaled",
                                 "r_h2", "r_pack_hi", "r_pack"))
            r_soft, r_exp, r_count, r_send, sent = (sem(n) for n in ("r_soft", "r_exp", "r_count", "r_send", "sent"))
            PROJ = 2 * PAIRS + 2 * TILES

            def proj_no(c, name):
                order = HEAD_QK + HEAD_V if isinstance(c, int) and c == 0 else [n for n in chunk_groups(False, False) if n[0] in "qkv"]
                return c * PROJ + order.index(name) + 1

            def batch(c):
                return c // CPB

            def rows_seen(eng, c):
                if isinstance(c, int) and c == NC:
                    eng.wait_ge(sent, 16 * TILES * K * (NC - 1))
                else:
                    eng.wait_ge(prev_ready, H * c + 2)

            with nc.Block() as block:
                @block.sync
                def _(sp):
                    with sp.Fori(0, SLOTS // P) as i:
                        sp.dma_start(xbuf[bass.ts(i, P), :], zero_row[:]).then_inc(zero_sent, 16)
                    sp.wait_ge(zero_sent, 16 * (SLOTS // P))
                    sp.wait_ge(x2_ready, 2 * (NC - 1))
                    load_expert(sp, w32, 0)

                @block.tensor
                def _(pe):
                    def claim(c, name):
                        bank, before = group(c, name)
                        at_least(pe, gen_free[bank], before)
                        return gen[bank], gen_full[bank]

                    def ln_transposes(c, cn, label):
                        pe.wait_ge(ln_xn, cn + 1)
                        for kd in range(KD):
                            dst, full = claim(c, (label, kd))
                            for s in range(TILES):
                                mm = pe.transpose(dst[:, s * P:(s + 1) * P], xn[:, s, kd * P:(kd + 1) * P], identf[:])
                            mm.then_inc(full, 1)

                    def project_qk(c, name):
                        cn = c + 1
                        j = name[1]
                        col = j * P + (INNER if name[0] == "k" else 0)
                        if name == ("q", 0):
                            pe.wait_ge(ln_lo, cn + 1)
                        dst, full = claim(c, name)
                        n = 0
                        for a, b in SPLIT_PRODUCTS:
                            for kd in range(KD):
                                mm = pe.matmul(dst[:], wqkv[:, kd, a, col:col + P], hT[:, cn % 2, kd, b, :],
                                               start=(n == 0), stop=(n == 5))
                                n += 1
                        mm.then_inc(full, 1)

                    def project_v(c, half, tiles=range(TILES)):
                        cn = c + 1
                        for s in tiles:
                            dst, full = claim(c, ("v", half, s))
                            n = 0
                            for a, b in SPLIT_PRODUCTS:
                                for kd in range(KD):
                                    mm = pe.matmul(dst[:], hT[:, cn % 2, kd, a, s * P:(s + 1) * P],
                                                   wqkv[:, kd, b, 2 * INNER + half * 512:2 * INNER + (half + 1) * 512],
                                                   start=(n == 0), stop=(n == 5))
                                    n += 1
                            mm.then_inc(full, 1)

                    def scores(c, h):
                        if h >= H:
                            c, h = c + 1, h - H
                        u, j, r = H * c + h, h // 2, DH * (h % 2)
                        dst = score[h % 2]
                        if h % 2 == 0:
                            if isinstance(c, int) and c == 0:
                                for name in qk_pair(j):
                                    bank, before = group(-1, name)
                                    pe.wait_ge(gen_free[bank], before + 1)
                            else:
                                pe.wait_ge(norm_ready, H * (c - 1) + h + 6)
                        at_least(pe, exp_done, u - 1)
                        for b in range(TILES):
                            for n, (a, m) in enumerate(SPLIT_PRODUCTS):
                                mm = pe.matmul(dst[:, b, :], q[r:r + DH, j, a, b * P:(b + 1) * P],
                                               k[r:r + DH, j, m, b * P:(b + 2) * P], start=(n == 0),
                                               stop=(n == 2), skip_group_check=(b == 0))
                            if b == 0:
                                mm = pe.matmul(dst[:, 0, 0:P], ones_row[:], no_prev[:, c, :], start=False, stop=True,
                                               skip_group_check=True)
                        mm.then_inc(scores_done, 1)

                    def transposes(c, h):
                        u = H * c + h
                        pe.wait_ge(lo_ready, u + 1)
                        at_least(pe, probT_ready, u)
                        for part in range(2):
                            for b in range(TILES):
                                mm = pe.transpose(pt[:, part * TILES + b, :], prob16[:, h % 2, part, b, :], ident16[:])
                        mm.then_inc(pt_done, 1)

                    def weighted_values(c, h):
                        u, j, r = H * c + h, h // 2, DH * (h % 2)
                        pe.wait_ge(prev_ready, u + 1)
                        pe.wait_ge(cur_ready, u + 1)
                        if h % 2 == 0:
                            at_least(pe, attn_lo, PAIRS * c + j)
                        if h % (H // 2) == 0:
                            half = h // (H // 2)
                            if isinstance(c, int) and c == 0:
                                for s in range(TILES):
                                    bank, before = group(-1, ("v", half, s))
                                    pe.wait_ge(gen_free[bank], before + 1)
                            elif half == 0:
                                pe.wait_ge(attn_lo, PAIRS * c)
                            else:
                                pe.wait_ge(x2_ready, 2 * c)
                        for b in range(TILES):
                            n = 0
                            for a, m in SPLIT_PRODUCTS:
                                for blk, pr in ((b + 1, probT_cur), (b, probT_prev)):
                                    mm = pe.matmul(pv[r:r + DH, b * P:(b + 1) * P], v[:, blk, a, h * DH:(h + 1) * DH],
                                                   pr[:, h % 2, m * TILES + b, :], start=(n == 0), stop=(n == 5))
                                    n += 1
                        mm.then_inc(pv_done, 1)

                    def project_out(c):
                        pe.wait_ge(attn_lo, PAIRS * (c + 1))
                        for p in range(2):
                            dst, full = claim(c, ("out", p))
                            for s in range(2):
                                t = 2 * p + s
                                n = 0
                                for j in range(PAIRS):
                                    for a, b in SPLIT_PRODUCTS:
                                        mm = pe.matmul(dst[:, s * D:(s + 1) * D], attn[:, j, a, t * P:(t + 1) * P],
                                                       wout[:, j, b, :], start=(n == 0), stop=(n == 3 * PAIRS - 1))
                                        n += 1
                            mm.then_inc(full, 1)

                    def route_transposes(c):
                        pe.wait_ge(r_h2, c)
                        for kd in range(KD):
                            dst, full = claim(c, ("h2T", kd))
                            for s in range(TILES):
                                mm = pe.transpose(dst[:, s * P:(s + 1) * P], h2[:, s, kd * P:(kd + 1) * P], identf[:])
                            mm.then_inc(full, 1)

                    def route_logits(c):
                        for kd in range(KD):
                            bank, before = group(c, ("h2T", kd))
                            pe.wait_ge(gen_free[bank], before + 1)
                        dst, full = claim(c, ("logits",))
                        for s in range(TILES):
                            for kd in range(KD):
                                mm = pe.matmul(dst[:, s * E:(s + 1) * E], h2T[:, kd, s * P:(s + 1) * P], gwT[:, kd, :],
                                               start=(kd == 0), stop=(kd == KD - 1))
                        mm.then_inc(full, 1)

                    def route_counts(c):
                        pe.wait_ge(r_soft, 11 * c)
                        dst, full = claim(c, ("counts",))
                        KE = K * E
                        hot = onehot[:].rearrange("p s c e -> p s (c e)")
                        for s in range(TILES + 1):
                            last = min(s, TILES - 1)
                            for m in range(last + 1):
                                mm = pe.matmul(dst[:, s * KE:(s + 1) * KE], above[:] if m == s else onesf[:], hot[:, m, :],
                                               start=(m == 0), stop=(m == last))
                        mm.then_inc(full, 1)

                    def chunk(c, first, last):
                        for i in STEPS:
                            if i < H or not last:
                                scores(c, i)
                            weighted_values(c, i - 4)
                            if i - 2 < H or not last:
                                transposes(c, i - 2)
                            if not first and i == 9:
                                route_transposes(c)
                            if not first and i == 10:
                                route_logits(c)
                            if not first and i == 14:
                                route_counts(c)
                            if i == 11 and not last:
                                ln_transposes(c, c + 2, "lnT")
                            for name in [] if last else projections_at(i):
                                if name[0] == "v":
                                    project_v(c, 0, [name[2]])
                                else:
                                    project_qk(c, name)
                        if not last:
                            project_v(c, 1)
                        project_out(c)

                    ln_transposes(-1, 0, "ln0")
                    for j in range(PAIRS):
                        project_qk(-1, ("q", j))
                        project_qk(-1, ("k", j))
                    ln_transposes(-1, 1, "lnT")
                    for i in range(LAG):
                        scores(0, i)
                        if i >= 2:
                            transposes(0, i - 2)
                        project_v(-1, i // 2, range(2 * (i % 2), 2 * (i % 2) + 2))
                    chunk(0, True, False)
                    with pe.Fori(1, NC - 1) as c:
                        chunk(c, False, False)
                    chunk(NC - 1, False, True)
                    route_transposes(NC)
                    route_logits(NC)
                    route_counts(NC)

                @block.scalar
                def _(act):
                    def ln_modulate(c, cn, label):
                        for kd in range(KD):
                            bank, before = group(c, (label, kd))
                            stand_ge(act, (gen_full[bank], before + 1))
                            at_least(act, ln_lo, cn)
                            b = batch(clip(cn))
                            act.activation(h32[:, kd, :], gen[bank][:], ACT.Identity,
                                           bias=modcol[:, kd, bass.ds(b, 1)], scale=modcol[:, 2 + kd, bass.ds(b, 1)])\
                               .then_inc(gen_free[bank], 1)

                    def high(c, name):
                        cn = c + 1
                        bank, before = group(c, name)
                        act.wait_ge(gen_full[bank], before + 1)
                        if name[0] == "q":
                            at_least(act, scores_done, H * c + 2 * name[1] + 2)
                            dst = q[:, name[1], 0, :]
                        elif name[0] == "k":
                            act.wait_ge(k_halo, PAIRS * cn + name[1] + 1)
                            dst = k[:, name[1], 0, P:]
                        else:
                            act.wait_ge(v_halo, 2 * cn + name[1] + 1)
                            dst = v[:, 1 + name[2], 0, name[1] * 512:(name[1] + 1) * 512]
                        act.activation(dst, gen[bank][:], ACT.Copy, scale=1 / W_SCALE).then_inc(proj_hi, 1)

                    def exponentials(c, h):
                        u = H * c + h
                        act.wait_ge(neg_ready, u + 1)
                        at_least(act, lo_ready, u - 1)
                        for b in range(TILES):
                            mm = act.activation(prob[:, h % 2, b, :], score[h % 2][:, b, P:], ACT.Exp, scale=DH ** -0.5,
                                                bias=negmax[:, h % 2, b:b + 1], accum_out=rowsum[:, h % 2, b:b + 1])
                        mm.then_inc(exp_done, 1)

                    def prob_high(c, h):
                        u = H * c + h
                        act.wait_ge(norm_ready, u + 1)
                        at_least(act, pt_done, u - 1)
                        act.activation(prob16[:, h % 2, 0], prob[:, h % 2], ACT.Copy).then_inc(hi_ready, 1)

                    def copy_probT(c, h):
                        u = H * c + h
                        act.wait_ge(pt_done, u + 1)
                        at_least(act, prev_ready, u - 1)
                        at_least(act, cur_ready, u - 1)
                        act.activation(probT[:, h % 2], pt[:], ACT.Copy).then_inc(probT_ready, 1)

                    def attn_high(c, j):
                        act.wait_ge(pv_done, H * c + 2 * j + 2)
                        if j == 0:
                            at_least(act, x2_ready, 2 * c)
                        act.activation(attn[:, j, 0, :], pv[:], ACT.Copy).then_inc(attn_hi, 1)

                    def route_pack(c):
                        act.wait_ge(r_h2, c)
                        rows_seen(act, c)
                        act.activation(packed[:, :, 0:D], h2[:], ACT.Copy).then_inc(r_pack_hi, 1)

                    def route_h2T(c):
                        for kd in range(KD):
                            bank, before = group(c, ("h2T", kd))
                            act.wait_ge(gen_full[bank], before + 1)
                            act.activation(h2T[:, kd, :], gen[bank][:], ACT.Copy).then_inc(gen_free[bank], 1)

                    def route_exp(c):
                        act.wait_ge(r_soft, 11 * (c - 1) + 3)
                        act.activation(logit[:], logit[:], ACT.Exp).then_inc(r_exp, 1)

                    def chunk(c, first, last):
                        for i in STEPS:
                            if i <= H or not last:
                                exponentials(c, i - 1)
                            if i % 2 == 1:
                                attn_high(c, (i - 5) // 2)
                            if i - 2 < H or not last:
                                copy_probT(c, i - 2)
                            if i <= H or not last:
                                prob_high(c, i - 1)
                            if not first and i == 9:
                                route_h2T(c)
                            if i == 11 and not last:
                                ln_modulate(c, c + 2, "lnT")
                            for name in [] if last else projections_at(i):
                                high(c, name)
                            if not first and i == 10:
                                route_pack(c)
                            if not first and i == 11:
                                route_exp(c)
                        if not last:
                            for s in range(TILES):
                                high(c, ("v", 1, s))

                    def clip(cn):
                        return cn % NC

                    ln_modulate(-1, 0, "ln0")
                    for name in HEAD_QK:
                        high(-1, name)
                    ln_modulate(-1, 1, "lnT")
                    for i in range(LAG):
                        if i >= 1:
                            exponentials(0, i - 1)
                        if i >= 2:
                            copy_probT(0, i - 2)
                        if i >= 1:
                            prob_high(0, i - 1)
                        for name in HEAD_V[2 * i:2 * i + 2]:
                            high(-1, name)
                    chunk(0, True, False)
                    with act.Fori(1, NC - 1) as c:
                        chunk(c, False, False)
                    chunk(NC - 1, False, True)
                    route_h2T(NC)
                    route_pack(NC)
                    route_exp(NC)

                @block.vector
                def _(dve):
                    def clip(cn):
                        return cn % NC

                    def norm_stats(tile0, st, mv, stat_sem, mv_sem, n):
                        for s in range(TILES):
                            op = dve.bn_stats(st[:, s, :], x[:, tile0 + s, :])
                        op.then_inc(stat_sem, 1)
                        stand_ge(dve, (stat_sem, n))
                        for s in range(TILES):
                            op = dve.bn_aggr(mv[:, s, :], st[:, s, :])
                        op.then_inc(mv_sem, 1)

                    def norm_rows(tile0, dst, mv, rs, rs_sem, xn_sem, n):
                        dve.wait_ge(rs_sem, n)
                        for s in range(TILES):
                            op = dve.tensor_scalar(dst[:, s, :], x[:, tile0 + s, :], mv[:, s, 0:1], rs[:, 1, s:s + 1],
                                                   ALU.subtract, ALU.mult)
                        op.then_inc(xn_sem, 1)

                    def ln_first(cn):
                        norm_stats(clip(cn) * TILES, stats[0], meanvar[0], ln_stat, ln_mv, cn + 1)

                    def ln_second(cn):
                        norm_rows(clip(cn) * TILES, xn, meanvar[0], rstd[0], ln_rstd, ln_xn, cn + 1)

                    def ln_high(c, cn, label):
                        for kd in range(KD):
                            bank, before = group(c, (label, kd))
                            dve.wait_ge(gen_free[bank], before + 1)
                        dve.tensor_copy(hT[:, cn % 2, :, 0, :], h32[:]).then_inc(ln_hi, 1)

                    def low(c, name):
                        cn = c + 1
                        bank, _ = group(c, name)
                        dve.wait_ge(proj_hi, proj_no(cn, name))
                        if name[0] == "q":
                            hi, lo = q[:, name[1], 0, :], q[:, name[1], 1, :]
                        elif name[0] == "k":
                            hi, lo = k[:, name[1], 0, P:], k[:, name[1], 1, P:]
                        else:
                            hi, lo = (v[:, 1 + name[2], m, name[1] * 512:(name[1] + 1) * 512] for m in range(2))
                        dve.scalar_tensor_tensor(lo, gen[bank][:], 1 / W_SCALE, hi, ALU.mult, ALU.subtract)\
                           .then_inc(gen_free[bank], 1)

                    def keep_k(c, j):
                        dve.wait_ge(scores_done, H * c + 2 * j + 2)
                        dve.tensor_copy(k[:, j, :, 0:P], k[:, j, :, CHUNK:]).then_inc(k_halo, 1)

                    def keep_v(c, half):
                        dve.wait_ge(pv_done, H * c + (H // 2) * (half + 1))
                        cols = slice(half * 512, (half + 1) * 512)
                        dve.tensor_copy(v[:, 0, :, cols], v[:, TILES, :, cols]).then_inc(v_halo, 1)

                    def mask_own(c, h):
                        u = H * c + h
                        dve.wait_ge(probT_ready, u + 1)
                        at_least(dve, pv_done, u - 1)
                        dve.tensor_tensor(probT_cur[:, h % 2], probT[:, h % 2],
                                          keys_cur[:].unsqueeze(1).to_broadcast([P, 2 * TILES, P]), ALU.mult).then_inc(cur_ready, 1)

                    def merge(c, h):
                        sc = score[h % 2]
                        stand_ge(dve, (scores_done, H * c + h + 1))
                        dve.copy_predicated(sc[:, :, P:], above[:].bitcast(I32).unsqueeze(1).to_broadcast([P, TILES, P]), sc[:, :, 0:P])\
                           .then_inc(merged, 1)

                    def row_max(c, h):
                        dve.wait_ge(merged, H * c + h + 1)
                        dve.reduce_max(rowmax[:, h % 2, :], score[h % 2][:, :, P:], AX.X).then_inc(maxed, 1)

                    def negate_max(c, h):
                        dve.wait_ge(maxed, H * c + h + 1)
                        dve.tensor_scalar(negmax[:, h % 2, :], rowmax[:, h % 2, :], -(DH ** -0.5), None, ALU.mult).then_inc(neg_ready, 1)

                    def invert_sum(c, h):
                        dve.wait_ge(exp_done, H * c + h + 1)
                        dve.reciprocal(rinv[:, h % 2, :], rowsum[:, h % 2, :]).then_inc(rinv_ready, 1)

                    def normalise(c, h):
                        dve.wait_ge(rinv_ready, H * c + h + 1)
                        dve.tensor_tensor(prob[:, h % 2], prob[:, h % 2], rinv[:, h % 2, :].unsqueeze(2).to_broadcast([P, TILES, P]), ALU.mult)\
                           .then_inc(norm_ready, 1)

                    def softmax_step(c, i, last):
                        new, old = i < H or not last, i >= 1 and (i <= H or not last)
                        for stage, unit, there in ((merge, i, new), (invert_sum, i - 1, old), (row_max, i, new),
                                                   (normalise, i - 1, old), (negate_max, i, new)):
                            if there:
                                stage(c, unit)

                    def attn_low(c, j):
                        dve.wait_ge(attn_hi, PAIRS * c + j + 1)
                        dve.tensor_tensor(attn[:, j, 1, :], pv[:], attn[:, j, 0, :], ALU.subtract).then_inc(attn_lo, 1)

                    def add_attention(c, p):
                        bank, before = group(c, ("out", p))
                        at_least(dve, x2_ready, 2 * c + p)
                        dve.wait_ge(gen_full[bank], before + 1)
                        ga = modrow[:, batch(c), 0:1, :].to_broadcast([P, 2, D])
                        dve.scalar_tensor_tensor(gated[:], gen[bank][:].rearrange("p (s d) -> p s d", s=2), 1 / W_SCALE,
                                                 ga, ALU.mult, ALU.mult).then_inc(gen_free[bank], 1)
                        dve.wait_ge(gen_free[bank], before + 1)
                        tiles = x[:, bass.ds(c * TILES + 2 * p, 2), :]
                        dve.tensor_tensor(tiles, tiles, gated[:], ALU.add).then_inc(x2_ready, 1)

                    def route_low(c):
                        dve.wait_ge(r_pack_hi, c)
                        dve.tensor_tensor(packed[:, :, D:], h2[:], packed[:, :, 0:D], ALU.subtract).then_inc(r_pack, 1)

                    def route_softmax(c):
                        bank, before = group(c, ("logits",))
                        n = 11 * (c - 1)
                        dve.wait_ge(gen_full[bank], before + 1)
                        dve.tensor_tensor(logit[:], gen[bank][:, 0:TILES * E].rearrange("p (s e) -> p s e", e=E),
                                          gbB[:].unsqueeze(1).to_broadcast([P, TILES, E]), ALU.add).then_inc(gen_free[bank], 1)
                        dve.wait_ge(gen_free[bank], before + 1)
                        dve.reduce_max(lmax[:], logit[:], AX.X).then_inc(r_soft, 2)
                        dve.wait_ge(r_soft, n + 2)
                        dve.tensor_tensor(logit[:], logit[:], lmax[:].unsqueeze(2).to_broadcast([P, TILES, E]), ALU.subtract).then_inc(r_soft, 1)

                    def route_top(c):
                        n = 11 * (c - 1)
                        dve.wait_ge(r_exp, c)
                        dve.reduce_sum(lsum[:, 0, :], logit[:], AX.X).then_inc(r_soft, 1)
                        dve.wait_ge(r_soft, n + 4)
                        dve.reciprocal(lsum[:, 1, :], lsum[:, 0, :]).then_inc(r_soft, 1)
                        dve.wait_ge(r_soft, n + 5)
                        dve.tensor_tensor(logit[:], logit[:], lsum[:, 1, :].unsqueeze(2).to_broadcast([P, TILES, E]), ALU.mult).then_inc(r_soft, 1)
                        stand_ge(dve, (r_soft, n + 6))
                        for s in range(TILES):
                            op = dve.max(top[:, s, :], logit[:, s, :])
                        op.then_inc(r_soft, 1)
                        stand_ge(dve, (r_soft, n + 7))
                        for s in range(TILES):
                            op = dve.max_index(topi[:, s, :], top[:, s, :], logit[:, s, :])
                        op.then_inc(r_soft, 1)
                        dve.wait_ge(r_soft, n + 8)
                        dve.tensor_copy(topf[:], topi[:, :, 0:K]).then_inc(r_soft, 1)
                        dve.wait_ge(r_soft, n + 9)
                        for m in range(K):
                            dve.tensor_tensor(onehot[:, :, m, :], expert_no[:].unsqueeze(1).to_broadcast([P, TILES, E]),
                                              topf[:, :, m:m + 1].to_broadcast([P, TILES, E]), ALU.is_equal).then_inc(r_soft, 1)

                    def route_slots(c):
                        g = c - 1
                        n = 8 * (c - 1)
                        KE = K * E
                        bank, before = group(c, ("counts",))
                        dve.wait_ge(gen_full[bank], before + 1)
                        flat = cum[:].rearrange("p s c e -> p s (c e)")
                        cflat = carry[:].rearrange("p c e -> p (c e)")
                        dve.tensor_tensor(flat, gen[bank][:, 0:TILES * KE].rearrange("p (s n) -> p s n", n=KE),
                                          cflat.unsqueeze(1).to_broadcast([P, TILES, KE]), ALU.add).then_inc(r_count, 1)
                        dve.wait_ge(r_count, n + 1)
                        dve.tensor_tensor(cflat, cflat, gen[bank][:, TILES * KE:(TILES + 1) * KE], ALU.add).then_inc(gen_free[bank], 1)
                        dve.tensor_tensor(cum[:], cum[:], onehot[:], ALU.mult).then_inc(r_count, 1)
                        dve.wait_ge(r_count, n + 2)
                        dve.reduce_sum(pos[:], cum[:], AX.X).then_inc(r_count, 1)
                        dve.wait_ge(r_count, n + 3)
                        tile0 = g * TILES
                        dve.scalar_tensor_tensor(weight[:, bass.ds(tile0, TILES), :], pos[:], float(CAP), top[:, :, 0:K], ALU.is_lt, ALU.mult)
                        dve.tensor_scalar(drop[:], pos[:], float(CAP), FAR, ALU.is_ge, ALU.mult)
                        dve.tensor_tensor(posc[:], pos[:], choice_base[:], ALU.add).then_inc(r_count, 1)
                        dve.wait_ge(r_count, n + 4)
                        dve.scalar_tensor_tensor(slot[:], topf[:], float(K * CAP), posc[:], ALU.mult, ALU.add).then_inc(r_count, 1)
                        dve.wait_ge(r_count, n + 5)
                        dve.tensor_scalar(fetch[:, bass.ds(tile0, TILES), :], slot[:], float(SLOTS - 1), None, ALU.min).then_inc(r_count, 3)
                        rows_seen(dve, c)
                        dve.tensor_tensor(send[:], slot[:], drop[:], ALU.add).then_inc(r_send, 1)

                    def chunk(c, first, last):
                        for i in STEPS:
                            if i >= 6 and i % 2 == 0:
                                attn_low(c, (i - 6) // 2)
                            if not first and i == 11:
                                route_softmax(c)
                            if not first and i == 15:
                                route_slots(c)
                            for name in [] if i == LAG or last else projections_at(i - 1):
                                low(c, name)
                            if i % 2 == 0 and not last:
                                keep_k(c, (i - LAG) // 2)
                            if i == 12 and not last:
                                keep_v(c, 0)
                            softmax_step(c, i, last)
                            if i - 3 < H or not last:
                                mask_own(c, i - 3)
                            if not first and i == 4:
                                dve.wait_ge(x2_ready, 2 * c)
                                norm_stats((c - 1) * TILES, stats[1], meanvar[1], r_stat, r_mv, c)
                            if not first and i == 5:
                                norm_rows((c - 1) * TILES, h2, meanvar[1], rstd[1], r_rstd, r_xn, c)
                            if not first and i == 14:
                                route_low(c)
                            if not first and i == 12:
                                route_top(c)
                            if i == 13 and not last:
                                ln_high(c, c + 2, "lnT")
                        attn_low(c, PAIRS - 1)
                        if not last:
                            keep_v(c, 1)
                            for name in projections_at(STEPS[-1]) + v_half(1):
                                low(c, name)
                            ln_first(c + 3)
                        add_attention(c, 0)
                        if not last:
                            ln_second(c + 3)
                        add_attention(c, 1)

                    dve.wait_ge(x0_loaded, 16)
                    ln_first(0)
                    dve.memset(k[:, :, :, 0:P], 0.0).then_inc(k_halo, PAIRS)
                    ln_second(0)
                    dve.memset(v[:, 0, :, :], 0.0).then_inc(v_halo, 2)
                    ln_high(-1, 0, "ln0")
                    for n, name in enumerate(HEAD_QK):
                        low(-1, name)
                        if n == 3:
                            ln_first(1)
                        if n == 5:
                            ln_second(1)
                    ln_high(-1, 1, "lnT")
                    dve.wait_ge(x_loaded, 16)
                    ln_first(2)
                    for i in range(LAG):
                        softmax_step(0, i, False)
                        if i >= 3:
                            mask_own(0, i - 3)
                        for name in HEAD_V[2 * i:2 * i + 2]:
                            low(-1, name)
                        if i == 1:
                            ln_second(2)
                    chunk(0, True, False)
                    with dve.Fori(1, NC - 1) as c:
                        chunk(c, False, False)
                    chunk(NC - 1, False, True)
                    dve.wait_ge(x2_ready, 2 * NC)
                    norm_stats((NC - 1) * TILES, stats[1], meanvar[1], r_stat, r_mv, NC)
                    norm_rows((NC - 1) * TILES, h2, meanvar[1], rstd[1], r_rstd, r_xn, NC)
                    route_low(NC)
                    route_softmax(NC)
                    route_top(NC)
                    route_slots(NC)

                @block.gpsimd
                def _(pool):
                    def reciprocal_std(mv, rs, mv_sem, var_sem, rs_sem, n):
                        stand_ge(pool, (mv_sem, n))
                        pool.tensor_scalar(rs[:, 0, :], mv[:, :, 1], 1e-5, None, ALU.add).then_inc(var_sem, 1)
                        pool.wait_ge(var_sem, n)
                        pool.tensor_tensor(rs[:, 1, :], rs[:, 0, :], half_neg[:], ALU.pow).then_inc(rs_sem, 1)

                    def ln_rstd_of(cn):
                        reciprocal_std(meanvar[0], rstd[0], ln_mv, ln_var, ln_rstd, cn + 1)

                    def ln_low(cn):
                        pool.wait_ge(ln_hi, cn + 1)
                        pool.tensor_tensor(hT[:, cn % 2, :, 1, :], h32[:], hT[:, cn % 2, :, 0, :], ALU.subtract).then_inc(ln_lo, 1)

                    def route_scale(c):
                        pool.wait_ge(r_xn, c)
                        pool.tensor_tensor(h2[:], h2[:], modrow[:, batch(c - 1), 2:3, :].to_broadcast([P, TILES, D]), ALU.mult).then_inc(r_scaled, 1)

                    def route_shift(c):
                        pool.wait_ge(r_scaled, c)
                        pool.tensor_tensor(h2[:], h2[:], modrow[:, batch(c - 1), 1:2, :].to_broadcast([P, TILES, D]), ALU.add).then_inc(r_h2, 1)

                    def prob_low(c, h):
                        pool.wait_ge(hi_ready, H * c + h + 1)
                        pool.tensor_tensor(prob16[:, h % 2, 1], prob[:, h % 2], prob16[:, h % 2, 0], ALU.subtract).then_inc(lo_ready, 1)

                    def mask_previous(c, h):
                        u = H * c + h
                        waits = [(probT_ready, u + 1)]
                        if not isinstance(c, int) or u >= 2:
                            waits.append((pv_done, u - 1))
                        stand_ge(pool, *waits)
                        pool.affine_select(out=probT_prev[:, h % 2], in_=probT[:, h % 2], pattern=[[0, 2 * TILES], [-1, P]],
                                           compare_op=ALU.is_gt, fill=zero, base=0, channel_multiplier=1).then_inc(prev_ready, 1)

                    def scatter(c, tiles):
                        if tiles[0] == 0:
                            stand_ge(pool, (r_pack, c))
                            pool.wait_ge(r_send, c)
                        for s in tiles:
                            for m in range(K):
                                pool.indirect_dma_start(
                                    out=xbuf, out_offset=bass.IndirectOffsetOnAxis(ap=send[:, s, m:m + 1], axis=0),
                                    in_=packed[:, s, :], in_offset=None, bounds_check=limit, oob_is_err=False)\
                                    .then_inc(sent, 16)

                    def chunk(c, first, last):
                        for i in STEPS:
                            if i - 3 < H or not last:
                                mask_previous(c, i - 3)
                            if i <= H or not last:
                                prob_low(c, i - 1)
                            if not first and i == 4:
                                reciprocal_std(meanvar[1], rstd[1], r_mv, r_var, r_rstd, c)
                            if not first and i == 5:
                                route_scale(c)
                            if not first and i == 7:
                                route_shift(c)
                            if i == 13 and not last:
                                ln_low(c + 2)
                            if not first and 15 <= i < 15 + TILES:
                                scatter(c, [i - 15])
                        if first:
                            pool.wait_ge(zero_sent, 16 * (SLOTS // P))
                        if not last:
                            ln_rstd_of(c + 3)
                        if not first and not last:
                            pool.wait_ge(sent, 16 * TILES * K * c)

                    limit = pool.to_reg(SLOTS - 1)
                    zero = pool.to_reg(0.0)
                    ln_rstd_of(0)
                    ln_low(0)
                    ln_rstd_of(1)
                    ln_low(1)
                    ln_rstd_of(2)
                    for i in range(1, LAG):
                        if i >= 3:
                            mask_previous(0, i - 3)
                        prob_low(0, i - 1)
                    chunk(0, True, False)
                    with pool.Fori(1, NC - 1) as c:
                        chunk(c, False, False)
                    chunk(NC - 1, False, True)
                    reciprocal_std(meanvar[1], rstd[1], r_mv, r_var, r_rstd, NC)
                    route_scale(NC)
                    route_shift(NC)
                    scatter(NC, range(TILES))
                    pool.wait_ge(sent, 16 * TILES * K * NC)

        ffn_stack = ExitStack()
        with ffn_stack:
            sb = alloc(ffn_stack)
            ps = lambda name, shape, dt: ffn_stack.enter_context(nc.psum_tensor(name, shape, dt))
            w1 = sb("w1", [P, 2, KD, 2, FF], F16)
            w2 = sb("w2", [P, 2, FT, 2, D], F16)
            rows = sb("rows", [P, 2, ST, 2 * D], F16)
            xT = sb("xT", [P, 2, 2 * KD, ST * P], F16)
            hid = sb("hid", [P, FT, 2, ST * P], F16)
            hid32 = sb("hid32", [P, 4, 512], F32)
            b2B = sb("b2B", [P, E, D], F32)
            y32 = sb("y32", [P, 2, 2, D], F32)
            up = [ps(f"up{i}", [P, 512], F32) for i in range(4)]
            down = [ps(f"down{i}", [P, 2, D], F32) for i in range(2)]
            tp = [ps(f"tp{i}", [P, 2 * KD, 2, P], F16) for i in range(2)]

            b2_loaded = sem("b2_loaded")
            rows_loaded = [sem(f"rows_loaded{i}") for i in range(2)]
            (w_hi, w_lo, xT_full, xT_ready, up_full, up_out, hid_hi, hid_ready, down_full,
             y_ready) = (sem(n) for n in ("w_hi", "w_lo", "xT_full", "xT_ready", "up_full",
                                          "up_out", "hid_hi", "hid_ready", "down_full", "y_ready"))
            y_sent = [sem(f"y_sent{i}") for i in range(2)]
            UG = len(NPART) * FT
            DG = ST // 2
            rowv = xbuf.rearrange("(e t p) d -> e p t d", p=P, t=ST)
            yv = ybuf.rearrange("(e g s p) d -> e g p s d", p=P, s=2, g=DG)

            def split_views(par, i, part):
                if i < 2:
                    return w32[:, 0, i * FF:(i + 1) * FF], w1[:, par, i, part, :]
                f = (i - 2) * FT // 2
                return (w32[:, 1, (i - 2) * 1024:(i - 1) * 1024].rearrange("p (f n) -> p f n", n=D),
                        w2[:, par, f:f + FT // 2, part, :])

            with nc.Block() as block:
                @block.sync
                def _(sp):

                    def load_weights(e):
                        if not isinstance(e, int) or e > 0:
                            sp.wait_ge(w_lo, 4 * e)
                        load_expert(sp, w32, e)

                    def load_rows(e, par):
                        if not isinstance(e, int) or e > 0:
                            sp.wait_ge(xT_full, DG * e)
                        sp.dma_start(rows[:, par], rowv[bass.ds(e, 1)].rearrange("e p t d -> (e p) t d")).then_inc(rows_loaded[par], 16)

                    def store(e, g, par):
                        sp.wait_ge(y_ready, 2 + DG * e + g + 1)
                        n = (par * DG + g) % 2
                        sp.dma_start(yv[bass.ds(e, 1), g].rearrange("e p s d -> (e p) s d"), y32[:, n]).then_inc(y_sent[n], 16)

                    for n in range(2):
                        sp.sem_inc(y_sent[n], 16)
                    load_rows(0, 0)
                    sp.dma_start(b2B[:], b2_in.partition_broadcast(P)).then_inc(b2_loaded, 16)
                    def expert(e, par, last):
                        if not last:
                            load_weights(e + 1)
                            load_rows(e + 1, 1 - par)
                        for g in range(DG):
                            store(e, g, par)

                    with sp.Fori(0, E // 2 - 1) as i:
                        for par in range(2):
                            expert(2 * i + par, par, False)
                    expert(E - 2, 0, False)
                    expert(E - 1, 1, True)
                    for n in range(2):
                        sp.wait_ge(y_sent[n], 16 * (E * DG // 2 + 1))

                @block.tensor
                def _(pe):
                    def transposes(e, par):
                        pe.wait_ge(rows_loaded[par], 8 * (e - par) + 16)
                        for g in range(DG):
                            n = (par * DG + g) % 2
                            pe.wait_ge(xT_ready, DG * e + g + 1)
                            for s in range(2):
                                for m in range(2 * KD):
                                    mm = pe.transpose(tp[n][:, m, s, :], rows[:, par, 2 * g + s, m * P:(m + 1) * P], ident16[:])
                            mm.then_inc(xT_full, 1)

                    def go_up(e, par, n):
                        if n == 0:
                            pe.wait_ge(w_lo, 4 * (e + 1))
                        lo, size = NPART[n]
                        pe.wait_ge(xT_ready, 2 + DG * e + (lo + size) // (2 * P))
                        for ft in range(FT):
                            g = UG * e + n * FT + ft
                            bank = up[ft % 4]
                            pe.wait_ge(up_out, g + 1)
                            i = 0
                            for kd in range(KD):
                                for a, b in SPLIT_PRODUCTS:
                                    mm = pe.matmul(bank[:, 0:size], w1[:, par, kd, a, ft * P:(ft + 1) * P],
                                                   xT[:, par, b * KD + kd, lo:lo + size], start=(i == 0), stop=(i == 5))
                                    i += 1
                            mm.then_inc(up_full, 1)

                    def go_down(e, par, g):
                        n = (par * DG + g) % 2
                        part = min(g // 2, 2)
                        pe.wait_ge(hid_ready, 4 + UG * e + (part + 1) * FT)
                        pe.wait_ge(y_ready, DG * e + g + 1)
                        for s in range(2):
                            t = 2 * g + s
                            i = 0
                            for ft in range(FT):
                                for a, b in SPLIT_PRODUCTS:
                                    mm = pe.matmul(down[n][:, s, :], hid[:, ft, a, t * P:(t + 1) * P], w2[:, par, ft, b, :],
                                                   start=(i == 0), stop=(i == 3 * FT - 1))
                                    i += 1
                        mm.then_inc(down_full, 1)

                    def expert(e, par, last):
                        go_up(e, par, 0)
                        go_up(e, par, 1)
                        go_down(e, par, 0)
                        go_down(e, par, 1)
                        go_up(e, par, 2)
                        go_down(e, par, 2)
                        go_down(e, par, 3)
                        if not last:
                            transposes(e + 1, 1 - par)
                        go_down(e, par, 4)

                    pe.sem_inc(down_full, DG)
                    pe.sem_inc(xT_full, DG)
                    pe.sem_inc(up_full, UG)
                    transposes(0, 0)
                    with pe.Fori(0, E // 2 - 1) as i:
                        for par in range(2):
                            expert(2 * i + par, par, False)
                    expert(E - 2, 0, False)
                    expert(E - 1, 1, True)

                @block.scalar
                def _(act):
                    act.wait_ge(b1_loaded, 16)

                    def split_high(e, par, i):
                        if i == 0:
                            act.wait_ge(w_loaded, 32 * (e + 1))
                            if not isinstance(e, int) or e > 1:
                                act.wait_ge(down_full, DG * e)
                        src, dst = split_views(par, i, 0)
                        act.activation(dst, src, ACT.Copy, scale=W_SCALE).then_inc(w_hi, 1)

                    def expert(e, par, last):
                        for k_ in range(UG):
                            n, ft = divmod(k_, FT)
                            g = UG * e + k_
                            size = NPART[n][1]
                            stand_ge(act, (up_full, UG + g + 1), (hid_ready, g + 1))
                            act.activation(hid32[:, k_ % 4, 0:size], up[ft % 4][:, 0:size], ACT.Relu, scale=1 / W_SCALE,
                                           bias=b1T[:, bass.ds(e, 1), ft:ft + 1].rearrange("p a b -> p (a b)")).then_inc(up_out, 1)
                            if k_ % 4 == 3 and 1 <= k_ // 4 <= 4 and not last:
                                split_high(e + 1, 1 - par, k_ // 4 - 1)

                    act.sem_inc(up_out, len(up))
                    for i in range(4):
                        split_high(0, 0, i)
                    with act.Fori(0, E // 2 - 1) as i:
                        for par in range(2):
                            expert(2 * i + par, par, False)
                    expert(E - 2, 0, False)
                    expert(E - 1, 1, True)

                @block.vector
                def _(dve):

                    def split_low(e, par, i):
                        dve.wait_ge(w_hi, 4 * e + i + 1)
                        src, hi = split_views(par, i, 0)
                        _, lo = split_views(par, i, 1)
                        dve.scalar_tensor_tensor(lo, src, W_SCALE, hi, ALU.mult, ALU.subtract).then_inc(w_lo, 1)

                    def copy_xT(e, par):
                        for g in range(DG):
                            n = (par * DG + g) % 2
                            dve.wait_ge(xT_full, DG * (e + 1) + g + 1)
                            if g == 0 and (not isinstance(e, int) or e > 0):
                                dve.wait_ge(up_full, UG * e)
                            dve.tensor_copy(xT[:, par, :, 2 * g * P:2 * (g + 1) * P],
                                            tp[n][:].rearrange("p m s q -> p m (s q)")).then_inc(xT_ready, 1)

                    def hidden(e, k_):
                        n, ft = divmod(k_, FT)
                        g = UG * e + k_
                        lo, size = NPART[n]
                        dve.wait_ge(up_out, 4 + g + 1)
                        if ft == 0:
                            dve.wait_ge(down_full, DG * e + min(2 * (n + 1), DG))
                        dve.tensor_copy(hid[:, ft, 0, lo:lo + size], hid32[:, k_ % 4, 0:size]).then_inc(hid_hi, 1)
                        dve.wait_ge(hid_hi, g + 1)
                        dve.tensor_tensor(hid[:, ft, 1, lo:lo + size], hid32[:, k_ % 4, 0:size],
                                          hid[:, ft, 0, lo:lo + size], ALU.subtract).then_inc(hid_ready, 1)

                    def finish(e, par, g):
                        n = (par * DG + g) % 2
                        dve.wait_ge(down_full, DG * (e + 1) + g + 1)
                        dve.wait_ge(y_sent[n], 8 * (DG * e + g - n) + 16)
                        b2 = b2B[:, bass.ds(e, 1), :].to_broadcast([P, 2, D])
                        dve.scalar_tensor_tensor(y32[:, n], down[n][:], 1 / W_SCALE, b2, ALU.mult, ALU.add).then_inc(y_ready, 1)

                    def expert(e, par, last):
                        for k_ in range(2 * FT):
                            hidden(e, k_)
                            if k_ % 4 == 3 and k_ // 4 >= 1 and not last:
                                split_low(e + 1, 1 - par, k_ // 4 - 1)
                        finish(e, par, 0)
                        finish(e, par, 1)
                        for k_ in range(2 * FT, UG):
                            hidden(e, k_)
                            if k_ % 4 == 3 and k_ == 19 and not last:
                                split_low(e + 1, 1 - par, 3)
                        finish(e, par, 2)
                        finish(e, par, 3)
                        if not last:
                            copy_xT(e + 1, 1 - par)
                        finish(e, par, 4)

                    dve.sem_inc(hid_ready, 4)
                    dve.sem_inc(xT_ready, len(tp))
                    dve.sem_inc(y_ready, len(down))
                    for i in range(4):
                        split_low(0, 0, i)
                    copy_xT(0, 0)
                    dve.wait_ge(b2_loaded, 16)
                    with dve.Fori(0, E // 2 - 1) as i:
                        for par in range(2):
                            expert(2 * i + par, par, False)
                    expert(E - 2, 0, False)
                    expert(E - 1, 1, True)

        fin_stack = ExitStack()
        with fin_stack:
            sb = alloc(fin_stack)
            RING = 4
            ytok = sb("ytok", [P, RING, K, D], F32)
            mixed = sb("mixed", [P, RING, 2, D], F32)
            fetched = [sem(f"fetched{r}") for r in range(RING)]
            out_sent = sem("out_sent")
            f_mix, out_ready = sem("f_mix"), sem("out_ready")
            with nc.Block() as block:
                @block.gpsimd
                def _(pool):
                    def fetch_tiles(i):
                        for r in range(RING):
                            at_least(pool, f_mix, 3 * (RING * (i - 1) + r + 1))
                            for m in range(K):
                                pool.indirect_dma_start(
                                    out=ytok[:, r, m, :], out_offset=None, in_=ybuf,
                                    in_offset=bass.IndirectOffsetOnAxis(
                                        ap=fetch[:, RING * i + r, m:m + 1], axis=0),
                                    bounds_check=SLOTS - 1, oob_is_err=False).then_inc(fetched[r], 16)

                    for i in range(NT // RING):
                        fetch_tiles(i)

                @block.vector
                def _(dve):
                    with dve.Fori(0, NT // RING) as i:
                        for r in range(RING):
                            t = RING * i + r
                            n = 3 * t
                            dve.wait_ge(fetched[r], 32 * (i + 1))
                            w = [weight[:, bass.ds(t, 1), m:m + 1].rearrange("p a b -> p (a b)") for m in range(K)]
                            dve.tensor_scalar(mixed[:, r, 0, :], ytok[:, r, 0, :], w[0], None, ALU.mult).then_inc(f_mix, 1)
                            dve.wait_ge(f_mix, n + 1)
                            dve.scalar_tensor_tensor(mixed[:, r, 1, :], ytok[:, r, 1, :], w[1], mixed[:, r, 0, :], ALU.mult, ALU.add)\
                               .then_inc(f_mix, 1)
                            dve.wait_ge(f_mix, n + 2)
                            gb = modrow[:, t // (NT // B), 3, :]
                            dve.tensor_tensor(mixed[:, r, 0, :], mixed[:, r, 1, :], gb, ALU.mult).then_inc(f_mix, 1)
                            dve.wait_ge(f_mix, n + 3)
                            dve.tensor_tensor(x[:, t, :], x[:, t, :], mixed[:, r, 0, :], ALU.add).then_inc(out_ready, 1)

                @block.sync
                def _(sp):
                    ot = out_rows.rearrange("(t p) d -> t p d", p=P)
                    with sp.Fori(0, NT) as t:
                        sp.wait_ge(out_ready, t + 1)
                        sp.dma_start(ot[bass.ds(t, 1)].rearrange("a p d -> (a p) d"), x[:, t, :]).then_inc(out_sent, 16)
                    sp.wait_ge(out_sent, 16 * NT)


_INS = ["L0_attn_x", "L0_attn_Wqkv", "L0_attn_Wout", "L0_ffn_gate_w", "L0_ffn_gate_b", "L0_ffn_W1", "L0_ffn_b1",
        "L0_ffn_W2", "L0_ffn_b2", "L0_c", "L0_wmod"]


def kernel(**inputs):
    import numpy as _np
    import concourse.bacc as _bacc
    from concourse import mybir as _mybir
    from concourse.bass_utils import run_bass_kernel_spmd as _run

    nc = _bacc.Bacc("TRN2", target_bir_lowering=False, num_devices=1)
    arrays, args = {}, []
    for name in _INS:
        a = _np.ascontiguousarray(inputs[name])
        arrays[f"in_{name}"] = a
        args.append(nc.dram_tensor(f"in_{name}", a.shape, _mybir.dt.from_np(a.dtype), kind="ExternalInput").ap())
    out = nc.dram_tensor("out", inputs["L0_attn_x"].shape, _mybir.dt.float32, kind="ExternalOutput").ap()
    build(nc, *args, out)
    r = _run(nc, [arrays], core_ids=[0])
    return r.results[0]["out"]
```

```python
from contextlib import ExitStack

import concourse.bass as bass
from concourse import mybir

ALU = mybir.AluOpType
ACT = mybir.ActivationFunctionType
AX = mybir.AxisListType
F32 = mybir.dt.float32
F16 = mybir.dt.float16
BF16 = mybir.dt.bfloat16
I32 = mybir.dt.int32
U32 = mybir.dt.uint32

W_SCALE = 64.0
SPLIT_PRODUCTS = ((0, 0), (0, 1), (1, 0))
MASKED = -3.0e38

P = 128
D = 256
KD = D // P
H, DH = 16, 64
PAIRS = H // 2
INNER = H * DH
CHUNK = 512
TILES = CHUNK // P
FF, E, K = 1024, 8, 2
FT = FF // P


def group_order(names):
    place, count = {}, [0, 0]
    for n, name in enumerate(names):
        place[name] = (n % 2, count[n % 2])
        count[n % 2] += 1
    return place, count


def build(nc, x_in, wqkv_in, wout_in, gate_w, gate_b, w1_in, b1_in, w2_in, b2_in, c_in, wmod_in, out):
    B, S, _ = x_in.shape
    T = B * S
    NT = T // P
    NC = T // CHUNK
    CPB = S // CHUNK
    CAP = 640
    SLOTS = E * K * CAP
    ST = K * CAP // P
    NPART = ((0, 512), (512, 512), (1024, 256))
    FAR = 100000.0

    x_rows = x_in.rearrange("b s d -> (b s) d")
    out_rows = out.rearrange("b s d -> (b s) d")
    w1v = w1_in.rearrange("e (k p) n -> e p k n", p=P)
    w2v = w2_in.rearrange("e (f p) n -> e p f n", p=P)
    ROW = 2 * D + 2
    xbuf = nc.dram_tensor("slot_inputs", (SLOTS, ROW), F16, kind="Internal").ap()
    ytok = [nc.dram_tensor(f"choice{m}_outputs", (T, D), F32, kind="Internal").ap() for m in range(K)]

    whole = ExitStack()
    with whole:
        def alloc(stack):
            return lambda name, shape, dt: stack.enter_context(nc.sbuf_tensor(name, shape, dt))

        def sem(name):
            return whole.enter_context(nc.semaphore(name))

        keep_sb = alloc(whole)
        x = keep_sb("x", [P, NT, D], F32)
        modrow = keep_sb("modrow", [P, B, 4, D], F32)
        weight = keep_sb("weight", [P, NT, K], F32)
        b1T = keep_sb("b1T", [P, E, FT], F32)
        big = keep_sb("big", [P, KD * 2 * 3 * INNER], F16)
        w32 = big[:, 0:4 * KD * FF].bitcast(F32).rearrange("p (m n) -> p m n", m=2)
        ident16 = keep_sb("ident16", [P, P], F16)

        x0_loaded, x_loaded, small_loaded, zero_sent = (sem(n) for n in ("x0_loaded", "x_loaded", "small_loaded", "zero_sent"))
        stage_loaded = [sem(f"stage_loaded{i}") for i in range(4)]
        consts, b1_loaded, stage_scaled, rows_made, y_zeroed, token_put = (
            sem(n) for n in ("consts", "b1_loaded", "stage_scaled", "rows_made", "y_zeroed", "token_put"))
        w_loaded = sem("w_loaded")
        exp_c, sil, sil_b, mod_mm, mod_row, split_hi, split_lo = (
            sem(n) for n in ("exp_c", "sil", "sil_b", "mod_mm", "mod_row", "split_hi", "split_lo"))

        def stand_ge(eng, *waits):
            ready = [(s, v if isinstance(v, int) else eng.compute_val(v)) for s, v in waits]
            if not all(isinstance(v, int) for _, v in ready):
                eng.wait_ge(consts, 2)
            for s, v in ready:
                eng.wait_ge(s, v)

        def load_expert(sp, dst, e):
            sp.dma_start(dst[:, 0, :].rearrange("p (k n) -> p k n", k=KD),
                         w1v[bass.ds(e, 1)].rearrange("e p k n -> (e p) k n")).then_inc(w_loaded, 16)
            sp.dma_start(dst[:, 1, :].rearrange("p (f n) -> p f n", f=FT),
                         w2v[bass.ds(e, 1)].rearrange("e p f n -> (e p) f n")).then_inc(w_loaded, 16)

        def at_least(eng, s, value):
            if not isinstance(value, int) or value > 0:
                eng.wait_ge(s, value)

        attn_stack = ExitStack()
        with attn_stack:
            sb = alloc(attn_stack)
            ps = lambda name, shape, dt: attn_stack.enter_context(nc.psum_tensor(name, shape, dt))
            wqkv = big[:].rearrange("p (a b c) -> p a b c", a=KD, b=2)
            wout = sb("wout", [P, PAIRS, 2, D], F16)
            hT = sb("hT", [P, 2, KD, 2, CHUNK], F16)
            q = sb("q", [P, PAIRS, 2, CHUNK], F16)
            k = sb("k", [P, PAIRS, 2, P + CHUNK], F16)
            v = sb("v", [P, 1 + TILES, 2, INNER], F16)
            attn = sb("attn", [P, PAIRS, 2, CHUNK], F16)
            prob = sb("prob", [P, 2, TILES, P], F32)
            prob16 = sb("prob16", [P, 2, 2, TILES, P], F16)
            probT = sb("probT", [P, 2, 2 * TILES, P], F16)
            probT_cur = sb("probT_cur", [P, 2, 2 * TILES, P], F16)
            probT_prev = sb("probT_prev", [P, 2, 2 * TILES, P], F16)
            xn = sb("xn", [P, TILES, D], F32)
            h32 = sb("h32", [P, KD, CHUNK], F32)
            h2 = sb("h2", [P, TILES, D], F32)
            packed = sb("packed", [P, TILES, ROW], F16)
            token_no = sb("token_no", [P, NT], F32)
            h2T = sb("h2T", [P, 2, KD, CHUNK], F16)
            gated = sb("gated", [P, 2, D], F32)
            empty_row = sb("empty_row", [P, ROW], F16)
            zero_row = sb("zero_row", [P, 2, D], F32)
            identf = sb("identf", [P, P], F32)
            onesf = sb("onesf", [P, P], F32)
            ones16 = sb("ones16", [P, P], F16)
            above16 = sb("above16", [P, P], F16)
            above = sb("above", [P, P], F32)
            keys_cur = sb("keys_cur", [P, P], F16)
            ones_row = sb("ones_row", [1, P], BF16)
            no_prev = sb("no_prev", [1, NC, P], BF16)
            cT = sb("cT", [P, KD, B], F32)
            silT = sb("silT", [P, 3, KD * B], F32)
            silB = sb("silB", [P, KD * B, P], F32)
            modcol = sb("modcol", [P, 4, B], F32)
            gwT = sb("gwT", [P, KD, E], F32)
            gate16 = sb("gate16", [P, KD, 2, E], F16)
            gbB = sb("gbB", [P, E], F32)
            expert_no = sb("expert_no", [P, E], F32)
            choice_base = sb("choice_base", [P, TILES, K], F32)
            half_neg = sb("half_neg", [P, TILES], F32)
            rowmax = sb("rowmax", [P, 2, TILES], F32)
            negmax = sb("negmax", [P, 2, TILES], F32)
            rowsum = sb("rowsum", [P, 2, TILES], F32)
            rinv = sb("rinv", [P, 2, TILES], F32)
            stats = [sb(f"stats{i}", [P, TILES, 6], F32) for i in range(2)]
            meanvar = [sb(f"meanvar{i}", [P, TILES, 2], F32) for i in range(2)]
            rstd = [sb(f"rstd{i}", [P, 2, TILES], F32) for i in range(2)]
            logit = sb("logit", [P, TILES, E], F32)
            lmax = sb("lmax", [P, TILES], F32)
            lsum = sb("lsum", [P, 2, TILES], F32)
            top = sb("top", [P, TILES, 8], F32)
            topi = sb("topi", [P, TILES, 8], U32)
            topf = sb("topf", [P, TILES, K], F32)
            onehot = sb("onehot", [P, TILES, K, E], F16)
            cum = sb("cum", [P, TILES, K, E], F32)
            carry = sb("carry", [P, K, E], F32)
            pos = sb("pos", [P, TILES, K], F32)
            posc = sb("posc", [P, TILES, K], F32)
            slot = sb("slot", [P, TILES, K], F32)
            drop = sb("drop", [P, TILES, K], F32)
            send = sb("send", [P, TILES, K], U32)

            score = [ps(f"score{i}", [P, TILES, 2 * P], F32) for i in range(2)]
            pt = ps("pt", [P, 2 * TILES, P], F16)
            pv = ps("pv", [P, CHUNK], F32)
            gen = [ps(f"gen{i}", [P, 512], F32) for i in range(2)]

            stage = [t[:].rearrange("p a b c -> p (a b c)").bitcast(F32)[:, i * 2048:(i + 1) * 2048]
                     for t in (q, attn) for i in range(2)]
            wmod = k[:].rearrange("p a b c -> p (a b c)").bitcast(F32)[:, 0:KD * 6 * D].rearrange("p (k n) -> p k n", k=KD)
            stage_src = [wqkv_in.rearrange("(k p) n -> p k n", p=P)[:, :, i * INNER:(i + 1) * INNER] for i in range(3)]
            stage_src.append(wout_in.rearrange("(j p) n -> p j n", p=P))
            stage_view = [stage[i].rearrange("p (k n) -> p k n", k=KD if i < 3 else PAIRS) for i in range(4)]

            def stage_dst(i, part):
                return wqkv[:, :, part, i * INNER:(i + 1) * INNER] if i < 3 else wout[:, :, part, :]

            ln_stat, ln_mv, ln_var, ln_rstd, ln_xn, ln_hi, ln_lo = (
                sem(n) for n in ("ln_stat", "ln_mv", "ln_var", "ln_rstd", "ln_xn", "ln_hi", "ln_lo"))

            def norm_stats(dve, tile0, st, mv, stat_sem, mv_sem, n):
                for s in range(TILES):
                    op = dve.bn_stats(st[:, s, :], x[:, tile0 + s, :])
                op.then_inc(stat_sem, 1)
                stand_ge(dve, (stat_sem, n))
                for s in range(TILES):
                    op = dve.bn_aggr(mv[:, s, :], st[:, s, :])
                op.then_inc(mv_sem, 1)

            def norm_rows(dve, tile0, dst, mv, rs, rs_sem, xn_sem, n):
                dve.wait_ge(rs_sem, n)
                for s in range(TILES):
                    op = dve.tensor_scalar(dst[:, s, :], x[:, tile0 + s, :], mv[:, s, 0:1], rs[:, 1, s:s + 1],
                                           ALU.subtract, ALU.mult)
                op.then_inc(xn_sem, 1)

            def reciprocal_std(pool, mv, rs, mv_sem, var_sem, rs_sem, n):
                stand_ge(pool, (mv_sem, n))
                pool.tensor_scalar(rs[:, 0, :], mv[:, :, 1], 1e-5, None, ALU.add).then_inc(var_sem, 1)
                pool.wait_ge(var_sem, n)
                pool.tensor_tensor(rs[:, 1, :], rs[:, 0, :], half_neg[:], ALU.pow).then_inc(rs_sem, 1)


            with nc.Block() as block:
                @block.sync
                def _(sp):
                    for b in range(B):
                        sp.dma_start(cT[:, :, b], c_in[b].rearrange("(k p) -> p k", p=P), allow_slow_non_contiguous=True)\
                          .then_inc(small_loaded, 16)
                    sp.dma_start(wmod, wmod_in.rearrange("(k p) n -> p k n", p=P)).then_inc(small_loaded, 16)
                    for kd in range(KD):
                        sp.dma_start(gwT[:, kd, :], gate_w[:, kd * P:(kd + 1) * P].rearrange("e p -> p e"),
                                     allow_slow_non_contiguous=True).then_inc(small_loaded, 16)
                    sp.dma_start(gbB[:], gate_b.partition_broadcast(P)).then_inc(small_loaded, 16)
                    xt = x_rows.rearrange("(t p) d -> p t d", p=P)
                    sp.dma_start(x[:, 0:TILES, :], xt[:, 0:TILES, :]).then_inc(x0_loaded, 16)
                    for i in range(4):
                        sp.dma_start(stage_view[i], stage_src[i]).then_inc(stage_loaded[i], 16)
                    sp.dma_start(x[:, TILES:, :], xt[:, TILES:, :]).then_inc(x_loaded, 16)
                    sp.dma_start(b1T[:].rearrange("p e f -> p (e f)"), b1_in.rearrange("e (f p) -> p (e f)", p=P),
                                 allow_slow_non_contiguous=True).then_inc(b1_loaded, 16)

                @block.gpsimd
                def _(pool):
                    pool.memset(onesf[:], 1.0)
                    pool.memset(identf[:], 0.0)
                    pool.memset(keys_cur[:], 1.0).then_inc(consts, 1)
                    pool.wait_ge(consts, 1)
                    pool.affine_select(out=identf[:], in_=identf[:], pattern=[[-1, P]], compare_op=ALU.not_equal,
                                       fill=1.0, base=0, channel_multiplier=1)
                    pool.affine_select(out=above[:], in_=onesf[:], pattern=[[1, P]], compare_op=ALU.is_gt,
                                       fill=0.0, base=0, channel_multiplier=-1)
                    pool.affine_select(out=keys_cur[:], in_=keys_cur[:], pattern=[[1, P]], compare_op=ALU.is_ge,
                                       fill=0.0, base=0, channel_multiplier=-1)
                    pool.iota(token_no[:], pattern=[[P, NT]], base=0, channel_multiplier=1, allow_small_or_imprecise_dtypes=True)
                    pool.iota(expert_no[:], pattern=[[1, E]], base=0, channel_multiplier=0,
                              allow_small_or_imprecise_dtypes=True).then_inc(consts, 1)
                    reciprocal_std(pool, meanvar[0], rstd[0], ln_mv, ln_var, ln_rstd, 1)
                    for i in range(2, 4):
                        pool.wait_ge(split_hi, i + 1)
                        pool.tensor_tensor(stage_dst(i, 1), stage_view[i], stage_dst(i, 0), ALU.subtract).then_inc(split_lo, 1)

                @block.vector
                def _(dve):
                    dve.memset(zero_row[:], 0.0)
                    dve.memset(empty_row[:], 0.0).then_inc(rows_made, 1)
                    dve.wait_ge(rows_made, 1)
                    dve.memset(empty_row[:, 2 * D:].bitcast(I32), int(FAR))
                    dve.memset(ones_row[:], 1.0)
                    for c in range(NC):
                        dve.memset(no_prev[:, c, :], MASKED if c % CPB == 0 else 0.0)
                    dve.memset(carry[:], 0.0)
                    for c in range(K):
                        dve.memset(choice_base[:, :, c:c + 1], float(c * CAP))
                    dve.memset(half_neg[:], -0.5)
                    dve.wait_ge(consts, 2)
                    dve.tensor_copy(ident16[:], identf[:])
                    dve.tensor_copy(ones16[:], onesf[:])
                    dve.tensor_copy(above16[:], above[:])
                    dve.wait_ge(exp_c, 1)
                    dve.tensor_scalar(silT[:, 1, :], silT[:, 0, :], 1.0, None, ALU.add).then_inc(sil, 1)
                    dve.wait_ge(sil, 1)
                    dve.reciprocal(silT[:, 2, :], silT[:, 1, :]).then_inc(sil, 1)
                    dve.wait_ge(sil, 2)
                    dve.tensor_tensor(silT[:, 0, :], silT[:, 2, :], cT[:].rearrange("p k b -> p (k b)"), ALU.mult).then_inc(sil, 1)
                    dve.wait_ge(sil, 3)
                    dve.tensor_copy(silB[:], silT[:, 0, :].unsqueeze(2).to_broadcast([P, KD * B, P])).then_inc(sil_b, 1)
                    dve.tensor_scalar(gate16[:, :, 0, :], gwT[:], W_SCALE, None, ALU.mult).then_inc(sil, 1)
                    dve.wait_ge(sil, 4)
                    dve.scalar_tensor_tensor(gate16[:, :, 1, :], gwT[:], W_SCALE, gate16[:, :, 0, :], ALU.mult, ALU.subtract)
                    dve.wait_ge(x0_loaded, 16)
                    norm_stats(dve, 0, stats[0], meanvar[0], ln_stat, ln_mv, 1)
                    norm_rows(dve, 0, xn, meanvar[0], rstd[0], ln_rstd, ln_xn, 1)
                    dve.wait_ge(mod_mm, 1)
                    mc = gen[0][:, 0:4 * B].rearrange("p (j b) -> p j b", b=B)
                    dve.tensor_copy(modcol[:, 0:2, :], mc[:, 0:2, :])
                    dve.tensor_scalar(modcol[:, 2:4, :], mc[:, 2:4, :], 1.0, None, ALU.add)
                    for i in range(2):
                        dve.wait_ge(split_hi, i + 1)
                        dve.scalar_tensor_tensor(stage_dst(i, 1), stage_view[i], W_SCALE, stage_dst(i, 0),
                                                 ALU.mult, ALU.subtract).then_inc(split_lo, 1)
                    for b in range(B):
                        dve.wait_ge(mod_mm, 2 + b)
                        ga, gb = score[b][:, 0:1, :], score[b][:, 3:4, :]
                        dve.tensor_copy(modrow[:, b, 1:2, :], score[b][:, 1:2, :])
                        dve.tensor_scalar(modrow[:, b, 2:3, :], score[b][:, 2:3, :], 1.0, None, ALU.add)
                        for n, (gate, row) in enumerate(((ga, 0), (gb, 3))):
                            dve.tensor_scalar(gated[:, 0:1, :], gate, 0.0, 2.0, ALU.is_ge, ALU.mult).then_inc(mod_row, 1)
                            dve.tensor_scalar(h2[:, 0:1, :], gate, -1.0, None, ALU.mult).then_inc(mod_row, 1)
                            dve.wait_ge(mod_row, 8 * b + 4 * n + 2)
                            dve.scalar_tensor_tensor(gated[:, 1:2, :], gate, 0.25, h2[:, 0:1, :], ALU.max, ALU.max).then_inc(mod_row, 1)
                            dve.wait_ge(mod_row, 8 * b + 4 * n + 3)
                            dve.scalar_tensor_tensor(modrow[:, b, row:row + 1, :], gated[:, 0:1, :], -1.0,
                                                     gated[:, 1:2, :], ALU.add, ALU.mult).then_inc(mod_row, 1)
                            dve.wait_ge(mod_row, 8 * b + 4 * n + 4)

                @block.scalar
                def _(act):
                    act.wait_ge(small_loaded, 16 * (B + KD + 2))
                    act.activation(silT[:, 0, :], cT[:].rearrange("p k b -> p (k b)"), ACT.Exp, scale=-1.0).then_inc(exp_c, 1)
                    for i in range(4):
                        act.wait_ge(stage_loaded[i], 16)
                        if i >= 2:
                            act.activation(stage_view[i], stage_view[i], ACT.Copy, scale=W_SCALE).then_inc(stage_scaled, 1)
                            act.wait_ge(stage_scaled, i - 1)
                        act.activation(stage_dst(i, 0), stage_view[i], ACT.Copy, scale=1.0 if i >= 2 else W_SCALE).then_inc(split_hi, 1)

                @block.tensor
                def _(pe):
                    pe.wait_ge(sil, 3)
                    pe.wait_ge(small_loaded, 16 * (B + KD + 2))
                    silm = silT[:, 0, :].rearrange("p (k b) -> p k b", b=B)
                    for j in range(4):
                        for kd in range(KD):
                            mm = pe.matmul(gen[0][:, j * B:(j + 1) * B], wmod[:, kd, j * P:(j + 1) * P], silm[:, kd, :],
                                           start=(kd == 0), stop=(kd == KD - 1))
                    mm.then_inc(mod_mm, 1)
                    pe.wait_ge(sil_b, 1)
                    for b in range(B):
                        flat = score[b][:].rearrange("p a b -> p (a b)")
                        for half in range(2):
                            for kd in range(KD):
                                mm = pe.matmul(flat[:, half * 512:(half + 1) * 512], silB[:, kd * B + b, :],
                                               wmod[:, kd, 2 * D + half * 512:2 * D + (half + 1) * 512],
                                               start=(kd == 0), stop=(kd == KD - 1))
                        mm.then_inc(mod_mm, 1)

            ln_groups = [("lnT", 0), ("lnT", 1)]
            route_groups = [("h2T", 0), ("h2T", 1), ("logits",), ("counts",)]
            out_groups = [("out", 0), ("out", 1)]
            LAG = 4
            STEPS = range(LAG, H + LAG)
            v_half = lambda half: [("v", half, s) for s in range(TILES)]
            qk_pair = lambda j: [("q", j), ("k", j)]
            HEAD_QK = sum([qk_pair(j) for j in range(PAIRS)], [])
            HEAD_V = v_half(0) + v_half(1)
            HEAD = [("ln0", 0), ("ln0", 1)] + HEAD_QK + ln_groups + HEAD_V

            def projections_at(i):
                v_tiles = {12: 0, 13: 1, 14: 2, 16: 3}
                return [("qk"[i % 2], (i - LAG) // 2)] + ([("v", 0, v_tiles[i])] if i in v_tiles else [])

            def chunk_groups(first, last):
                names = []
                for i in STEPS:
                    if not first:
                        names += {10: route_groups[0:2], 11: route_groups[2:3], 15: route_groups[3:4]}.get(i, [])
                    if i == 5 and not last:
                        names += ln_groups
                    if not last:
                        names += projections_at(i)
                return names + ([] if last else v_half(1)) + out_groups

            kinds = [HEAD, chunk_groups(True, False), chunk_groups(False, False), chunk_groups(False, True), route_groups]
            orders = [group_order(names) for names in kinds]

            def group(c, name):
                kind = 0 if isinstance(c, int) and c == -1 else 1 if isinstance(c, int) and c == 0 else \
                    4 if isinstance(c, int) and c == NC else 3 if isinstance(c, int) and c == NC - 1 else 2
                bank, before = orders[kind][0][name]
                counts = [o[1][bank] for o in orders]
                if kind >= 1:
                    before = before + counts[0]
                if kind == 2:
                    before = before + counts[1] + (c - 1) * counts[2]
                if kind >= 3:
                    before = before + counts[1] + (NC - 2) * counts[2]
                if kind == 4:
                    before = before + counts[3]
                return bank, before

            gen_full = [sem(f"gen_full{i}") for i in range(2)]
            gen_free = [sem(f"gen_free{i}") for i in range(2)]
            (scores_done, merged, maxed, neg_ready, exp_done, rinv_ready, norm_ready, hi_ready, lo_ready, pt_done,
             probT_ready, cur_ready, prev_ready, pv_done, attn_hi, attn_lo, proj_hi, k_halo, v_halo) = (sem(n) for n in (
                 "scores_done", "merged", "maxed", "neg_ready", "exp_done", "rinv_ready", "norm_ready", "hi_ready",
                 "lo_ready", "pt_done", "probT_ready", "cur_ready", "prev_ready", "pv_done", "attn_hi", "attn_lo",
                 "proj_hi", "k_halo", "v_halo"))
            x2_ready, r_stat, r_mv, r_var, r_rstd, r_xn, r_scaled, r_h2, r_pack_hi, r_pack = (
                sem(n) for n in ("x2_ready", "r_stat", "r_mv", "r_var", "r_rstd", "r_xn", "r_scaled",
                                 "r_h2", "r_pack_hi", "r_pack"))
            r_soft, r_exp, r_count, r_send, sent = (sem(n) for n in ("r_soft", "r_exp", "r_count", "r_send", "sent"))
            PROJ = 2 * PAIRS + 2 * TILES

            def proj_no(c, name):
                order = HEAD_QK + HEAD_V if isinstance(c, int) and c == 0 else [n for n in chunk_groups(False, False) if n[0] in "qkv"]
                return c * PROJ + order.index(name) + 1

            def batch(c):
                return c // CPB

            def rows_seen(eng, c):
                if isinstance(c, int) and c == NC:
                    eng.wait_ge(sent, 16 * TILES * K * (NC - 1))
                else:
                    eng.wait_ge(prev_ready, H * c + 2)

            def route_scale(eng, c):
                eng.wait_ge(r_xn, c)
                eng.tensor_tensor(h2[:], h2[:], modrow[:, batch(c - 1), 2:3, :].to_broadcast([P, TILES, D]), ALU.mult).then_inc(r_scaled, 1)

            def route_shift(eng, c):
                eng.wait_ge(r_scaled, c)
                eng.tensor_tensor(h2[:], h2[:], modrow[:, batch(c - 1), 1:2, :].to_broadcast([P, TILES, D]), ALU.add).then_inc(r_h2, 1)

            def route_low(eng, c):
                eng.wait_ge(r_pack_hi, c)
                eng.tensor_tensor(packed[:, :, D:2 * D], h2[:], packed[:, :, 0:D], ALU.subtract).then_inc(r_pack, 1)

            with nc.Block() as block:
                @block.sync
                def _(sp):
                    with sp.Fori(0, SLOTS // P) as i:
                        sp.dma_start(xbuf[bass.ts(i, P), :], empty_row[:]).then_inc(zero_sent, 16)
                    sp.wait_ge(zero_sent, 16 * (SLOTS // P))
                    with sp.Fori(0, T // (2 * P)) as i:
                        for m in range(K):
                            sp.dma_start(ytok[m].rearrange("(a s p) d -> a p s d", p=P, s=2)[bass.ds(i, 1)].rearrange("a p s d -> (a p) s d"),
                                         zero_row[:]).then_inc(y_zeroed, 16)
                    sp.wait_ge(y_zeroed, 16 * K * T // (2 * P))
                    sp.wait_ge(x2_ready, 2 * (NC - 1))
                    load_expert(sp, w32, 0)

                @block.tensor
                def _(pe):
                    def claim(c, name):
                        bank, before = group(c, name)
                        at_least(pe, gen_free[bank], before)
                        return gen[bank], gen_full[bank]

                    def ln_transposes(c, cn, label):
                        pe.wait_ge(ln_xn, cn + 1)
                        for kd in range(KD):
                            dst, full = claim(c, (label, kd))
                            for s in range(TILES):
                                mm = pe.transpose(dst[:, s * P:(s + 1) * P], xn[:, s, kd * P:(kd + 1) * P], identf[:])
                            mm.then_inc(full, 1)

                    def project_qk(c, name):
                        cn = c + 1
                        j = name[1]
                        col = j * P + (INNER if name[0] == "k" else 0)
                        if name == ("q", 0):
                            pe.wait_ge(ln_lo, cn + 1)
                        dst, full = claim(c, name)
                        n = 0
                        for a, b in SPLIT_PRODUCTS:
                            for kd in range(KD):
                                mm = pe.matmul(dst[:], wqkv[:, kd, a, col:col + P], hT[:, cn % 2, kd, b, :],
                                               start=(n == 0), stop=(n == 5))
                                n += 1
                        mm.then_inc(full, 1)

                    def project_v(c, half, tiles=range(TILES)):
                        cn = c + 1
                        for s in tiles:
                            dst, full = claim(c, ("v", half, s))
                            n = 0
                            for a, b in SPLIT_PRODUCTS:
                                for kd in range(KD):
                                    mm = pe.matmul(dst[:], hT[:, cn % 2, kd, a, s * P:(s + 1) * P],
                                                   wqkv[:, kd, b, 2 * INNER + half * 512:2 * INNER + (half + 1) * 512],
                                                   start=(n == 0), stop=(n == 5))
                                    n += 1
                            mm.then_inc(full, 1)

                    def scores(c, h):
                        if h >= H:
                            c, h = c + 1, h - H
                        u, j, r = H * c + h, h // 2, DH * (h % 2)
                        dst = score[h % 2]
                        if h % 2 == 0:
                            if isinstance(c, int) and c == 0:
                                for name in qk_pair(j):
                                    bank, before = group(-1, name)
                                    pe.wait_ge(gen_free[bank], before + 1)
                            else:
                                pe.wait_ge(norm_ready, H * (c - 1) + h + 6)
                        at_least(pe, exp_done, u - 1)
                        for b in range(TILES):
                            for n, (a, m) in enumerate(SPLIT_PRODUCTS):
                                mm = pe.matmul(dst[:, b, :], q[r:r + DH, j, a, b * P:(b + 1) * P],
                                               k[r:r + DH, j, m, b * P:(b + 2) * P], start=(n == 0),
                                               stop=(n == 2), skip_group_check=(b == 0))
                            if b == 0:
                                mm = pe.matmul(dst[:, 0, 0:P], ones_row[:], no_prev[:, c, :], start=False, stop=True,
                                               skip_group_check=True)
                        mm.then_inc(scores_done, 1)

                    def transposes(c, h):
                        u = H * c + h
                        pe.wait_ge(lo_ready, u + 1)
                        at_least(pe, probT_ready, u)
                        for part in range(2):
                            for b in range(TILES):
                                mm = pe.transpose(pt[:, part * TILES + b, :], prob16[:, h % 2, part, b, :], ident16[:])
                        mm.then_inc(pt_done, 1)

                    def weighted_values(c, h):
                        u, j, r = H * c + h, h // 2, DH * (h % 2)
                        pe.wait_ge(prev_ready, u + 1)
                        pe.wait_ge(cur_ready, u + 1)
                        if h % 2 == 0:
                            at_least(pe, attn_lo, PAIRS * c + j)
                        if h % (H // 2) == 0:
                            half = h // (H // 2)
                            if isinstance(c, int) and c == 0:
                                for s in range(TILES):
                                    bank, before = group(-1, ("v", half, s))
                                    pe.wait_ge(gen_free[bank], before + 1)
                            elif half == 0:
                                pe.wait_ge(attn_lo, PAIRS * c)
                            else:
                                pe.wait_ge(x2_ready, 2 * c)
                        for b in range(TILES):
                            n = 0
                            for a, m in SPLIT_PRODUCTS:
                                for blk, pr in ((b + 1, probT_cur), (b, probT_prev)):
                                    mm = pe.matmul(pv[r:r + DH, b * P:(b + 1) * P], v[:, blk, a, h * DH:(h + 1) * DH],
                                                   pr[:, h % 2, m * TILES + b, :], start=(n == 0), stop=(n == 5))
                                    n += 1
                        mm.then_inc(pv_done, 1)

                    def project_out(c):
                        pe.wait_ge(attn_lo, PAIRS * (c + 1))
                        for p in range(2):
                            dst, full = claim(c, ("out", p))
                            for s in range(2):
                                t = 2 * p + s
                                n = 0
                                for j in range(PAIRS):
                                    for a, b in SPLIT_PRODUCTS:
                                        mm = pe.matmul(dst[:, s * D:(s + 1) * D], attn[:, j, a, t * P:(t + 1) * P],
                                                       wout[:, j, b, :], start=(n == 0), stop=(n == 3 * PAIRS - 1))
                                        n += 1
                            mm.then_inc(full, 1)

                    def route_transposes(c):
                        pe.wait_ge(r_pack, c)
                        for part in range(2):
                            dst, full = claim(c, ("h2T", part))
                            half = dst[:].bitcast(F16)
                            for kd in range(KD):
                                for s in range(TILES):
                                    at = part * D + kd * P
                                    mm = pe.transpose(half[:, kd * CHUNK + s * P:kd * CHUNK + (s + 1) * P], packed[:, s, at:at + P], ident16[:])
                            mm.then_inc(full, 1)

                    def route_logits(c):
                        for kd in range(KD):
                            bank, before = group(c, ("h2T", kd))
                            pe.wait_ge(gen_free[bank], before + 1)
                        dst, full = claim(c, ("logits",))
                        for s in range(TILES):
                            n = 0
                            for kd in range(KD):
                                for a, b in SPLIT_PRODUCTS:
                                    mm = pe.matmul(dst[:, s * E:(s + 1) * E], h2T[:, a, kd, s * P:(s + 1) * P], gate16[:, kd, b, :],
                                                   start=(n == 0), stop=(n == 3 * KD - 1))
                                    n += 1
                        mm.then_inc(full, 1)

                    def route_counts(c):
                        pe.wait_ge(r_soft, 11 * c)
                        dst, full = claim(c, ("counts",))
                        KE = K * E
                        hot = onehot[:].rearrange("p s c e -> p s (c e)")
                        for s in range(TILES + 1):
                            last = min(s, TILES - 1)
                            for m in range(last + 1):
                                mm = pe.matmul(dst[:, s * KE:(s + 1) * KE], above16[:] if m == s else ones16[:], hot[:, m, :],
                                               start=(m == 0), stop=(m == last))
                        mm.then_inc(full, 1)

                    def chunk(c, first, last):
                        for i in STEPS:
                            if i < H or not last:
                                scores(c, i)
                            weighted_values(c, i - 4)
                            if i - 2 < H or not last:
                                transposes(c, i - 2)
                            if not first and i == 10:
                                route_transposes(c)
                            if not first and i == 11:
                                route_logits(c)
                            if not first and i == 15:
                                route_counts(c)
                            if i == 5 and not last:
                                ln_transposes(c, c + 2, "lnT")
                            for name in [] if last else projections_at(i):
                                if name[0] == "v":
                                    project_v(c, 0, [name[2]])
                                else:
                                    project_qk(c, name)
                        if not last:
                            project_v(c, 1)
                        project_out(c)

                    ln_transposes(-1, 0, "ln0")
                    for j in range(PAIRS):
                        project_qk(-1, ("q", j))
                        project_qk(-1, ("k", j))
                    ln_transposes(-1, 1, "lnT")
                    for i in range(LAG):
                        scores(0, i)
                        if i >= 2:
                            transposes(0, i - 2)
                        project_v(-1, i // 2, range(2 * (i % 2), 2 * (i % 2) + 2))
                    chunk(0, True, False)
                    with pe.Fori(1, NC - 1) as c:
                        chunk(c, False, False)
                    chunk(NC - 1, False, True)
                    route_transposes(NC)
                    route_logits(NC)
                    route_counts(NC)

                @block.scalar
                def _(act):
                    def ln_modulate(c, cn, label):
                        for kd in range(KD):
                            bank, before = group(c, (label, kd))
                            stand_ge(act, (gen_full[bank], before + 1))
                            at_least(act, ln_lo, cn)
                            b = batch(clip(cn))
                            act.activation(h32[:, kd, :], gen[bank][:], ACT.Identity,
                                           bias=modcol[:, kd, bass.ds(b, 1)], scale=modcol[:, 2 + kd, bass.ds(b, 1)])\
                               .then_inc(gen_free[bank], 1)

                    def high(c, name):
                        cn = c + 1
                        bank, before = group(c, name)
                        act.wait_ge(gen_full[bank], before + 1)
                        if name[0] == "q":
                            at_least(act, scores_done, H * c + 2 * name[1] + 2)
                            dst = q[:, name[1], 0, :]
                        elif name[0] == "k":
                            act.wait_ge(k_halo, PAIRS * cn + name[1] + 1)
                            dst = k[:, name[1], 0, P:]
                        else:
                            act.wait_ge(v_halo, 2 * cn + name[1] + 1)
                            dst = v[:, 1 + name[2], 0, name[1] * 512:(name[1] + 1) * 512]
                        act.activation(dst, gen[bank][:], ACT.Copy, scale=1 / W_SCALE).then_inc(proj_hi, 1)

                    def exponentials(c, h):
                        u = H * c + h
                        act.wait_ge(neg_ready, u + 1)
                        at_least(act, lo_ready, u - 1)
                        for b in range(TILES):
                            mm = act.activation(prob[:, h % 2, b, :], score[h % 2][:, b, P:], ACT.Exp, scale=DH ** -0.5,
                                                bias=negmax[:, h % 2, b:b + 1], accum_out=rowsum[:, h % 2, b:b + 1])
                        mm.then_inc(exp_done, 1)

                    def prob_high(c, h):
                        u = H * c + h
                        act.wait_ge(norm_ready, u + 1)
                        at_least(act, pt_done, u - 1)
                        act.activation(prob16[:, h % 2, 0], prob[:, h % 2], ACT.Copy).then_inc(hi_ready, 1)

                    def copy_probT(c, h):
                        u = H * c + h
                        act.wait_ge(pt_done, u + 1)
                        at_least(act, prev_ready, u - 1)
                        at_least(act, cur_ready, u - 1)
                        act.activation(probT[:, h % 2], pt[:], ACT.Copy).then_inc(probT_ready, 1)

                    def attn_high(c, j):
                        act.wait_ge(pv_done, H * c + 2 * j + 2)
                        if j == 0:
                            at_least(act, x2_ready, 2 * c)
                        act.activation(attn[:, j, 0, :], pv[:], ACT.Copy).then_inc(attn_hi, 1)

                    def route_pack(c):
                        act.wait_ge(r_h2, c)
                        rows_seen(act, c)
                        act.activation(packed[:, :, 0:D], h2[:], ACT.Copy).then_inc(r_pack_hi, 1)

                    def route_h2T(c):
                        for kd in range(KD):
                            bank, before = group(c, ("h2T", kd))
                            act.wait_ge(gen_full[bank], before + 1)
                            act.activation(h2T[:, kd].rearrange("p k n -> p (k n)"), gen[bank][:].bitcast(F16), ACT.Copy)\
                               .then_inc(gen_free[bank], 1)

                    def route_exp(c):
                        act.wait_ge(r_soft, 11 * (c - 1) + 3)
                        act.activation(logit[:], logit[:], ACT.Exp).then_inc(r_exp, 1)

                    def chunk(c, first, last):
                        for i in STEPS:
                            if i <= H or not last:
                                exponentials(c, i - 1)
                            if i % 2 == 1:
                                attn_high(c, (i - 5) // 2)
                            if not first and i == 12:
                                route_exp(c)
                            if not first and i == 9:
                                route_pack(c)
                            if not first and i == 10:
                                route_h2T(c)
                            if i == 5 and not last:
                                ln_modulate(c, c + 2, "lnT")
                            if i - 2 < H or not last:
                                copy_probT(c, i - 2)
                            if i <= H or not last:
                                prob_high(c, i - 1)
                            for name in [] if last else projections_at(i):
                                high(c, name)

                        if not last:
                            for s in range(TILES):
                                high(c, ("v", 1, s))

                    def clip(cn):
                        return cn % NC

                    ln_modulate(-1, 0, "ln0")
                    for name in HEAD_QK:
                        high(-1, name)
                    ln_modulate(-1, 1, "lnT")
                    for i in range(LAG):
                        if i >= 1:
                            exponentials(0, i - 1)
                        if i >= 2:
                            copy_probT(0, i - 2)
                        if i >= 1:
                            prob_high(0, i - 1)
                        for name in HEAD_V[2 * i:2 * i + 2]:
                            high(-1, name)
                    chunk(0, True, False)
                    with act.Fori(1, NC - 1) as c:
                        chunk(c, False, False)
                    chunk(NC - 1, False, True)
                    route_pack(NC)
                    route_h2T(NC)
                    route_exp(NC)

                @block.vector
                def _(dve):
                    def clip(cn):
                        return cn % NC

                    def ln_first(cn):
                        norm_stats(dve, clip(cn) * TILES, stats[0], meanvar[0], ln_stat, ln_mv, cn + 1)

                    def ln_second(cn):
                        norm_rows(dve, clip(cn) * TILES, xn, meanvar[0], rstd[0], ln_rstd, ln_xn, cn + 1)

                    def ln_high(c, cn, label):
                        for kd in range(KD):
                            bank, before = group(c, (label, kd))
                            dve.wait_ge(gen_free[bank], before + 1)
                        dve.tensor_copy(hT[:, cn % 2, :, 0, :], h32[:]).then_inc(ln_hi, 1)

                    def low(c, name):
                        cn = c + 1
                        bank, _ = group(c, name)
                        dve.wait_ge(proj_hi, proj_no(cn, name))
                        if name[0] == "q":
                            hi, lo = q[:, name[1], 0, :], q[:, name[1], 1, :]
                        elif name[0] == "k":
                            hi, lo = k[:, name[1], 0, P:], k[:, name[1], 1, P:]
                        else:
                            hi, lo = (v[:, 1 + name[2], m, name[1] * 512:(name[1] + 1) * 512] for m in range(2))
                        dve.scalar_tensor_tensor(lo, gen[bank][:], 1 / W_SCALE, hi, ALU.mult, ALU.subtract)\
                           .then_inc(gen_free[bank], 1)

                    def keep_k(c, j):
                        dve.wait_ge(scores_done, H * c + 2 * j + 2)
                        dve.tensor_copy(k[:, j, :, 0:P], k[:, j, :, CHUNK:]).then_inc(k_halo, 1)

                    def keep_v(c, half):
                        dve.wait_ge(pv_done, H * c + (H // 2) * (half + 1))
                        cols = slice(half * 512, (half + 1) * 512)
                        dve.tensor_copy(v[:, 0, :, cols], v[:, TILES, :, cols]).then_inc(v_halo, 1)

                    def mask_own(c, h):
                        u = H * c + h
                        dve.wait_ge(probT_ready, u + 1)
                        at_least(dve, pv_done, u - 1)
                        dve.tensor_tensor(probT_cur[:, h % 2], probT[:, h % 2],
                                          keys_cur[:].unsqueeze(1).to_broadcast([P, 2 * TILES, P]), ALU.mult).then_inc(cur_ready, 1)

                    def merge(c, h):
                        sc = score[h % 2]
                        stand_ge(dve, (scores_done, H * c + h + 1))
                        dve.copy_predicated(sc[:, :, P:], above[:].bitcast(I32).unsqueeze(1).to_broadcast([P, TILES, P]), sc[:, :, 0:P])\
                           .then_inc(merged, 1)

                    def row_max(c, h):
                        dve.wait_ge(merged, H * c + h + 1)
                        dve.reduce_max(rowmax[:, h % 2, :], score[h % 2][:, :, P:], AX.X).then_inc(maxed, 1)

                    def negate_max(c, h):
                        dve.wait_ge(maxed, H * c + h + 1)
                        dve.tensor_scalar(negmax[:, h % 2, :], rowmax[:, h % 2, :], -(DH ** -0.5), None, ALU.mult).then_inc(neg_ready, 1)

                    def invert_sum(c, h):
                        dve.wait_ge(exp_done, H * c + h + 1)
                        dve.reciprocal(rinv[:, h % 2, :], rowsum[:, h % 2, :]).then_inc(rinv_ready, 1)

                    def normalise(c, h):
                        dve.wait_ge(rinv_ready, H * c + h + 1)
                        dve.tensor_tensor(prob[:, h % 2], prob[:, h % 2], rinv[:, h % 2, :].unsqueeze(2).to_broadcast([P, TILES, P]), ALU.mult)\
                           .then_inc(norm_ready, 1)

                    def softmax_step(c, i, last):
                        new, old = i < H or not last, i >= 1 and (i <= H or not last)
                        for stage, unit, there in ((merge, i, new), (invert_sum, i - 1, old), (row_max, i, new),
                                                   (normalise, i - 1, old), (negate_max, i, new)):
                            if there:
                                stage(c, unit)

                    def attn_low(c, j):
                        dve.wait_ge(attn_hi, PAIRS * c + j + 1)
                        dve.tensor_tensor(attn[:, j, 1, :], pv[:], attn[:, j, 0, :], ALU.subtract).then_inc(attn_lo, 1)

                    def add_attention(c, p):
                        bank, before = group(c, ("out", p))
                        at_least(dve, x2_ready, 2 * c + p)
                        dve.wait_ge(gen_full[bank], before + 1)
                        ga = modrow[:, batch(c), 0:1, :].to_broadcast([P, 2, D])
                        dve.scalar_tensor_tensor(gated[:], gen[bank][:].rearrange("p (s d) -> p s d", s=2), 1 / W_SCALE,
                                                 ga, ALU.mult, ALU.mult).then_inc(gen_free[bank], 1)
                        dve.wait_ge(gen_free[bank], before + 1)
                        tiles = x[:, bass.ds(c * TILES + 2 * p, 2), :]
                        dve.tensor_tensor(tiles, tiles, gated[:], ALU.add).then_inc(x2_ready, 1)

                    def route_tokens(c):
                        rows_seen(dve, c)
                        dve.tensor_copy(packed[:, :, 2 * D:].bitcast(I32), token_no[:, bass.ds((c - 1) * TILES, TILES)].unsqueeze(2))\
                           .then_inc(token_put, 1)

                    def route_softmax(c):
                        bank, before = group(c, ("logits",))
                        n = 11 * (c - 1)
                        dve.wait_ge(gen_full[bank], before + 1)
                        dve.scalar_tensor_tensor(logit[:], gen[bank][:, 0:TILES * E].rearrange("p (s e) -> p s e", e=E), 1 / W_SCALE,
                                                 gbB[:].unsqueeze(1).to_broadcast([P, TILES, E]), ALU.mult, ALU.add)\
                           .then_inc(gen_free[bank], 1)
                        dve.wait_ge(gen_free[bank], before + 1)
                        dve.reduce_max(lmax[:], logit[:], AX.X).then_inc(r_soft, 2)
                        dve.wait_ge(r_soft, n + 2)
                        dve.tensor_tensor(logit[:], logit[:], lmax[:].unsqueeze(2).to_broadcast([P, TILES, E]), ALU.subtract).then_inc(r_soft, 1)

                    def route_top(c):
                        n = 11 * (c - 1)
                        dve.wait_ge(r_exp, c)
                        dve.reduce_sum(lsum[:, 0, :], logit[:], AX.X).then_inc(r_soft, 1)
                        dve.wait_ge(r_soft, n + 4)
                        dve.reciprocal(lsum[:, 1, :], lsum[:, 0, :]).then_inc(r_soft, 1)
                        dve.wait_ge(r_soft, n + 5)
                        dve.tensor_tensor(logit[:], logit[:], lsum[:, 1, :].unsqueeze(2).to_broadcast([P, TILES, E]), ALU.mult).then_inc(r_soft, 1)
                        stand_ge(dve, (r_soft, n + 6))
                        for s in range(TILES):
                            op = dve.max(top[:, s, :], logit[:, s, :])
                        op.then_inc(r_soft, 1)
                        stand_ge(dve, (r_soft, n + 7))
                        for s in range(TILES):
                            op = dve.max_index(topi[:, s, :], top[:, s, :], logit[:, s, :])
                        op.then_inc(r_soft, 1)
                        dve.wait_ge(r_soft, n + 8)
                        dve.tensor_copy(topf[:], topi[:, :, 0:K]).then_inc(r_soft, 1)
                        dve.wait_ge(r_soft, n + 9)
                        for m in range(K):
                            dve.tensor_tensor(onehot[:, :, m, :], expert_no[:].unsqueeze(1).to_broadcast([P, TILES, E]),
                                              topf[:, :, m:m + 1].to_broadcast([P, TILES, E]), ALU.is_equal).then_inc(r_soft, 1)

                    def route_slots(c):
                        g = c - 1
                        n = 8 * (c - 1)
                        KE = K * E
                        bank, before = group(c, ("counts",))
                        dve.wait_ge(gen_full[bank], before + 1)
                        flat = cum[:].rearrange("p s c e -> p s (c e)")
                        cflat = carry[:].rearrange("p c e -> p (c e)")
                        dve.tensor_tensor(flat, gen[bank][:, 0:TILES * KE].rearrange("p (s n) -> p s n", n=KE),
                                          cflat.unsqueeze(1).to_broadcast([P, TILES, KE]), ALU.add).then_inc(r_count, 1)
                        dve.wait_ge(r_count, n + 1)
                        dve.tensor_tensor(cflat, cflat, gen[bank][:, TILES * KE:(TILES + 1) * KE], ALU.add).then_inc(gen_free[bank], 1)
                        dve.tensor_tensor(cum[:], cum[:], onehot[:], ALU.mult).then_inc(r_count, 1)
                        dve.wait_ge(r_count, n + 2)
                        dve.reduce_sum(pos[:], cum[:], AX.X).then_inc(r_count, 1)
                        dve.wait_ge(r_count, n + 3)
                        tile0 = g * TILES
                        dve.scalar_tensor_tensor(weight[:, bass.ds(tile0, TILES), :], pos[:], float(CAP), top[:, :, 0:K], ALU.is_lt, ALU.mult)
                        dve.tensor_scalar(drop[:], pos[:], float(CAP), FAR, ALU.is_ge, ALU.mult)
                        dve.tensor_tensor(posc[:], pos[:], choice_base[:], ALU.add).then_inc(r_count, 1)
                        dve.wait_ge(r_count, n + 4)
                        dve.scalar_tensor_tensor(slot[:], topf[:], float(K * CAP), posc[:], ALU.mult, ALU.add).then_inc(r_count, 4)
                        dve.wait_ge(r_count, n + 8)
                        rows_seen(dve, c)
                        dve.tensor_tensor(send[:], slot[:], drop[:], ALU.add).then_inc(r_send, 1)

                    def chunk(c, first, last):
                        for i in STEPS:
                            if i >= 6 and i % 2 == 0:
                                attn_low(c, (i - 6) // 2)
                            if not first and i == 12:
                                route_softmax(c)
                            if not first and i == 16:
                                route_slots(c)
                            for name in [] if i == LAG or last else projections_at(i - 1):
                                low(c, name)
                            if i % 2 == 0 and not last:
                                keep_k(c, (i - LAG) // 2)
                            if i == 12 and not last:
                                keep_v(c, 0)
                            softmax_step(c, i, last)
                            if i - 3 < H or not last:
                                mask_own(c, i - 3)
                            if not first and i == 4:
                                dve.wait_ge(x2_ready, 2 * c)
                                norm_stats(dve, (c - 1) * TILES, stats[1], meanvar[1], r_stat, r_mv, c)
                            if not first and i == 6:
                                norm_rows(dve, (c - 1) * TILES, h2, meanvar[1], rstd[1], r_rstd, r_xn, c)
                            if not first and i == 8:
                                route_tokens(c)
                            if not first and i == 12:
                                route_top(c)
                            if i == 10 and not last:
                                ln_high(c, c + 2, "lnT")
                        attn_low(c, PAIRS - 1)
                        if not last:
                            keep_v(c, 1)
                            for name in projections_at(STEPS[-1]) + v_half(1):
                                low(c, name)
                            ln_first(c + 3)
                        add_attention(c, 0)
                        if not last:
                            ln_second(c + 3)
                        add_attention(c, 1)

                    dve.memset(k[:, :, :, 0:P], 0.0).then_inc(k_halo, PAIRS)
                    dve.memset(v[:, 0, :, :], 0.0).then_inc(v_halo, 2)
                    ln_high(-1, 0, "ln0")
                    for n, name in enumerate(HEAD_QK):
                        low(-1, name)
                        if n == 3:
                            dve.wait_ge(x_loaded, 16)
                            ln_first(1)
                        if n == 5:
                            ln_second(1)
                    ln_high(-1, 1, "lnT")
                    ln_first(2)
                    for i in range(LAG):
                        softmax_step(0, i, False)
                        if i >= 3:
                            mask_own(0, i - 3)
                        for name in HEAD_V[2 * i:2 * i + 2]:
                            low(-1, name)
                        if i == 1:
                            ln_second(2)
                    chunk(0, True, False)
                    with dve.Fori(1, NC - 1) as c:
                        chunk(c, False, False)
                    chunk(NC - 1, False, True)
                    dve.wait_ge(x2_ready, 2 * NC)
                    norm_stats(dve, (NC - 1) * TILES, stats[1], meanvar[1], r_stat, r_mv, NC)
                    norm_rows(dve, (NC - 1) * TILES, h2, meanvar[1], rstd[1], r_rstd, r_xn, NC)
                    route_scale(dve, NC)
                    route_shift(dve, NC)
                    route_tokens(NC)
                    route_low(dve, NC)
                    route_softmax(NC)
                    route_top(NC)
                    route_slots(NC)

                @block.gpsimd
                def _(pool):
                    def ln_rstd_of(cn):
                        reciprocal_std(pool, meanvar[0], rstd[0], ln_mv, ln_var, ln_rstd, cn + 1)

                    def ln_low(cn):
                        pool.wait_ge(ln_hi, cn + 1)
                        pool.tensor_tensor(hT[:, cn % 2, :, 1, :], h32[:], hT[:, cn % 2, :, 0, :], ALU.subtract).then_inc(ln_lo, 1)

                    def prob_low(c, h):
                        pool.wait_ge(hi_ready, H * c + h + 1)
                        pool.tensor_tensor(prob16[:, h % 2, 1], prob[:, h % 2], prob16[:, h % 2, 0], ALU.subtract).then_inc(lo_ready, 1)

                    def mask_previous(c, h):
                        u = H * c + h
                        waits = [(probT_ready, u + 1)]
                        if not isinstance(c, int) or u >= 2:
                            waits.append((pv_done, u - 1))
                        stand_ge(pool, *waits)
                        pool.affine_select(out=probT_prev[:, h % 2], in_=probT[:, h % 2], pattern=[[0, 2 * TILES], [-1, P]],
                                           compare_op=ALU.is_gt, fill=zero, base=0, channel_multiplier=1).then_inc(prev_ready, 1)

                    def scatter(c, tiles):
                        if tiles[0] == 0:
                            stand_ge(pool, (r_pack, c), (token_put, c), (r_send, c))
                        for s in tiles:
                            for m in range(K):
                                pool.indirect_dma_start(
                                    out=xbuf, out_offset=bass.IndirectOffsetOnAxis(ap=send[:, s, m:m + 1], axis=0),
                                    in_=packed[:, s, :], in_offset=None, bounds_check=limit, oob_is_err=False)\
                                    .then_inc(sent, 16)

                    def chunk(c, first, last):
                        for i in STEPS:
                            if i - 3 < H or not last:
                                mask_previous(c, i - 3)
                            if i <= H or not last:
                                prob_low(c, i - 1)
                            if not first and i == 5:
                                reciprocal_std(pool, meanvar[1], rstd[1], r_mv, r_var, r_rstd, c)
                            if not first and i == 6:
                                route_scale(pool, c)
                            if not first and i == 7:
                                route_shift(pool, c)
                            if not first and i == 9:
                                route_low(pool, c)
                            if i == 11 and not last:
                                ln_low(c + 2)
                            if not first and 16 <= i < 16 + TILES:
                                scatter(c, [i - 16])
                        if first:
                            pool.wait_ge(zero_sent, 16 * (SLOTS // P))
                        if not last:
                            ln_rstd_of(c + 3)
                        if not first and not last:
                            pool.wait_ge(sent, 16 * TILES * K * c)

                    limit = pool.to_reg(SLOTS - 1)
                    zero = pool.to_reg(0.0)
                    ln_low(0)
                    ln_rstd_of(1)
                    ln_low(1)
                    ln_rstd_of(2)
                    for i in range(1, LAG):
                        if i >= 3:
                            mask_previous(0, i - 3)
                        prob_low(0, i - 1)
                    chunk(0, True, False)
                    with pool.Fori(1, NC - 1) as c:
                        chunk(c, False, False)
                    chunk(NC - 1, False, True)
                    reciprocal_std(pool, meanvar[1], rstd[1], r_mv, r_var, r_rstd, NC)
                    scatter(NC, range(TILES))
                    pool.wait_ge(sent, 16 * TILES * K * NC)

        ffn_stack = ExitStack()
        with ffn_stack:
            sb = alloc(ffn_stack)
            ps = lambda name, shape, dt: ffn_stack.enter_context(nc.psum_tensor(name, shape, dt))
            w1 = sb("w1", [P, 2, KD, 2, FF], F16)
            w2 = sb("w2", [P, 2, FT, 2, D], F16)
            rows = sb("rows", [P, 2, ST, ROW], F16)
            xT = sb("xT", [P, 2, 2 * KD, ST * P], F16)
            hid = sb("hid", [P, FT, 2, ST * P], F16)
            hid32 = sb("hid32", [P, 4, 512], F32)
            b2B = sb("b2B", [P, E, D], F32)
            y32 = sb("y32", [P, 2, 2, D], F32)
            up = [ps(f"up{i}", [P, 512], F32) for i in range(4)]
            down = [ps(f"down{i}", [P, 2, D], F32) for i in range(2)]
            tp = [ps(f"tp{i}", [P, 2 * KD, 2, P], F16) for i in range(2)]

            b2_loaded = sem("b2_loaded")
            rows_loaded = [sem(f"rows_loaded{i}") for i in range(2)]
            (w_hi, w_lo, xT_full, xT_ready, up_full, up_out, hid_hi, hid_ready, down_full,
             y_ready) = (sem(n) for n in ("w_hi", "w_lo", "xT_full", "xT_ready", "up_full",
                                          "up_out", "hid_hi", "hid_ready", "down_full", "y_ready"))
            y_sent, y_free = sem("y_sent"), sem("y_free")
            UG = len(NPART) * FT
            DG = ST // 2
            rowv = xbuf.rearrange("(e t p) d -> e p t d", p=P, t=ST)

            def split_views(par, i, part):
                if i < 2:
                    return w32[:, 0, i * FF:(i + 1) * FF], w1[:, par, i, part, :]
                f = (i - 2) * FT // 2
                return (w32[:, 1, (i - 2) * 1024:(i - 1) * 1024].rearrange("p (f n) -> p f n", n=D),
                        w2[:, par, f:f + FT // 2, part, :])

            with nc.Block() as block:
                @block.sync
                def _(sp):

                    def load_weights(e):
                        if not isinstance(e, int) or e > 0:
                            sp.wait_ge(w_lo, 4 * e)
                        load_expert(sp, w32, e)

                    def load_rows(e, par):
                        if not isinstance(e, int) or e > 0:
                            sp.wait_ge(y_free, 2 + DG * (e - 1))
                        sp.dma_start(rows[:, par], rowv[bass.ds(e, 1)].rearrange("e p t d -> (e p) t d")).then_inc(rows_loaded[par], 16)

                    load_rows(0, 0)
                    sp.dma_start(b2B[:], b2_in.partition_broadcast(P)).then_inc(b2_loaded, 16)
                    def expert(e, par, last):
                        if not last:
                            load_weights(e + 1)
                            load_rows(e + 1, 1 - par)

                    with sp.Fori(0, E // 2 - 1) as i:
                        for par in range(2):
                            expert(2 * i + par, par, False)
                    expert(E - 2, 0, False)
                    expert(E - 1, 1, True)

                @block.gpsimd
                def _(pool):
                    def send_on(e, g, par):
                        n = (par * DG + g) % 2
                        stand_ge(pool, (y_ready, 2 + DG * e + g + 1))
                        for s in range(2):
                            t = 2 * g + s
                            pool.indirect_dma_start(
                                out=ytok[t // (ST // K)],
                                out_offset=bass.IndirectOffsetOnAxis(ap=rows[:, par, t, 2 * D:].bitcast(U32), axis=0),
                                in_=y32[:, n, s, :], in_offset=None, bounds_check=last_token, oob_is_err=False)\
                                .then_inc(y_sent, 16)
                        pool.wait_ge(y_sent, 32 * (DG * e + g + 1))
                        pool.sem_inc(y_free, 1)

                    last_token = pool.to_reg(T - 1)
                    pool.sem_inc(y_free, 2)
                    with pool.Fori(0, E // 2 - 1) as i:
                        for par in range(2):
                            for g in range(DG):
                                send_on(2 * i + par, g, par)
                    for e in (E - 2, E - 1):
                        for g in range(DG):
                            send_on(e, g, e % 2)

                @block.tensor
                def _(pe):
                    def transposes(e, par):
                        pe.wait_ge(rows_loaded[par], 8 * (e - par) + 16)
                        for g in range(DG):
                            n = (par * DG + g) % 2
                            pe.wait_ge(xT_ready, DG * e + g + 1)
                            for s in range(2):
                                for m in range(2 * KD):
                                    mm = pe.transpose(tp[n][:, m, s, :], rows[:, par, 2 * g + s, m * P:(m + 1) * P], ident16[:])
                            mm.then_inc(xT_full, 1)

                    def go_up(e, par, n):
                        if n == 0:
                            pe.wait_ge(w_lo, 4 * (e + 1))
                        lo, size = NPART[n]
                        pe.wait_ge(xT_ready, 2 + DG * e + (lo + size) // (2 * P))
                        for ft in range(FT):
                            g = UG * e + n * FT + ft
                            bank = up[ft % 4]
                            pe.wait_ge(up_out, g + 1)
                            i = 0
                            for kd in range(KD):
                                for a, b in SPLIT_PRODUCTS:
                                    mm = pe.matmul(bank[:, 0:size], w1[:, par, kd, a, ft * P:(ft + 1) * P],
                                                   xT[:, par, b * KD + kd, lo:lo + size], start=(i == 0), stop=(i == 5))
                                    i += 1
                            mm.then_inc(up_full, 1)

                    def go_down(e, par, g):
                        n = (par * DG + g) % 2
                        part = min(g // 2, 2)
                        pe.wait_ge(hid_ready, 4 + UG * e + (part + 1) * FT)
                        pe.wait_ge(y_ready, DG * e + g + 1)
                        for s in range(2):
                            t = 2 * g + s
                            i = 0
                            for ft in range(FT):
                                for a, b in SPLIT_PRODUCTS:
                                    mm = pe.matmul(down[n][:, s, :], hid[:, ft, a, t * P:(t + 1) * P], w2[:, par, ft, b, :],
                                                   start=(i == 0), stop=(i == 3 * FT - 1))
                                    i += 1
                        mm.then_inc(down_full, 1)

                    def expert(e, par, last):
                        go_up(e, par, 0)
                        go_up(e, par, 1)
                        go_down(e, par, 0)
                        go_down(e, par, 1)
                        go_up(e, par, 2)
                        go_down(e, par, 2)
                        go_down(e, par, 3)
                        if not last:
                            transposes(e + 1, 1 - par)
                        go_down(e, par, 4)

                    pe.sem_inc(down_full, DG)
                    pe.sem_inc(xT_full, DG)
                    pe.sem_inc(up_full, UG)
                    transposes(0, 0)
                    with pe.Fori(0, E // 2 - 1) as i:
                        for par in range(2):
                            expert(2 * i + par, par, False)
                    expert(E - 2, 0, False)
                    expert(E - 1, 1, True)

                @block.scalar
                def _(act):
                    act.wait_ge(b1_loaded, 16)

                    def split_high(e, par, i):
                        if i == 0:
                            act.wait_ge(w_loaded, 32 * (e + 1))
                            if not isinstance(e, int) or e > 1:
                                act.wait_ge(down_full, DG * e)
                        src, dst = split_views(par, i, 0)
                        act.activation(dst, src, ACT.Copy, scale=W_SCALE).then_inc(w_hi, 1)

                    def expert(e, par, last):
                        for k_ in range(UG):
                            n, ft = divmod(k_, FT)
                            g = UG * e + k_
                            size = NPART[n][1]
                            stand_ge(act, (up_full, UG + g + 1), (hid_ready, g + 1))
                            act.activation(hid32[:, k_ % 4, 0:size], up[ft % 4][:, 0:size], ACT.Relu, scale=1 / W_SCALE,
                                           bias=b1T[:, bass.ds(e, 1), ft:ft + 1].rearrange("p a b -> p (a b)")).then_inc(up_out, 1)
                            if k_ % 4 == 3 and 1 <= k_ // 4 <= 4 and not last:
                                split_high(e + 1, 1 - par, k_ // 4 - 1)

                    act.sem_inc(up_out, len(up))
                    for i in range(4):
                        split_high(0, 0, i)
                    with act.Fori(0, E // 2 - 1) as i:
                        for par in range(2):
                            expert(2 * i + par, par, False)
                    expert(E - 2, 0, False)
                    expert(E - 1, 1, True)

                @block.vector
                def _(dve):

                    def split_low(e, par, i):
                        dve.wait_ge(w_hi, 4 * e + i + 1)
                        src, hi = split_views(par, i, 0)
                        _, lo = split_views(par, i, 1)
                        dve.scalar_tensor_tensor(lo, src, W_SCALE, hi, ALU.mult, ALU.subtract).then_inc(w_lo, 1)

                    def copy_xT(e, par):
                        for g in range(DG):
                            n = (par * DG + g) % 2
                            dve.wait_ge(xT_full, DG * (e + 1) + g + 1)
                            if g == 0 and (not isinstance(e, int) or e > 0):
                                dve.wait_ge(up_full, UG * e)
                            dve.tensor_copy(xT[:, par, :, 2 * g * P:2 * (g + 1) * P],
                                            tp[n][:].rearrange("p m s q -> p m (s q)")).then_inc(xT_ready, 1)

                    def hidden(e, k_):
                        n, ft = divmod(k_, FT)
                        g = UG * e + k_
                        lo, size = NPART[n]
                        dve.wait_ge(up_out, 4 + g + 1)
                        if ft == 0:
                            dve.wait_ge(down_full, DG * e + min(2 * (n + 1), DG))
                        dve.tensor_copy(hid[:, ft, 0, lo:lo + size], hid32[:, k_ % 4, 0:size]).then_inc(hid_hi, 1)
                        dve.wait_ge(hid_hi, g + 1)
                        dve.tensor_tensor(hid[:, ft, 1, lo:lo + size], hid32[:, k_ % 4, 0:size],
                                          hid[:, ft, 0, lo:lo + size], ALU.subtract).then_inc(hid_ready, 1)

                    def finish(e, par, g):
                        n = (par * DG + g) % 2
                        dve.wait_ge(down_full, DG * (e + 1) + g + 1)
                        dve.wait_ge(y_free, DG * e + g + 1)
                        b2 = b2B[:, bass.ds(e, 1), :].to_broadcast([P, 2, D])
                        dve.scalar_tensor_tensor(y32[:, n], down[n][:], 1 / W_SCALE, b2, ALU.mult, ALU.add).then_inc(y_ready, 1)

                    def expert(e, par, last):
                        for k_ in range(2 * FT):
                            hidden(e, k_)
                            if k_ % 4 == 3 and k_ // 4 >= 1 and not last:
                                split_low(e + 1, 1 - par, k_ // 4 - 1)
                        finish(e, par, 0)
                        finish(e, par, 1)
                        for k_ in range(2 * FT, UG):
                            hidden(e, k_)
                            if k_ % 4 == 3 and k_ == 19 and not last:
                                split_low(e + 1, 1 - par, 3)
                        finish(e, par, 2)
                        finish(e, par, 3)
                        if not last:
                            copy_xT(e + 1, 1 - par)
                        finish(e, par, 4)

                    dve.sem_inc(hid_ready, 4)
                    dve.sem_inc(xT_ready, len(tp))
                    dve.sem_inc(y_ready, len(down))
                    for i in range(4):
                        split_low(0, 0, i)
                    copy_xT(0, 0)
                    dve.wait_ge(b2_loaded, 16)
                    with dve.Fori(0, E // 2 - 1) as i:
                        for par in range(2):
                            expert(2 * i + par, par, False)
                    expert(E - 2, 0, False)
                    expert(E - 1, 1, True)

        fin_stack = ExitStack()
        with fin_stack:
            sb = alloc(fin_stack)
            GROUP = 4
            NG = NT // GROUP
            y = sb("y", [P, NG, K, GROUP, D], F32)
            mixed = sb("mixed", [P, NG, GROUP, D], F32)
            y_loaded = [sem(f"y_loaded{i}") for i in range(NG)]
            out_sent = sem("out_sent")
            f_first, f_both, f_scaled, f_added = (sem(n) for n in ("f_first", "f_both", "f_scaled", "f_added"))
            with nc.Block() as block:
                @block.scalar
                def _(act):
                    for i in range(NG):
                        act.wait_ge(y_loaded[i], 16 * K)
                        for t in range(GROUP):
                            op = act.activation(mixed[:, i, t, :], y[:, i, 0, t, :], ACT.Copy,
                                                scale=weight[:, GROUP * i + t, 0:1])
                        op.then_inc(f_first, 1)

                @block.vector
                def _(dve):
                    for i in range(NG):
                        dve.wait_ge(f_first, i + 1)
                        y1 = y[:, i, 1]
                        for t in range(GROUP):
                            op = dve.scalar_tensor_tensor(y1[:, t, :], y1[:, t, :], weight[:, GROUP * i + t, 1:2],
                                                          mixed[:, i, t, :], ALU.mult, ALU.add)
                        op.then_inc(f_both, 1)
                        dve.wait_ge(f_both, i + 1)
                        gb = modrow[:, GROUP * i // (NT // B), 3:4, :].to_broadcast([P, GROUP, D])
                        dve.tensor_tensor(mixed[:, i], y1, gb, ALU.mult).then_inc(f_scaled, 1)

                @block.gpsimd
                def _(pool):
                    for i in range(NG):
                        pool.wait_ge(f_scaled, i + 1)
                        tiles = x[:, GROUP * i:GROUP * (i + 1), :]
                        pool.tensor_tensor(tiles, tiles, mixed[:, i], ALU.add).then_inc(f_added, 1)

                @block.sync
                def _(sp):
                    def grouped(rows):
                        return rows.rearrange("(i t p) d -> i p t d", p=P, t=GROUP)

                    for i in range(NG):
                        for m in range(K):
                            sp.dma_start(y[:, i, m], grouped(ytok[m])[i]).then_inc(y_loaded[i], 16)
                    for i in range(NG):
                        sp.wait_ge(f_added, i + 1)
                        sp.dma_start(grouped(out_rows)[i], x[:, GROUP * i:GROUP * (i + 1), :]).then_inc(out_sent, 16)
                    sp.wait_ge(out_sent, 16 * NG)


_INS = ["L0_attn_x", "L0_attn_Wqkv", "L0_attn_Wout", "L0_ffn_gate_w", "L0_ffn_gate_b", "L0_ffn_W1", "L0_ffn_b1",
        "L0_ffn_W2", "L0_ffn_b2", "L0_c", "L0_wmod"]


def kernel(**inputs):
    import numpy as _np
    import concourse.bacc as _bacc
    from concourse import mybir as _mybir
    from concourse.bass_utils import run_bass_kernel_spmd as _run

    nc = _bacc.Bacc("TRN2", target_bir_lowering=False, num_devices=1)
    arrays, args = {}, []
    for name in _INS:
        a = _np.ascontiguousarray(inputs[name])
        arrays[f"in_{name}"] = a
        args.append(nc.dram_tensor(f"in_{name}", a.shape, _mybir.dt.from_np(a.dtype), kind="ExternalInput").ap())
    out = nc.dram_tensor("out", inputs["L0_attn_x"].shape, _mybir.dt.float32, kind="ExternalOutput").ap()
    build(nc, *args, out)
    r = _run(nc, [arrays], core_ids=[0])
    return r.results[0]["out"]
```
